# Optimizing a Trainium2 kernel written in Bass

```python
import numpy as np
import jax
import jax.numpy as jnp

def _softmax(x, axis=-1):
    return jax.nn.softmax(x, axis=axis)

def _gelu(x):
    return jax.nn.gelu(x, approximate=True)

def _silu(x):
    return jax.nn.silu(x)

def _sigmoid(x):
    return jax.nn.sigmoid(x)

def _layernorm(x, axis=-1, eps=1e-05):
    m = jnp.mean(x, axis=axis, keepdims=True)
    v = jnp.var(x, axis=axis, keepdims=True)
    return (x - m) / jnp.sqrt(v + eps)

def _scatter_add(tgt, idx, src, axis=0):
    return tgt.at[idx].add(src)

def _segment_sum(src, seg, n):
    return jax.ops.segment_sum(src, seg, n)
kernel_name = 'mk_pixart_seq_d2_seqx_r4_fa24f5'

def setup_inputs(seed: int=0):
    np.random.seed(seed)
    _w = jnp.asarray

    def _rec_inputs():
        import jax
        import jax.numpy as jnp
        _rk = jax.random.key(seed)
        x = -0.0003929 + 0.9999 * jax.random.normal(jax.random.fold_in(_rk, 1), (2, 1024, 256), jnp.float32)
        _lenS = 1024 - jax.random.randint(jax.random.fold_in(_rk, 7), (2,), 0, max(1, 1024 // 4) + 1, jnp.int32)
        _lenS2 = 64 - jax.random.randint(jax.random.fold_in(_rk, 8), (2,), 0, max(1, 64 // 4) + 1, jnp.int32)
        _ctx_1024P = jax.random.normal(jax.random.fold_in(_rk, 11), (2, 16, 256), jnp.float32)
        _ctx_1024c = jax.random.dirichlet(jax.random.fold_in(_rk, 511), 0.3 * jnp.ones((16,), jnp.float32), (2, 64))
        _ctx_1024t = jnp.einsum('bsk,bkd->bsd', _ctx_1024c, _ctx_1024P)
        _ctx_1024t = _ctx_1024t * jax.lax.rsqrt(jnp.mean(jnp.square(_ctx_1024t)) + 1e-12) * 0.953939
        ctx_1024 = -1.39393e-06 + 0.999914 * (_ctx_1024t + 0.3 * jax.random.normal(jax.random.fold_in(_rk, 611), (2, 64, 256), jnp.float32))
        cond_1024 = -0.00920427 + 1.00102 * jax.random.normal(jax.random.fold_in(_rk, 12), (2, 256), jnp.float32)
        return (x, ctx_1024, cond_1024)
    x, ctx_1024, cond_1024 = _rec_inputs()

    def _L0_xcond_setup():
        import jax, jax.numpy as jnp
        import numpy as np
        EPS = 1e-05

        def _ada_ln(x, c, W_ss, b_ss):
            mu = jnp.mean(x, axis=-1, keepdims=True)
            var = jnp.mean((x - mu) ** 2, axis=-1, keepdims=True)
            h = (x - mu) / jnp.sqrt(var + EPS)
            ss = jax.nn.silu(c) @ W_ss + b_ss
            scale, bias = jnp.split(ss, 2, axis=-1)
            return (1.0 + scale)[:, None, :] * h + bias[:, None, :]
        key = jax.random.key(seed)
        ks = jax.random.split(key, 12)
        B, Lq, Lkv, H = (8, 512, 128, 256)
        s = 0.02
        return {'x_q': jax.random.normal(ks[0], (B, Lq, H), jnp.float32), 'x_kv': jax.random.normal(ks[1], (B, Lkv, H), jnp.float32), 't_vec': jax.random.normal(ks[2], (B, H), jnp.float32), 'Wq': jax.random.normal(ks[3], (H, H), jnp.float32) * s, 'bq': jnp.zeros((H,), jnp.float32), 'Wkv': jax.random.normal(ks[4], (H, 2 * H), jnp.float32) * s, 'bkv': jnp.zeros((2 * H,), jnp.float32), 'Wp': jax.random.normal(ks[5], (H, H), jnp.float32) * s, 'bp': jnp.zeros((H,), jnp.float32), 'Wss_q': jax.random.normal(ks[6], (H, 2 * H), jnp.float32) * s, 'bss_q': jnp.zeros((2 * H,), jnp.float32), 'Wss_kv': jax.random.normal(ks[7], (H, 2 * H), jnp.float32) * s, 'bss_kv': jnp.zeros((2 * H,), jnp.float32)}
    _L0_xcond_all = _L0_xcond_setup()
    _L0_xcond_in = {k: v for k, v in _L0_xcond_all.items() if k in ('Wq', 'bq', 'Wkv', 'bkv', 'Wp', 'bp', 'Wss_q', 'bss_q', 'Wss_kv', 'bss_kv')}
    del _L0_xcond_all

    def _L1_xcond_setup():
        import jax, jax.numpy as jnp
        import numpy as np
        D = 256
        H = 16
        DH = D // H
        DFF = 1024
        B = 2
        L = 512
        EPS = 1e-05

        def layer_norm(x, g, b):
            mu = jnp.mean(x, axis=-1, keepdims=True)
            var = jnp.mean(jnp.square(x - mu), axis=-1, keepdims=True)
            return (x - mu) * jax.lax.rsqrt(var + EPS) * g + b

        def ada_ln(x, t_emb, ln_g, ln_b, aff_w, aff_b):
            normed = layer_norm(x, ln_g, ln_b)
            affine = t_emb @ aff_w + aff_b
            gamma, beta = jnp.split(affine, 2, axis=-1)
            return gamma[:, None, :] * normed + beta[:, None, :]

        def mha(q_in, k_in, v_in, qw, qb, kw, kb, vw, vb, ow, ob):
            Bq, Lq, _ = q_in.shape
            Lk = k_in.shape[1]
            Q = (q_in @ qw + qb).reshape(Bq, Lq, H, DH)
            K = (k_in @ kw + kb).reshape(Bq, Lk, H, DH)
            V = (v_in @ vw + vb).reshape(Bq, Lk, H, DH)
            scores = jnp.einsum('bqhd,bkhd->bhqk', Q, K) / np.sqrt(DH).astype(np.float32)
            attn = jax.nn.softmax(scores, axis=-1)
            out = jnp.einsum('bhqk,bkhd->bqhd', attn, V).reshape(Bq, Lq, D)
            return out @ ow + ob
        key = jax.random.key(seed)
        ks = jax.random.split(key, 32)
        s = lambda k, shape, scale=0.02: jax.random.normal(k, shape, dtype=jnp.float32) * scale
        inp = {'x': jax.random.normal(ks[0], (B, L, D), dtype=jnp.float32), 'u': jax.random.normal(ks[1], (B, L, D), dtype=jnp.float32), 't_emb': jax.random.normal(ks[2], (B, D), dtype=jnp.float32), 'ln1_g': jnp.ones((D,), jnp.float32), 'ln1_b': jnp.zeros((D,), jnp.float32), 'aff1_w': s(ks[3], (D, 2 * D)), 'aff1_b': jnp.zeros((2 * D,), jnp.float32), 'ln2_g': jnp.ones((D,), jnp.float32), 'ln2_b': jnp.zeros((D,), jnp.float32), 'aff2_w': s(ks[4], (D, 2 * D)), 'aff2_b': jnp.zeros((2 * D,), jnp.float32), 'sa_qw': s(ks[5], (D, D)), 'sa_qb': jnp.zeros((D,), jnp.float32), 'sa_kw': s(ks[6], (D, D)), 'sa_kb': jnp.zeros((D,), jnp.float32), 'sa_vw': s(ks[7], (D, D)), 'sa_vb': jnp.zeros((D,), jnp.float32), 'sa_ow': s(ks[8], (D, D)), 'sa_ob': jnp.zeros((D,), jnp.float32), 'ca_qw': s(ks[9], (D, D)), 'ca_qb': jnp.zeros((D,), jnp.float32), 'ca_kw': s(ks[10], (D, D)), 'ca_kb': jnp.zeros((D,), jnp.float32), 'ca_vw': s(ks[11], (D, D)), 'ca_vb': jnp.zeros((D,), jnp.float32), 'ca_ow': s(ks[12], (D, D)), 'ca_ob': jnp.zeros((D,), jnp.float32), 'ffn_w1': s(ks[13], (D, DFF)), 'ffn_b1': jnp.zeros((DFF,), jnp.float32), 'ffn_w2': s(ks[14], (DFF, D)), 'ffn_b2': jnp.zeros((D,), jnp.float32)}
        return inp
    _L1_xcond_all = _L1_xcond_setup()
    _L1_xcond_in = {k: v for k, v in _L1_xcond_all.items() if k in ('ln1_g', 'ln1_b', 'aff1_w', 'aff1_b', 'ln2_g', 'ln2_b', 'aff2_w', 'aff2_b', 'sa_qw', 'sa_qb', 'sa_kw', 'sa_kb', 'sa_vw', 'sa_vb', 'sa_ow', 'sa_ob', 'ca_qw', 'ca_qb', 'ca_kw', 'ca_kb', 'ca_vw', 'ca_vb', 'ca_ow', 'ca_ob', 'ffn_w1', 'ffn_b1', 'ffn_w2', 'ffn_b2')}
    del _L1_xcond_all
    return {'x': x, 'ctx_1024': ctx_1024, 'cond_1024': cond_1024, 'L0_xcond_Wq': _L0_xcond_in['Wq'], 'L0_xcond_bq': _L0_xcond_in['bq'], 'L0_xcond_Wkv': _L0_xcond_in['Wkv'], 'L0_xcond_bkv': _L0_xcond_in['bkv'], 'L0_xcond_Wp': _L0_xcond_in['Wp'], 'L0_xcond_bp': _L0_xcond_in['bp'], 'L0_xcond_Wss_q': _L0_xcond_in['Wss_q'], 'L0_xcond_bss_q': _L0_xcond_in['bss_q'], 'L0_xcond_Wss_kv': _L0_xcond_in['Wss_kv'], 'L0_xcond_bss_kv': _L0_xcond_in['bss_kv'], 'L1_xcond_ln1_g': _L1_xcond_in['ln1_g'], 'L1_xcond_ln1_b': _L1_xcond_in['ln1_b'], 'L1_xcond_aff1_w': _L1_xcond_in['aff1_w'], 'L1_xcond_aff1_b': _L1_xcond_in['aff1_b'], 'L1_xcond_ln2_g': _L1_xcond_in['ln2_g'], 'L1_xcond_ln2_b': _L1_xcond_in['ln2_b'], 'L1_xcond_aff2_w': _L1_xcond_in['aff2_w'], 'L1_xcond_aff2_b': _L1_xcond_in['aff2_b'], 'L1_xcond_sa_qw': _L1_xcond_in['sa_qw'], 'L1_xcond_sa_qb': _L1_xcond_in['sa_qb'], 'L1_xcond_sa_kw': _L1_xcond_in['sa_kw'], 'L1_xcond_sa_kb': _L1_xcond_in['sa_kb'], 'L1_xcond_sa_vw': _L1_xcond_in['sa_vw'], 'L1_xcond_sa_vb': _L1_xcond_in['sa_vb'], 'L1_xcond_sa_ow': _L1_xcond_in['sa_ow'], 'L1_xcond_sa_ob': _L1_xcond_in['sa_ob'], 'L1_xcond_ca_qw': _L1_xcond_in['ca_qw'], 'L1_xcond_ca_qb': _L1_xcond_in['ca_qb'], 'L1_xcond_ca_kw': _L1_xcond_in['ca_kw'], 'L1_xcond_ca_kb': _L1_xcond_in['ca_kb'], 'L1_xcond_ca_vw': _L1_xcond_in['ca_vw'], 'L1_xcond_ca_vb': _L1_xcond_in['ca_vb'], 'L1_xcond_ca_ow': _L1_xcond_in['ca_ow'], 'L1_xcond_ca_ob': _L1_xcond_in['ca_ob'], 'L1_xcond_ffn_w1': _L1_xcond_in['ffn_w1'], 'L1_xcond_ffn_b1': _L1_xcond_in['ffn_b1'], 'L1_xcond_ffn_w2': _L1_xcond_in['ffn_w2'], 'L1_xcond_ffn_b2': _L1_xcond_in['ffn_b2']}

def reference(x, ctx_1024, cond_1024, L0_xcond_Wq, L0_xcond_bq, L0_xcond_Wkv, L0_xcond_bkv, L0_xcond_Wp, L0_xcond_bp, L0_xcond_Wss_q, L0_xcond_bss_q, L0_xcond_Wss_kv, L0_xcond_bss_kv, L1_xcond_ln1_g, L1_xcond_ln1_b, L1_xcond_aff1_w, L1_xcond_aff1_b, L1_xcond_ln2_g, L1_xcond_ln2_b, L1_xcond_aff2_w, L1_xcond_aff2_b, L1_xcond_sa_qw, L1_xcond_sa_qb, L1_xcond_sa_kw, L1_xcond_sa_kb, L1_xcond_sa_vw, L1_xcond_sa_vb, L1_xcond_sa_ow, L1_xcond_sa_ob, L1_xcond_ca_qw, L1_xcond_ca_qb, L1_xcond_ca_kw, L1_xcond_ca_kb, L1_xcond_ca_vw, L1_xcond_ca_vb, L1_xcond_ca_ow, L1_xcond_ca_ob, L1_xcond_ffn_w1, L1_xcond_ffn_b1, L1_xcond_ffn_w2, L1_xcond_ffn_b2):
    import jax
    import jax.numpy as jnp

    def _L0_xcond_ref(x_q, x_kv, t_vec, Wq, bq, Wkv, bkv, Wp, bp, Wss_q, bss_q, Wss_kv, bss_kv):
        import jax, jax.numpy as jnp
        import numpy as np
        EPS = 1e-05

        def _ada_ln(x, c, W_ss, b_ss):
            mu = jnp.mean(x, axis=-1, keepdims=True)
            var = jnp.mean((x - mu) ** 2, axis=-1, keepdims=True)
            h = (x - mu) / jnp.sqrt(var + EPS)
            ss = jax.nn.silu(c) @ W_ss + b_ss
            scale, bias = jnp.split(ss, 2, axis=-1)
            return (1.0 + scale)[:, None, :] * h + bias[:, None, :]
        B, Lq, H = x_q.shape
        Lkv = x_kv.shape[1]
        nh = 16
        dh = H // nh
        xq = _ada_ln(x_q, t_vec, Wss_q, bss_q)
        xkv = _ada_ln(x_kv, t_vec, Wss_kv, bss_kv)
        q = (xq @ Wq + bq).reshape(B, Lq, nh, dh)
        kv = (xkv @ Wkv + bkv).reshape(B, Lkv, 2, nh, dh)
        k = kv[:, :, 0]
        v = kv[:, :, 1]
        scores = jnp.einsum('bqhd,bkhd->bhqk', q, k) / jnp.sqrt(jnp.float32(dh))
        attn = jax.nn.softmax(scores, axis=-1)
        out = jnp.einsum('bhqk,bkhd->bqhd', attn, v).reshape(B, Lq, H)
        return x_q + (out @ Wp + bp)

    def _L1_xcond_ref(x, u, t_emb, ln1_g, ln1_b, aff1_w, aff1_b, ln2_g, ln2_b, aff2_w, aff2_b, sa_qw, sa_qb, sa_kw, sa_kb, sa_vw, sa_vb, sa_ow, sa_ob, ca_qw, ca_qb, ca_kw, ca_kb, ca_vw, ca_vb, ca_ow, ca_ob, ffn_w1, ffn_b1, ffn_w2, ffn_b2):
        import jax, jax.numpy as jnp
        import numpy as np
        D = 256
        H = 16
        DH = D // H
        DFF = 1024
        B = 2
        L = 512
        EPS = 1e-05

        def layer_norm(x, g, b):
            mu = jnp.mean(x, axis=-1, keepdims=True)
            var = jnp.mean(jnp.square(x - mu), axis=-1, keepdims=True)
            return (x - mu) * jax.lax.rsqrt(var + EPS) * g + b

        def ada_ln(x, t_emb, ln_g, ln_b, aff_w, aff_b):
            normed = layer_norm(x, ln_g, ln_b)
            affine = t_emb @ aff_w + aff_b
            gamma, beta = jnp.split(affine, 2, axis=-1)
            return gamma[:, None, :] * normed + beta[:, None, :]

        def mha(q_in, k_in, v_in, qw, qb, kw, kb, vw, vb, ow, ob):
            Bq, Lq, _ = q_in.shape
            Lk = k_in.shape[1]
            Q = (q_in @ qw + qb).reshape(Bq, Lq, H, DH)
            K = (k_in @ kw + kb).reshape(Bq, Lk, H, DH)
            V = (v_in @ vw + vb).reshape(Bq, Lk, H, DH)
            scores = jnp.einsum('bqhd,bkhd->bhqk', Q, K) / np.sqrt(DH).astype(np.float32)
            attn = jax.nn.softmax(scores, axis=-1)
            out = jnp.einsum('bhqk,bkhd->bqhd', attn, V).reshape(Bq, Lq, D)
            return out @ ow + ob
        xn = ada_ln(x, t_emb, ln1_g, ln1_b, aff1_w, aff1_b)
        x = x + mha(xn, xn, xn, sa_qw, sa_qb, sa_kw, sa_kb, sa_vw, sa_vb, sa_ow, sa_ob)
        x = x + mha(x, u, u, ca_qw, ca_qb, ca_kw, ca_kb, ca_vw, ca_vb, ca_ow, ca_ob)
        xn = ada_ln(x, t_emb, ln2_g, ln2_b, aff2_w, aff2_b)
        h = jax.nn.gelu(xn @ ffn_w1 + ffn_b1, approximate=False)
        x = x + (h @ ffn_w2 + ffn_b2)
        return x
    x = _L0_xcond_ref(x, ctx_1024, cond_1024, L0_xcond_Wq, L0_xcond_bq, L0_xcond_Wkv, L0_xcond_bkv, L0_xcond_Wp, L0_xcond_bp, L0_xcond_Wss_q, L0_xcond_bss_q, L0_xcond_Wss_kv, L0_xcond_bss_kv)
    x = _L1_xcond_ref(x, ctx_1024, cond_1024, L1_xcond_ln1_g, L1_xcond_ln1_b, L1_xcond_aff1_w, L1_xcond_aff1_b, L1_xcond_ln2_g, L1_xcond_ln2_b, L1_xcond_aff2_w, L1_xcond_aff2_b, L1_xcond_sa_qw, L1_xcond_sa_qb, L1_xcond_sa_kw, L1_xcond_sa_kb, L1_xcond_sa_vw, L1_xcond_sa_vb, L1_xcond_sa_ow, L1_xcond_sa_ob, L1_xcond_ca_qw, L1_xcond_ca_qb, L1_xcond_ca_kw, L1_xcond_ca_kb, L1_xcond_ca_vw, L1_xcond_ca_vb, L1_xcond_ca_ow, L1_xcond_ca_ob, L1_xcond_ffn_w1, L1_xcond_ffn_b1, L1_xcond_ffn_w2, L1_xcond_ffn_b2)
    return x

_drawn_inputs = setup_inputs


def setup_inputs(seed=0):
    import zlib

    import numpy as np

    out = dict(_drawn_inputs(seed))
    spreads = {'L0_xcond_bq': (0.0, 2.0),
     'L0_xcond_bkv': (0.0, 0.1),
     'L0_xcond_bp': (0.0, 0.1),
     'L0_xcond_bss_q': (0.0, 0.8),
     'L0_xcond_bss_kv': (0.0, 0.664),
     'L1_xcond_ln1_g': (1.0, 0.6),
     'L1_xcond_ln1_b': (0.0, 0.8),
     'L1_xcond_aff1_b': (0.0, 0.723),
     'L1_xcond_ln2_g': (1.0, 0.6),
     'L1_xcond_ln2_b': (0.0, 0.8),
     'L1_xcond_aff2_b': (0.0, 0.514),
     'L1_xcond_sa_qb': (0.0, 0.8),
     'L1_xcond_sa_kb': (0.0, 2.0),
     'L1_xcond_sa_vb': (0.0, 0.1),
     'L1_xcond_sa_ob': (0.0, 0.1),
     'L1_xcond_ca_qb': (0.0, 0.8),
     'L1_xcond_ca_kb': (0.0, 2.0),
     'L1_xcond_ca_vb': (0.0, 0.273),
     'L1_xcond_ca_ob': (0.0, 0.1),
     'L1_xcond_ffn_b1': (0.0, 0.1),
     'L1_xcond_ffn_b2': (0.0, 0.1)}
    factors = {'L0_xcond_Wq': 8.0,
     'L0_xcond_Wss_q': 8.0,
     'L1_xcond_sa_qw': 8.0,
     'L1_xcond_sa_kw': 8.0,
     'L1_xcond_ca_qw': 8.0,
     'L1_xcond_ca_kw': 8.0}
    for name, (base, spread) in spreads.items():
        noise = np.random.default_rng([zlib.crc32(name.encode()), seed]).standard_normal(out[name].shape)
        drawn = base * np.exp(spread * noise) if base else spread * noise
        out[name] = jnp.asarray(drawn.astype(out[name].dtype))
    for name, factor in factors.items():
        out[name] = (out[name] * factor).astype(out[name].dtype)
    return out
```

```python
from contextlib import ExitStack

import concourse.bass as bass
from concourse import mybir

ALU = mybir.AluOpType
ACT = mybir.ActivationFunctionType
AX = mybir.AxisListType
F32 = mybir.dt.float32
BF16 = mybir.dt.bfloat16
I32 = mybir.dt.int32
ds = bass.ds

P = 128
NB = 2
L = 1024
D = 256
H = 16
DH = D // H
LK = 64
FF = 1024
EPS = 1e-5
NEWTON = 3
NORM_STEPS = 7 + 3 * NEWTON
SCALE = 1.0 / DH ** 0.5

DB = D // P
CH = 512
NC = L // CH
QB = CH // P
TB = L // P
HB = H // DB
NP = H // 2
PB = NP // DB
FB = FF // P

HG = 4
NG = H // HG
QT = HG * TB
STEPS = NC * TB
A_STEPS = STEPS - 2
PARTS = 3
PR = 32
Q_TERMS = (0, 0, 0, 1, 1, 2)
K_TERMS = (0, 1, 2, 0, 1, 0)
ROWS = len(Q_TERMS) * DH
ROWS_M = ROWS + PARTS

VECS = (("cond_1024", 4), ("L0_xcond_bq", 2), ("L0_xcond_bkv", 4), ("L0_xcond_bss_q", 4), ("L0_xcond_bss_kv", 4),
        ("L1_xcond_aff1_b", 4), ("L1_xcond_aff2_b", 4), ("L1_xcond_ln1_g", 2), ("L1_xcond_ln1_b", 2),
        ("L1_xcond_ln2_g", 2), ("L1_xcond_ln2_b", 2), ("L1_xcond_sa_qb", 2), ("L1_xcond_sa_kb", 2),
        ("L1_xcond_ca_qb", 2), ("L1_xcond_ca_kb", 2), ("L1_xcond_ffn_b1", 8))
VCOL = {}
for _name, _rows in VECS:
    VCOL[_name] = sum(r for n, r in VECS[:len(VCOL)])
NVEC = sum(r for _, r in VECS)
BROAD = ("L0_xcond_bv", "L0_xcond_bp", "L1_xcond_sa_vb", "L1_xcond_sa_ob", "L1_xcond_ca_vb", "L1_xcond_ca_ob",
         "L1_xcond_ffn_b2")
ADA = (("L0_xcond_Wss_q", "L0_xcond_bss_q"), ("L0_xcond_Wss_kv", "L0_xcond_bss_kv"),
       ("L1_xcond_aff1_w", "L1_xcond_aff1_b"), ("L1_xcond_aff2_w", "L1_xcond_aff2_b"))
ADA_Q, ADA_KV, ADA_1, ADA_2 = range(4)


def build(nc, t, out):
    with ExitStack() as ctx:
        def sb(name, shape, dt=F32):
            return ctx.enter_context(nc.sbuf_tensor(name, shape, dt))

        def sem(name):
            return ctx.enter_context(nc.semaphore(name))

        def sems(name, n=NB):
            return [sem(f"{name}_{k}") for k in range(n)]

        q_parts = nc.dram_tensor("q_parts", [H, PARTS * DH, NB * L], BF16, kind="Internal").ap()
        k_parts = nc.dram_tensor("k_parts", [H, PARTS * DH, NB * L], BF16, kind="Internal").ap()
        att_sums = nc.dram_tensor("att_sums", [NG, P, NB * L], F32, kind="Internal").ap()

        x_tok = sb("x_tok", [P, NB * TB, D])
        xh = sb("xh", [P, NB, QB, D])
        xT = sb("xT", [P, NB, DB, CH])
        qT = sb("qT", [P, NB, DB, CH])
        kbd_ca = sb("kbd_ca", [P, NB, DB, HB * LK])
        vbd_ca = sb("vbd_ca", [P, NB, NP, 2 * DH])
        probs = sb("probs", [P, 2 * HG, CH])
        w_q0 = sb("w_q0", [P, DB, D])
        w_kv0 = sb("w_kv0", [P, DB, 2 * D])
        w_p0 = sb("w_p0", [P, DB, D])
        w_sa = sb("w_sa", [P, 4, DB, D])
        w_ca = sb("w_ca", [P, 4, DB, D])
        v_area = sb("v_area", [P, NB * TB * H * 2 * DH])
        v_grp = sb("v_grp", [P, NB, TB, HG, 2 * DH])
        arena = sb("arena", [P, 6 * HG * L // 2])
        bc = sb("bc", [P, len(BROAD), D])
        vrow = sb("vrow", [NVEC, P])
        vec = sb("vec", [P, NVEC])
        silu = sb("silu", [P, 3, 4])
        ss = sb("ss", [P, 4, 4, NB])
        ada_a = sb("ada_a", [P, 4, DB, NB])
        ada_b = sb("ada_b", [P, 4, DB, NB])
        ident = sb("ident", [P, P])
        ident_h = sb("ident_h", [P, P], BF16)
        head_mask = sb("head_mask", [P, HB])
        half_mask = sb("half_mask", [P, 2])
        ones_bd = sb("ones_bd", [P, 2, DH])
        pick = sb("pick", [PARTS * PR, NP, 2, LK], BF16)
        stats = sb("stats", [P, NB, QB, 6])
        mean = sb("mean", [P, NB, QB])
        rstd = sb("rstd", [P, NB, QB])
        newton = sb("newton", [P, 4, QB])
        negmax = sb("negmax", [P, NB, QB, H])
        max_rest = sb("max_rest", [P, NB, QB, H])
        max_parts = sb("max_parts", [P, NB, QB, PARTS * PR], BF16)
        maxT = sb("maxT", [PARTS * PR, NB, CH], BF16)
        recip = sb("recip", [P, NB, CH])
        negmax_g = sb("negmax_g", [P, QT])
        max_rest_g = sb("max_rest_g", [P, QT])
        max_parts_g = sb("max_parts_g", [P, PARTS, QT], BF16)
        maxT_g = sb("maxT_g", [PARTS * QT, P], BF16)
        sums = sb("sums", [P, NC, CH])

        def view(area, at, *shape):
            n = 1
            for k in shape:
                n *= k
            names = "abcde"[:len(shape)]
            sizes = dict(zip(names, shape))
            return area[:, at:at + n].rearrange(f"p ({' '.join(names)}) -> p {' '.join(names)}", **sizes)

        w_ada = view(v_area, 0, 4, DB, 2 * D)
        v_all = view(v_area, 0, NB * TB, H, 2 * DH)
        hidT = view(v_area, 0, NB, FB, CH)
        p_area = probs[:].rearrange("p a n -> p (a n)")
        ctx_tok = view(p_area, 0, D)
        ctx_hat = view(p_area, D, D)
        ctxT = view(p_area, 2 * D, 2, DB, NB, 2, LK)
        ktx = view(p_area, 6 * D, 2, DB, NB, LK)
        vtx = view(p_area, 8 * D, 2, NB, D)
        q_full = view(p_area, 0, NB, 4, CH)
        outT = view(arena, 0, NB, DB, CH)
        xc = view(arena, 2048, NB, QB, D)
        kbd_0 = view(arena, 4096, NB, DB, HB * LK)
        vbd_0 = view(arena, 6144, NB, NP, 2 * DH)
        attT = view(arena, 4096, NB, DB, CH)
        denT = view(arena, 6144, NB, DB, CH)
        w_1 = view(arena, 8192, DB, FF)
        w_2 = view(arena, 10240, FB, D)

        def half_view(at, *shape):
            n = 1
            for k in shape:
                n *= k
            names = "abc"[:len(shape)]
            return arena[:, at:at + n // 2].bitcast(BF16).rearrange(
                f"p ({' '.join(names)}) -> p {' '.join(names)}", **dict(zip(names, shape)))

        parts = half_view(2048, NB * 4, PARTS, CH)
        qa = half_view(0, HG, L)
        ka = half_view(2048, HG, L)
        qs = [half_view(4096 + 2048 * b, HG, L) for b in range(NB)]
        ks = [half_view(8192 + 2048 * b, HG, L) for b in range(NB)]

        ps = ctx.enter_context(nc.psum_tensor("ps", [P, 8, CH], F32))

        def bank(b, k):
            return ps[:, 4 * b + k, :]

        vec_in, x_in, ctx_in, bc_in = sem("vec_in"), sem("x_in"), sem("ctx_in"), sem("bc_in")
        w_ada_in, w_kv_in, w_0_in, w_sa_in, w_ca_in, w_mlp_in = (
            sem("w_ada_in"), sem("w_kv_in"), sem("w_0_in"), sem("w_sa_in"), sem("w_ca_in"), sem("w_mlp_in"))
        consts_made, mask_step = sem("consts_made"), sem("mask_step")
        vec_full, vec_ready, silu_step, silu_exp, silu_ready = (
            sem("vec_full"), sem("vec_ready"), sem("silu_step"), sem("silu_exp"), sem("silu_ready"))
        ss_full, ss_step, ada_ready = sem("ss_full"), sem("ss_step"), sem("ada_ready")
        ctx_step, ctx_hat_ready, ctxT_full, ctxT_ready = (
            sem("ctx_step"), sem("ctx_hat_ready"), sem("ctxT_full"), sem("ctxT_ready"))
        ctx_k_full, ctx_v_full, ktx_ready, vtx_ready, ctx_ready = (
            sem("ctx_k_full"), sem("ctx_v_full"), sem("ktx_ready"), sem("vtx_ready"), sem("ctx_ready"))
        v_ones = sem("v_ones")

        def phase(name, *what):
            return {w: sems(f"{name}_{w}") for w in what}

        cross = ("xT_full", "xT_ready", "q_full", "q_ready", "s_full", "max_done", "split_step", "split_done",
                 "maxT_full", "maxT_ready", "st_full", "exp_done", "pv_full", "recip_step", "outT_ready",
                 "o_full", "biased", "added", "norm_step", "normed")
        px = phase("x", *cross)
        p2 = phase("qkv", "norm_step", "normed", "xT_full", "xT_ready", "qk_full", "qk_taken", "split_step",
                   "parts_ready", "parts_out", "v_full", "v_ready")
        p4 = phase("l1", "att_in", "att_recip", "attT_ready", "so_full", "x1_in", "x2_ready",
                   "hT_full", "hT_ready", "hid_full", "hid_ready", "y_full", "b2_added", "y_ready", "y_out")

        stack_a = sems("stack_a", HG)
        stack_s, shift_in, v_grp_ready = sems("stack_s"), sems("shift_in"), sems("v_grp_ready")
        sa_s_full, sa_max_done, sa_split_step, sa_split_done, sa_maxT_full, sa_maxT_ready = (
            sem("sa_s_full"), sem("sa_max_done"), sem("sa_split_step"), sem("sa_split_done"),
            sem("sa_maxT_full"), sem("sa_maxT_ready"))
        sa_st_full, sa_exp_done, sa_pv_done = sem("sa_st_full"), sem("sa_exp_done"), sem("sa_pv_done")
        sums_taken, sums_out = sems("sums_taken", NC), sems("sums_out", NC)
        ones_rows = sem("ones_rows")

        HALVES = NG * NB
        PARTS_OUT = 16 * PARTS * 4 * NC

        def tile_plan(s):
            upto = [min(QT, -(-QT * k // A_STEPS)) for k in (s, s + 1)]
            return list(range(*upto))

        block = ctx.enter_context(nc.Block())

        @block.sync
        def _(sp):
            for name, rows in VECS:
                src = t[name]
                src = (src.rearrange("b (k p) -> (b k) p", p=P) if name == "cond_1024"
                       else src.rearrange("(k p) -> k p", p=P))
                sp.dma_start(vrow[VCOL[name]:VCOL[name] + rows, :], src).then_inc(vec_in, 16)
            sp.dma_start(ctx_tok, t["ctx_1024"].rearrange("b k d -> (b k) d")).then_inc(ctx_in, 16)
            for k, (w, _) in enumerate(ADA):
                sp.dma_start(w_ada[:, k], t[w].rearrange("(k p) n -> p k n", p=P)).then_inc(w_ada_in, 16)
            x_dram = t["x"].rearrange("b (n p) d -> p (b n) d", p=P)
            for b in range(NB):
                sp.dma_start(x_tok[:, b * TB:(b + 1) * TB], x_dram[:, b * TB:(b + 1) * TB]).then_inc(x_in, 16)
            for w, name, s in ((w_kv0, "L0_xcond_Wkv", w_kv_in), (w_ca[:, 1], "L1_xcond_ca_kw", w_kv_in),
                               (w_ca[:, 2], "L1_xcond_ca_vw", w_kv_in), (w_q0, "L0_xcond_Wq", w_0_in),
                               (w_p0, "L0_xcond_Wp", w_0_in), (w_sa[:, 0], "L1_xcond_sa_qw", w_sa_in),
                               (w_sa[:, 1], "L1_xcond_sa_kw", w_sa_in), (w_sa[:, 2], "L1_xcond_sa_vw", w_sa_in),
                               (w_sa[:, 3], "L1_xcond_sa_ow", w_sa_in), (w_ca[:, 0], "L1_xcond_ca_qw", w_ca_in),
                               (w_ca[:, 3], "L1_xcond_ca_ow", w_ca_in)):
                sp.dma_start(w if w is w_ca[:, 1] else w[:], t[name].rearrange("(k p) n -> p k n", p=P)).then_inc(s, 16)

            with sp.Fori(0, NC) as c:
                for b in range(NB):
                    for u in range(4):
                        dst, d = (q_parts, k_parts)[u // DB], u % DB
                        sp.wait_ge(p2["parts_ready"][b], c * 4 + u + 1)
                        for part in range(PARTS):
                            to = dst[d * HB:(d + 1) * HB, part * DH:(part + 1) * DH, ds(c * CH + b * L, CH)]
                            sp.dma_start(to, parts[:, b * 4 + u, part, :]).then_inc(p2["parts_out"][b], 16)

            def load_rows(dst, src, heads, n, terms, b, done):
                k = 0
                while k < len(terms):
                    m = 1
                    while k + m < len(terms) and terms[k + m] == terms[k] + m:
                        m += 1
                    rows = src[ds(heads, n), terms[k] * DH:(terms[k] + m) * DH, b * L:(b + 1) * L]
                    to = dst[k * DH:(k + m) * DH]
                    sp.dma_start(to, rows.rearrange("j r n -> r j n")).then_inc(done, 16)
                    k += m

            def load_stack_a(g, b, j):
                load_rows(qa[:, j:j + 1], q_parts, g * HG + j, 1, Q_TERMS, b, stack_a[j])
                load_rows(ka[:, j:j + 1], k_parts, g * HG + j, 1, K_TERMS, b, stack_a[j])

            def load_stack_s(g, b):
                load_rows(qs[b], q_parts, g * HG, HG, Q_TERMS, b, stack_s[b])
                load_rows(ks[b], k_parts, g * HG, HG, K_TERMS, b, stack_s[b])

            def load_shift(a, b):
                sp.wait_ge(sa_maxT_ready, a + 1)
                for part in range(PARTS):
                    row = qs[b][ROWS + part:ROWS + part + 1].rearrange("o j (q n) -> o (j q) n", n=P)
                    sp.dma_start(row, maxT_g[part * QT:(part + 1) * QT, :]).then_inc(shift_in[b], 16)

            for b in range(NB):
                sp.wait_ge(p2["parts_out"][b], PARTS_OUT)
            for j in range(HG):
                load_stack_a(0, 0, j)
            load_stack_s(0, 0)
            for j in range(HG):
                sp.wait_ge(sa_s_full, TB * (j + 1))
                load_stack_a(0, 1, j)
            load_shift(0, 0)
            load_stack_s(0, 1)
            with sp.Fori(0, NG - 1) as g:
                for b in range(NB):
                    half = g * NB + b
                    for j in range(HG):
                        sp.wait_ge(sa_s_full, (half + 1) * QT + TB * (j + 1))
                        load_stack_a(g + 1, b, j)
                    load_shift(half + 1, 1 - b)
                    sp.wait_ge(sa_st_full, (half + 1) * STEPS * HG)
                    load_stack_s(g + 1, b)
            load_shift(HALVES - 1, NB - 1)

            sp.wait_ge(sa_st_full, HALVES * STEPS * HG)
            sp.dma_start(w_1, t["L1_xcond_ffn_w1"].rearrange("(k p) n -> p k n", p=P)).then_inc(w_mlp_in, 16)
            sp.dma_start(w_2, t["L1_xcond_ffn_w2"].rearrange("(k p) n -> p k n", p=P)).then_inc(w_mlp_in, 16)
            for ch in range(NC):
                sp.wait_ge(sums_out[ch], 16 * HALVES)
            out_tok = out.rearrange("b (n p) d -> p (b n) d", p=P)
            with sp.Fori(0, NC) as c:
                for b in range(NB):
                    sp.wait_ge(p4["so_full"][b], c * 2)
                    for h in range(H):
                        row = (h % HB) * DH
                        grp = att_sums[h // HG, :, ds(c * CH + b * L, CH)]
                        o = (h % HG) * 2 * DH
                        sp.dma_start(attT[row:row + DH, b, h // HB, :], grp[o:o + DH]).then_inc(p4["att_in"][b], 16)
                        sp.dma_start(denT[row:row + DH, b, h // HB, :],
                                     grp[o + DH:o + 2 * DH]).then_inc(p4["att_in"][b], 16)
                for b in range(NB):
                    sp.wait_ge(p4["y_ready"][b], (c + 1) * 2)
                    sp.dma_start(out_tok[:, ds(c * QB + b * TB, QB), :], xc[:, b]).then_inc(p4["y_out"][b], 16)
            for b in range(NB):
                sp.wait_ge(p4["y_out"][b], 16 * NC)

        @block.gpsimd
        def _(pool):
            names = {"L0_xcond_bv": t["L0_xcond_bkv"][D:2 * D]}
            for k, name in enumerate(BROAD):
                src = names.get(name, None)
                src = t[name] if src is None else src
                pool.dma_start(bc[:, k], src.partition_broadcast(P)).then_inc(bc_in, 16)
            nc.gpsimd.memset(max_parts[:], 0.0)
            nc.gpsimd.memset(ident[:], 0.0)
            nc.gpsimd.memset(head_mask[:], 1.0)
            nc.gpsimd.memset(half_mask[:], 1.0)
            nc.gpsimd.memset(ones_bd[:], 1.0)
            nc.gpsimd.memset(pick[:], 0.0).then_inc(mask_step, 1)
            pool.wait_ge(mask_step, 1)
            nc.gpsimd.affine_select(out=ident[:], in_=ident[:], compare_op=ALU.not_equal, fill=1.0, base=0,
                                    pattern=[[-1, P]], channel_multiplier=1)
            for tile, pat, width in ((head_mask, [[-DH, HB]], DH), (half_mask, [[-LK, 2]], LK),
                                     (ones_bd, [[-LK, 2], [0, DH]], LK)):
                nc.gpsimd.affine_select(out=tile[:], in_=tile[:], compare_op=ALU.is_ge, fill=0.0, base=0,
                                        pattern=pat, channel_multiplier=1)
            for part in range(PARTS):
                last = nc.gpsimd.affine_select(out=pick[:], in_=pick[:], compare_op=ALU.not_equal, fill=1.0,
                                               base=-part * PR, pattern=[[-2, NP], [-1, 2], [0, LK]],
                                               channel_multiplier=1)
                if part < PARTS - 1:
                    last.then_inc(mask_step, 1)
                    pool.wait_ge(mask_step, part + 2)
            last.then_inc(mask_step, 1)
            pool.wait_ge(mask_step, PARTS + 1)
            for tile, pat, width in ((head_mask, [[DH, HB]], DH), (half_mask, [[LK, 2]], LK),
                                     (ones_bd, [[LK, 2], [0, DH]], LK)):
                nc.gpsimd.affine_select(out=tile[:], in_=tile[:], compare_op=ALU.is_ge, fill=0.0, base=width - 1,
                                        pattern=pat, channel_multiplier=-1)
            nc.gpsimd.tensor_copy(ident_h[:], ident[:]).then_inc(consts_made, 1)

            pool.wait_ge(ss_full, 1)
            nc.gpsimd.memset(v_all[:, :, :, DH:2 * DH], 1.0).then_inc(v_ones, 1)

            pool.wait_ge(bc_in, 16 * len(BROAD))
            with pool.Fori(0, NC) as c:
                for b in range(NB):
                    pool.wait_ge(px["normed"][b], c + 1)
                    rows = x_tok[:, ds(c * QB + b * TB, QB), :]
                    bias = bc[:, BROAD.index("L0_xcond_bp")].unsqueeze(1).to_broadcast([P, QB, D])
                    nc.gpsimd.tensor_tensor(rows, rows, bias, ALU.add).then_inc(px["biased"][b], 1)

            for b in range(NB):
                pool.wait_ge(p2["parts_out"][b], PARTS_OUT)
                nc.gpsimd.memset(ks[b][ROWS:ROWS_M], 1.0).then_inc(ones_rows, 1)

            def take_values(g, b):
                src = v_all[:, b * TB:(b + 1) * TB, ds(g * HG, HG), :]
                nc.gpsimd.tensor_copy(v_grp[:, b], src).then_inc(v_grp_ready[b], 1)

            def store_sums(g, b, ch):
                pool.wait_ge(sums_taken[ch], g * NB + b + 1)
                dst = att_sums[ds(g, 1), :, b * L + ch * CH:b * L + (ch + 1) * CH]
                pool.dma_start(dst.rearrange("o p n -> (o p) n"), sums[:, ch]).then_inc(sums_out[ch], 16)

            pool.wait_ge(ones_rows, NB)
            for b in range(NB):
                pool.wait_ge(p2["v_ready"][b], 2 * NC)
                take_values(0, b)
            with pool.Fori(0, NG - 1) as g:
                for b in range(NB):
                    for ch in range(NC):
                        store_sums(g, b, ch)
                    pool.wait_ge(sa_pv_done, (g * NB + b + 1) * STEPS)
                    take_values(g + 1, b)
            for b in range(NB):
                for ch in range(NC):
                    store_sums(NG - 1, b, ch)

            def add_bias(name, b, done):
                bias = bc[:, BROAD.index(name)].unsqueeze(1).to_broadcast([P, QB, D])
                nc.gpsimd.tensor_tensor(xc[:, b], xc[:, b], bias, ALU.add).then_inc(done[b], 1)

            with pool.Fori(0, NC) as c:
                n = c + NC
                for b in range(NB):
                    pool.wait_ge(p4["y_out"][b], c * 16)
                    bias = bc[:, BROAD.index("L1_xcond_sa_ob")].unsqueeze(1).to_broadcast([P, QB, D])
                    nc.gpsimd.tensor_tensor(xc[:, b], x_tok[:, ds(c * QB + b * TB, QB), :], bias,
                                            ALU.add).then_inc(p4["x1_in"][b], 1)
                for b in range(NB):
                    pool.wait_ge(px["xT_full"][b], (n + 1) * DB)
                    add_bias("L1_xcond_ca_ob", b, px["biased"])
                for b in range(NB):
                    pool.wait_ge(px["normed"][b], n + 1)
                    add_bias("L1_xcond_ffn_b2", b, p4["b2_added"])

        @block.tensor
        def _(pe):
            def transpose_rows(src, b, k0, done):
                for d in range(DB):
                    for i in range(QB):
                        last = nc.tensor.transpose(bank(b, k0 + d)[:, i * P:(i + 1) * P],
                                                   src[:, b, i, d * P:(d + 1) * P], ident[:])
                    last.then_inc(done[b], 1)

            def project(w, b, k0, done):
                for o in range(DB):
                    for d in range(DB):
                        last = nc.tensor.matmul(bank(b, k0 + o), w[:, d, o * P:(o + 1) * P], xT[:, b, d, :],
                                                start=(d == 0), stop=(d == DB - 1))
                    last.then_inc(done[b], 1)

            def project_rows(src, w, n, b, k0, done):
                for i in range(QB):
                    for d in range(n):
                        last = nc.tensor.matmul(bank(b, k0 + i // 2)[:, (i % 2) * D:(i % 2 + 1) * D],
                                                src[:, b, d, i * P:(i + 1) * P], w[:, d, :],
                                                start=(d == 0), stop=(d == n - 1))
                    if i % 2:
                        last.then_inc(done[b], 1)

            def scores(ph, kbd, c, b):
                pe.wait_ge(ph["q_ready"][b], (c + 1) * DB)
                for i in range(QB):
                    for d in range(DB):
                        u = i * DB + d
                        if u >= 2:
                            pe.wait_ge(ph["max_done"][b], c * QB * DB + u - 1)
                        nc.tensor.matmul(bank(b, u % 2), qT[:, b, d, i * P:(i + 1) * P], kbd[:, b, d, :],
                                         start=True, stop=True).then_inc(ph["s_full"][b], 1)

            def attend(ph, kbd, vbd, c, b):
                pe.wait_ge(ph["split_done"][b], c + 1)
                turned = bank(b, 2)[0:PARTS * PR, 0:CH // 2].bitcast(BF16)
                for i in range(QB):
                    last = nc.tensor.transpose(turned[:, i * P:(i + 1) * P], max_parts[:, b, i, :], ident_h[:])
                last.then_inc(ph["maxT_full"][b], 1)
                pe.wait_ge(ph["maxT_ready"][b], c + 1)
                for d in range(DB):
                    for k in range(PB):
                        p = d * PB + k
                        if p >= 2:
                            pe.wait_ge(ph["exp_done"][b], c * NP + p - 1)
                        nc.tensor.matmul(bank(b, p % 2), kbd[:, b, d, k * P:(k + 1) * P], qT[:, b, d, :],
                                         start=True, stop=False)
                        nc.tensor.matmul(bank(b, p % 2), pick[:, p].rearrange("r e k -> r (e k)"), maxT[:, b, :],
                                         start=False, stop=True).then_inc(ph["st_full"][b], 1)
                    pe.wait_ge(ph["exp_done"][b], c * NP + (d + 1) * PB)
                    pe.wait_ge(ph["outT_ready"][b], c * DB + d)
                    for k in range(PB):
                        nc.tensor.matmul(bank(b, 2)[32 * k:32 * k + 32, :], vbd[:, b, d * PB + k, :],
                                         probs[:, d * PB + k, :], start=True, stop=True)
                    for k in range(PB):
                        last = nc.tensor.matmul(bank(b, 3)[32 * k:32 * k + 32, :],
                                                ones_bd[:].rearrange("p e k -> p (e k)"),
                                                probs[:, d * PB + k, :], start=True, stop=True)
                    last.then_inc(ph["pv_full"][b], 1)

            pe.wait_ge(consts_made, 1)
            pe.wait_ge(vec_in, 16 * len(VECS))
            nc.tensor.transpose(ps[:, 0, 0:NVEC], vrow[:], ident[0:NVEC, 0:NVEC]).then_inc(vec_full, 1)
            pe.wait_ge(ctx_hat_ready, 1)
            for k, src in enumerate((ctx_hat, ctx_tok)):
                for d in range(DB):
                    last = nc.tensor.transpose(ps[:, 2, (k * DB + d) * P:(k * DB + d + 1) * P],
                                               src[:, d * P:(d + 1) * P], ident[:])
            last.then_inc(ctxT_full, 1)
            pe.wait_ge(w_ada_in, 16 * len(ADA))
            pe.wait_ge(silu_ready, 1)
            cond = vec[:, 0:4].rearrange("p (b k) -> p k b", b=NB)
            silu_c = silu[:, 2, :].rearrange("p (b k) -> p k b", b=NB)
            for n in range(len(ADA)):
                for o in range(4):
                    for d in range(DB):
                        last = nc.tensor.matmul(ps[:, 1, (n * 4 + o) * NB:(n * 4 + o + 1) * NB],
                                                w_ada[:, n, d, o * P:(o + 1) * P],
                                                (silu_c if n in (ADA_Q, ADA_KV) else cond)[:, d, :],
                                                start=(d == 0), stop=(d == DB - 1))
            last.then_inc(ss_full, 1)
            pe.wait_ge(ctxT_ready, 2)
            pe.wait_ge(w_kv_in, 16 * 3)
            key_w, val_w = (w_kv0[:, :, 0:D], w_ca[:, 1]), (w_kv0[:, :, D:2 * D], w_ca[:, 2])
            for a in range(2):
                for o in range(DB):
                    for b in range(NB):
                        for d in range(DB):
                            last = nc.tensor.matmul(ps[:, 3, ((a * DB + o) * NB + b) * LK:((a * DB + o) * NB + b + 1) * LK],
                                                    key_w[a][:, d, o * P:(o + 1) * P], ctxT[:, a, d, b, 0, :],
                                                    start=(d == 0), stop=(d == DB - 1))
            last.then_inc(ctx_k_full, 1)
            for a in range(2):
                for b in range(NB):
                    for d in range(DB):
                        last = nc.tensor.matmul(ps[:, 4 + a, b * D:(b + 1) * D],
                                                ctxT[:, a, d, b].rearrange("p e k -> p (e k)"), val_w[a][:, d, :],
                                                start=(d == 0), stop=(d == DB - 1))
            last.then_inc(ctx_v_full, 1)
            pe.wait_ge(vtx_ready, 2)
            pe.wait_ge(ktx_ready, 1)
            pe.wait_ge(ss_step, 1)

            pe.wait_ge(ctx_ready, 2)
            pe.wait_ge(w_0_in, 16 * 2)
            with pe.Fori(0, NC) as c:
                for b in range(NB):
                    pe.wait_ge(px["normed"][b], c + 1)
                    pe.wait_ge(px["added"][b], c * 2)
                    transpose_rows(xh, b, 0, px["xT_full"])
                for b in range(NB):
                    pe.wait_ge(px["xT_ready"][b], (c + 1) * DB)
                    project(w_q0, b, 2, px["q_full"])
                for b in range(NB):
                    scores(px, kbd_0, c, b)
                for b in range(NB):
                    attend(px, kbd_0, vbd_0, c, b)
                for b in range(NB):
                    pe.wait_ge(px["outT_ready"][b], (c + 1) * DB)
                    project_rows(outT, w_p0, DB, b, 0, px["o_full"])

            pe.wait_ge(w_sa_in, 16 * 4)
            with pe.Fori(0, NC) as c:
                for b in range(NB):
                    pe.wait_ge(p2["normed"][b], c + 1)
                    pe.wait_ge(p2["qk_taken"][b], c * 4)
                    transpose_rows(xh, b, 0, p2["xT_full"])
                for b in range(NB):
                    pe.wait_ge(p2["xT_ready"][b], (c + 1) * DB)
                    pe.wait_ge(p2["v_ready"][b], c * 2)
                    project(w_sa[:, 0], b, 2, p2["qk_full"])
                for b in range(NB):
                    project(w_sa[:, 1], b, 0, p2["qk_full"])
                for b in range(NB):
                    pe.wait_ge(p2["qk_taken"][b], c * 4 + 2)
                    project_rows(xT, w_sa[:, 2], DB, b, 2, p2["v_full"])

            for b in range(NB):
                pe.wait_ge(p2["qk_taken"][b], 4 * NC)
                pe.wait_ge(p2["v_ready"][b], 2 * NC)

            def score_tile(a, n):
                j, q = n // TB, n % TB
                if q == 0:
                    pe.wait_ge(stack_a[j], (a + 1) * 16 * LOADS)
                if n == 0:
                    pe.wait_ge(sa_max_done, a * QT)
                    pe.wait_ge(sa_maxT_ready, a)
                elif n >= 2:
                    pe.wait_ge(sa_max_done, a * QT + n - 1)
                for k in range(2):
                    last = nc.tensor.matmul(ps[:, 4 + 2 * (n % 2) + k, :], qa[0:ROWS, j, q * P:(q + 1) * P],
                                            ka[0:ROWS, j, k * CH:(k + 1) * CH], start=True, stop=True)
                last.then_inc(sa_s_full, 1)

            def turn_maxima(a):
                pe.wait_ge(sa_split_done, a + 1)
                nc.tensor.transpose(ps[0:PARTS * QT, 4, 0:P // 2].bitcast(BF16),
                                    max_parts_g[:].rearrange("p a n -> p (a n)"), ident_h[:]).then_inc(sa_maxT_full, 1)

            def weigh(half, b, s):
                ch, kb = s // TB, s % TB
                pe.wait_ge(sa_exp_done, half * STEPS * HG + (s + 1) * HG)
                if s == 0:
                    pe.wait_ge(v_grp_ready[b], half_group(half, b) + 1)
                    pe.wait_ge(sums_taken[1], half)
                elif kb == 0:
                    pe.wait_ge(sums_taken[0], half + 1)
                for j in range(HG):
                    last = nc.tensor.matmul(ps[32 * j:32 * j + 32, 3, :], v_grp[:, b, kb, j, :],
                                            probs[:, (s % 2) * HG + j, :], start=(kb == 0), stop=(kb == TB - 1))
                last.then_inc(sa_pv_done, 1)

            groups = {}

            def half_group(half, b):
                return groups[b]

            def attend_group(g, b, more):
                half = g * NB + b
                groups[b] = g
                pe.wait_ge(stack_s[b], (g + 1) * 16 * LOADS)
                pe.wait_ge(shift_in[b], (g + 1) * 16 * PARTS)
                pe.wait_ge(sa_exp_done, half * STEPS * HG)
                for s in range(STEPS):
                    ch, kb = s // TB, s % TB
                    tiles = tile_plan(s) if more else []
                    for j in range(HG):
                        u = s * HG + j
                        if u >= 3:
                            pe.wait_ge(sa_exp_done, half * STEPS * HG + u - 2)
                        nc.tensor.matmul(ps[:, u % 3, :], ks[b][0:ROWS_M, j, kb * P:(kb + 1) * P],
                                         qs[b][0:ROWS_M, j, ch * CH:(ch + 1) * CH],
                                         start=True, stop=True).then_inc(sa_st_full, 1)
                        if j < len(tiles):
                            score_tile(half + 1, tiles[j])
                    if s == STEPS - 1 and more:
                        turn_maxima(half + 1)
                    if s > 0:
                        weigh(half, b, s - 1)
                weigh(half, b, STEPS - 1)

            pe.wait_ge(ones_rows, NB)
            for n in range(QT):
                score_tile(0, n)
            turn_maxima(0)
            with pe.Fori(0, NG - 1) as g:
                for b in range(NB):
                    attend_group(g, b, True)
            for b in range(NB):
                attend_group(NG - 1, b, b < NB - 1)

            pe.wait_ge(sa_exp_done, HALVES * STEPS * HG)
            pe.wait_ge(sa_max_done, HALVES * QT)
            pe.wait_ge(sa_maxT_ready, HALVES)
            for ch in range(NC):
                pe.wait_ge(sums_taken[ch], HALVES)
            pe.wait_ge(w_ca_in, 16 * 2)
            with pe.Fori(0, NC) as c:
                n = c + NC
                for b in range(NB):
                    pe.wait_ge(p4["attT_ready"][b], (c + 1) * DB)
                    pe.wait_ge(p4["y_ready"][b], c * 2)
                    project_rows(outT, w_sa[:, 3], DB, b, 2, p4["so_full"])
                for b in range(NB):
                    pe.wait_ge(p4["x2_ready"][b], (c + 1) * 2)
                    pe.wait_ge(p4["hid_ready"][b], c * FB)
                    transpose_rows(xc, b, 0, px["xT_full"])
                for b in range(NB):
                    pe.wait_ge(px["xT_ready"][b], (n + 1) * DB)
                    project(w_ca[:, 0], b, 2, px["q_full"])
                for b in range(NB):
                    scores(px, kbd_ca, n, b)
                for b in range(NB):
                    attend(px, kbd_ca, vbd_ca, n, b)
                for b in range(NB):
                    pe.wait_ge(px["outT_ready"][b], (n + 1) * DB)
                    project_rows(outT, w_ca[:, 3], DB, b, 0, px["o_full"])
                for b in range(NB):
                    pe.wait_ge(px["normed"][b], n + 1)
                    transpose_rows(xh, b, 2, p4["hT_full"])
                pe.wait_ge(w_mlp_in, 16 * 2)
                for b in range(NB):
                    pe.wait_ge(p4["hT_ready"][b], (c + 1) * DB)
                    for f in range(FB):
                        if f >= 2:
                            pe.wait_ge(p4["hid_ready"][b], c * FB + f - 1)
                        for d in range(DB):
                            last = nc.tensor.matmul(bank(b, f % 2), w_1[:, d, f * P:(f + 1) * P], xT[:, b, d, :],
                                                    start=(d == 0), stop=(d == DB - 1))
                        last.then_inc(p4["hid_full"][b], 1)
                for b in range(NB):
                    pe.wait_ge(p4["hid_ready"][b], (c + 1) * FB)
                    project_rows(hidT, w_2, FB, b, 2, p4["y_full"])

        @block.vector
        def _(dve):
            def aggregate(st, m, y, step, at):
                n = y.shape[1]
                v, w, a, q = (newton[:, k, 0:n] for k in range(4))
                dve.wait_ge(step, at)
                nc.vector.tensor_tensor(w, st[:, :, 1], st[:, :, 4], ALU.add)
                nc.vector.tensor_tensor(a, st[:, :, 1], st[:, :, 4], ALU.subtract)
                nc.vector.tensor_tensor(v, st[:, :, 2], st[:, :, 5], ALU.add).then_inc(step, 1)
                dve.wait_ge(step, at + 1)
                nc.vector.tensor_scalar(m, w, 0.5, None, ALU.mult)
                nc.vector.tensor_tensor(q, a, a, ALU.mult).then_inc(step, 1)
                dve.wait_ge(step, at + 2)
                nc.vector.scalar_tensor_tensor(out=a, in0=q, scalar=D / 4, in1=v, op0=ALU.mult,
                                               op1=ALU.add).then_inc(step, 1)
                dve.wait_ge(step, at + 3)
                at = at + 3
                nc.vector.tensor_scalar(v, a, 1.0 / D, EPS, ALU.mult, ALU.add).then_inc(step, 1)
                dve.wait_ge(step, at + 1)
                nc.vector.tensor_scalar(a.bitcast(I32), v.bitcast(I32), 1, None,
                                        ALU.logical_shift_right).then_inc(step, 1)
                dve.wait_ge(step, at + 2)
                nc.vector.tensor_scalar(y.bitcast(I32), a.bitcast(I32), -1.0, float(0x5f3759df), ALU.mult, ALU.add)
                nc.vector.tensor_scalar(w, v, -0.5, None, ALU.mult).then_inc(step, 1)
                for k in range(NEWTON):
                    dve.wait_ge(step, at + 3 + 3 * k)
                    nc.vector.tensor_tensor(a, y, w, ALU.mult).then_inc(step, 1)
                    dve.wait_ge(step, at + 4 + 3 * k)
                    nc.vector.tensor_tensor(a, a, y, ALU.mult).then_inc(step, 1)
                    dve.wait_ge(step, at + 5 + 3 * k)
                    nc.vector.scalar_tensor_tensor(out=y, in0=a, scalar=1.5, in1=y, op0=ALU.add,
                                                   op1=ALU.mult).then_inc(step, 1)
                dve.wait_ge(step, at + 3 + 3 * NEWTON)

            def norm_rows(ph, src, n, b):
                for i in range(QB):
                    last = nc.vector.bn_stats(stats[:, b, i, :], src[:, i, :])
                last.then_inc(ph["norm_step"][b], 1)
                aggregate(stats[:, b], mean[:, b, :], rstd[:, b, :], ph["norm_step"][b], n * NORM_STEPS + 1)
                for i in range(QB):
                    last = nc.vector.tensor_scalar(xh[:, b, i, :], src[:, i, :], mean[:, b, i:i + 1],
                                                   rstd[:, b, i:i + 1], ALU.subtract, ALU.mult)
                last.then_inc(ph["normed"][b], 1)

            def maxima(ph, c, b):
                for i in range(QB):
                    for d in range(DB):
                        u = i * DB + d
                        dve.wait_ge(ph["s_full"][b], c * QB * DB + u + 1)
                        last = nc.vector.tensor_reduce(negmax[:, b, i, d * HB:(d + 1) * HB],
                                                       bank(b, u % 2).rearrange("p (h k) -> p h k", k=LK),
                                                       AX.X, ALU.max, negate=True)
                        last.then_inc(ph["max_done"][b], 1)
                dve.wait_ge(ph["max_done"][b], (c + 1) * QB * DB)
                high, mid, low = (max_parts[:, b, :, k * PR:k * PR + H] for k in range(PARTS))
                nc.vector.tensor_copy(high, negmax[:, b]).then_inc(ph["split_step"][b], 1)
                dve.wait_ge(ph["split_step"][b], c * 3 + 1)
                nc.vector.tensor_tensor(max_rest[:, b], negmax[:, b], high, ALU.subtract).then_inc(ph["split_step"][b], 1)
                dve.wait_ge(ph["split_step"][b], c * 3 + 2)
                nc.vector.tensor_copy(mid, max_rest[:, b]).then_inc(ph["split_step"][b], 1)
                dve.wait_ge(ph["split_step"][b], c * 3 + 3)
                nc.vector.tensor_tensor(low, max_rest[:, b], mid, ALU.subtract).then_inc(ph["split_done"][b], 1)

            def normalise(ph, c, b):
                for d in range(DB):
                    dve.wait_ge(ph["pv_full"][b], c * DB + d + 1)
                    nc.vector.reciprocal(recip[:, b, :], bank(b, 3)).then_inc(ph["recip_step"][b], 1)
                    dve.wait_ge(ph["recip_step"][b], c * DB + d + 1)
                    nc.vector.tensor_tensor(outT[:, b, d, :], bank(b, 2), recip[:, b, :],
                                            ALU.mult).then_inc(ph["outT_ready"][b], 1)

            def add_rows(full, done, dst, n, b, k0):
                for k in range(2):
                    dve.wait_ge(full[b], n * 2 + k + 1)
                    nc.vector.tensor_tensor(dst(k), bank(b, k0 + k).rearrange("p (i n) -> p i n", i=2), dst(k),
                                            ALU.add).then_inc(done[b], 1)

            dve.wait_ge(ctx_in, 16)
            nc.vector.bn_stats(stats[:, 0, 0, :], ctx_tok).then_inc(ctx_step, 1)
            aggregate(stats[:, 0, 0:1], mean[:, 0, 0:1], rstd[:, 0, 0:1], ctx_step, 1)
            nc.vector.tensor_scalar(ctx_hat, ctx_tok, mean[:, 0, 0:1], rstd[:, 0, 0:1], ALU.subtract,
                                    ALU.mult).then_inc(ctx_hat_ready, 1)
            dve.wait_ge(silu_exp, 1)
            nc.vector.tensor_scalar(silu[:, 1], silu[:, 0], 1.0, None, ALU.add).then_inc(silu_step, 1)
            dve.wait_ge(silu_step, 1)
            nc.vector.reciprocal(silu[:, 0], silu[:, 1]).then_inc(silu_step, 1)
            dve.wait_ge(silu_step, 2)
            nc.vector.tensor_tensor(silu[:, 2], vec[:, 0:4], silu[:, 0], ALU.mult).then_inc(silu_ready, 1)
            dve.wait_ge(ss_full, 1)
            for n, (_, bias) in enumerate(ADA):
                cols = vec[:, VCOL[bias]:VCOL[bias] + 4].unsqueeze(2).to_broadcast([P, 4, NB])
                last = nc.vector.tensor_tensor(ss[:, n], ps[:, 1, n * 4 * NB:(n + 1) * 4 * NB].rearrange(
                    "p (o b) -> p o b", b=NB), cols, ALU.add)
            last.then_inc(ss_step, 1)
            dve.wait_ge(ss_step, 1)
            for n in (ADA_Q, ADA_KV):
                nc.vector.tensor_scalar(ada_a[:, n], ss[:, n, 0:DB, :], 1.0, None, ALU.add)
                nc.vector.tensor_copy(ada_b[:, n], ss[:, n, DB:2 * DB, :])
            for n, g, beta in ((ADA_1, "L1_xcond_ln1_g", "L1_xcond_ln1_b"), (ADA_2, "L1_xcond_ln2_g", "L1_xcond_ln2_b")):
                gain = vec[:, VCOL[g]:VCOL[g] + DB].unsqueeze(2).to_broadcast([P, DB, NB])
                shift = vec[:, VCOL[beta]:VCOL[beta] + DB].unsqueeze(2).to_broadcast([P, DB, NB])
                nc.vector.tensor_tensor(ada_a[:, n], ss[:, n, 0:DB, :], gain, ALU.mult)
                last = nc.vector.tensor_tensor(ada_b[:, n], ss[:, n, 0:DB, :], shift, ALU.mult)
            last.then_inc(ss_step, 1)
            dve.wait_ge(ss_step, 2)
            for n in (ADA_1, ADA_2):
                last = nc.vector.tensor_tensor(ada_b[:, n], ada_b[:, n], ss[:, n, DB:2 * DB, :], ALU.add)
            last.then_inc(ada_ready, 1)
            dve.wait_ge(ada_ready, 1)
            dve.wait_ge(ctxT_full, 1)
            for d in range(DB):
                for b in range(NB):
                    src = ps[:, 2, d * P + b * LK:d * P + (b + 1) * LK].unsqueeze(1).to_broadcast([P, 2, LK])
                    last = nc.vector.tensor_scalar(ctxT[:, 0, d, b], src, ada_a[:, ADA_KV, d, b:b + 1],
                                                   ada_b[:, ADA_KV, d, b:b + 1], ALU.mult, ALU.add)
            last.then_inc(ctxT_ready, 1)
            for d in range(DB):
                src = ps[:, 2, (DB + d) * P:(DB + d + 1) * P].rearrange("p (b k) -> p b k", b=NB)
                last = nc.vector.tensor_copy(ctxT[:, 1, d], src.unsqueeze(2).to_broadcast([P, NB, 2, LK]))
            last.then_inc(ctxT_ready, 1)
            dve.wait_ge(ctx_k_full, 1)
            for a, bias in enumerate(("L0_xcond_bkv", "L1_xcond_ca_kb")):
                for o in range(DB):
                    at = (a * DB + o) * NB * LK
                    last = nc.vector.tensor_scalar(ktx[:, a, o].rearrange("p b k -> p (b k)"),
                                                   ps[:, 3, at:at + NB * LK],
                                                   vec[:, VCOL[bias] + o:VCOL[bias] + o + 1], None, ALU.add)
            last.then_inc(ktx_ready, 1)
            dve.wait_ge(ktx_ready, 1)
            dve.wait_ge(consts_made, 1)
            dve.wait_ge(bc_in, 16 * len(BROAD))
            dve.wait_ge(ctx_v_full, 1)
            for a, name in enumerate(("L0_xcond_bv", "L1_xcond_ca_vb")):
                nc.vector.tensor_tensor(vtx[:, a], ps[:, 4 + a, :].rearrange("p (b n) -> p b n", b=NB),
                                        bc[:, BROAD.index(name)].unsqueeze(1).to_broadcast([P, NB, D]),
                                        ALU.add).then_inc(vtx_ready, 1)
            dve.wait_ge(vtx_ready, 2)
            for a, (kbd, vbd) in enumerate(((kbd_0, vbd_0), (kbd_ca, vbd_ca))):
                for b in range(NB):
                    for o in range(DB):
                        nc.vector.tensor_tensor(kbd[:, b, o, :].rearrange("p (h k) -> p h k", k=LK),
                                                ktx[:, a, o, b, :].unsqueeze(1).to_broadcast([P, HB, LK]),
                                                head_mask[:].unsqueeze(2).to_broadcast([P, HB, LK]), ALU.mult)
                    for e in range(2):
                        last = nc.vector.tensor_scalar(
                            vbd[:, b].rearrange("p n (e k) -> p n e k", e=2)[:, :, e, :],
                            vtx[:, a, b].rearrange("p (n e k) -> p n e k", e=2, k=DH)[:, :, e, :],
                            half_mask[:, e:e + 1], None, ALU.mult)
                last.then_inc(ctx_ready, 1)

            dve.wait_ge(x_in, 16 * NB)
            with dve.Fori(0, NC) as c:
                for b in range(NB):
                    dve.wait_ge(px["xT_full"][b], c * DB)
                    norm_rows(px, x_tok[:, ds(c * QB + b * TB, QB), :], c, b)
                for b in range(NB):
                    maxima(px, c, b)
                for b in range(NB):
                    normalise(px, c, b)
                for b in range(NB):
                    dve.wait_ge(px["biased"][b], c + 1)
                    add_rows(px["o_full"], px["added"],
                             lambda k: x_tok[:, ds(c * QB + b * TB + 2 * k, 2), :], c, b, 0)
            for b in range(NB):
                dve.wait_ge(px["added"][b], 2 * NC)

            dve.wait_ge(v_ones, 1)
            with dve.Fori(0, NC) as c:
                for b in range(NB):
                    dve.wait_ge(p2["xT_full"][b], c * DB)
                    norm_rows(p2, x_tok[:, ds(c * QB + b * TB, QB), :], c, b)
                for k in range(2):
                    for b in range(NB):
                        dve.wait_ge(p2["parts_out"][b], c * 16 * PARTS * 4)
                        for u in (2 * k, 2 * k + 1):
                            full = q_full[:, b, u, :]
                            high, mid, low = (parts[:, b * 4 + u, part, :] for part in range(PARTS))
                            dve.wait_ge(p2["qk_taken"][b], c * 4 + u + 1)
                            nc.vector.tensor_tensor(full, full, high, ALU.subtract).then_inc(p2["split_step"][b], 1)
                            dve.wait_ge(p2["split_step"][b], c * 8 + 2 * u + 1)
                            nc.vector.tensor_copy(mid, full).then_inc(p2["split_step"][b], 1)
                            dve.wait_ge(p2["split_step"][b], c * 8 + 2 * u + 2)
                            nc.vector.tensor_tensor(low, full, mid, ALU.subtract).then_inc(p2["parts_ready"][b], 1)
                for b in range(NB):
                    for k in range(2):
                        dve.wait_ge(p2["v_full"][b], c * 2 + k + 1)
                        bias = bc[:, BROAD.index("L1_xcond_sa_vb")].rearrange("p (h n) -> p h n", n=DH)
                        for i in range(2):
                            last = nc.vector.tensor_tensor(
                                v_all[:, ds(c * QB + b * TB + 2 * k + i, 1), :, 0:DH].rearrange("p o h n -> p (o h) n"),
                                bank(b, 2 + k)[:, i * D:(i + 1) * D].rearrange("p (h n) -> p h n", n=DH),
                                bias, ALU.add)
                        last.then_inc(p2["v_ready"][b], 1)

            def group_maxima(a):
                for n in range(QT):
                    dve.wait_ge(sa_s_full, a * QT + n + 1)
                    at = 4 + 2 * (n % 2)
                    nc.vector.tensor_reduce(negmax_g[:, n:n + 1], ps[:, at:at + 2, :].rearrange("p a n -> p (a n)"),
                                            AX.X, ALU.max, negate=True).then_inc(sa_max_done, 1)
                dve.wait_ge(sa_max_done, (a + 1) * QT)
                high, mid, low = (max_parts_g[:, k, :] for k in range(PARTS))
                nc.vector.tensor_copy(high, negmax_g[:]).then_inc(sa_split_step, 1)
                dve.wait_ge(sa_split_step, a * 3 + 1)
                nc.vector.tensor_tensor(max_rest_g[:], negmax_g[:], high, ALU.subtract).then_inc(sa_split_step, 1)
                dve.wait_ge(sa_split_step, a * 3 + 2)
                nc.vector.tensor_copy(mid, max_rest_g[:]).then_inc(sa_split_step, 1)
                dve.wait_ge(sa_split_step, a * 3 + 3)
                nc.vector.tensor_tensor(low, max_rest_g[:], mid, ALU.subtract).then_inc(sa_split_done, 1)
                dve.wait_ge(sa_maxT_full, a + 1)
                for b in range(NB):
                    dve.wait_ge(shift_in[b], shifts_before(a, b))
                nc.vector.tensor_copy(maxT_g[:], ps[0:PARTS * QT, 4, 0:P // 2].bitcast(BF16)).then_inc(sa_maxT_ready, 1)

            at_half = {}

            def shifts_before(a, b):
                g, nb = at_half["g"], at_half["b"]
                return (g + (1 if b < nb else 0)) * 16 * PARTS

            def take_sums_last(g, b):
                half = g * NB + b
                dve.wait_ge(sa_pv_done, (half + 1) * STEPS)
                dve.wait_ge(sums_out[1], half * 16)
                nc.vector.tensor_copy(sums[:, 1], ps[:, 3, :]).then_inc(sums_taken[1], 1)

            at_half.update(g=0, b=0)
            group_maxima(0)
            with dve.Fori(0, NG - 1) as g:
                for b in range(NB):
                    at_half.update(g=(g if b == 0 else g + 1), b=1 - b)
                    group_maxima(g * NB + b + 1)
                    take_sums_last(g, b)
            at_half.update(g=NG - 1, b=1)
            group_maxima(HALVES - 1)
            take_sums_last(NG - 1, 0)
            take_sums_last(NG - 1, 1)

            with dve.Fori(0, NC) as c:
                n = c + NC
                for b in range(NB):
                    dve.wait_ge(p4["att_in"][b], (c + 1) * 16 * 2 * H)
                    for d in range(DB):
                        nc.vector.reciprocal(denT[:, b, d, :], denT[:, b, d, :]).then_inc(p4["att_recip"][b], 1)
                    for d in range(DB):
                        dve.wait_ge(p4["att_recip"][b], c * DB + d + 1)
                        nc.vector.tensor_tensor(outT[:, b, d, :], attT[:, b, d, :], denT[:, b, d, :],
                                                ALU.mult).then_inc(p4["attT_ready"][b], 1)
                for b in range(NB):
                    dve.wait_ge(p4["x1_in"][b], c + 1)
                    add_rows(p4["so_full"], p4["x2_ready"], lambda k: xc[:, b, 2 * k:2 * k + 2, :], c, b, 2)
                for b in range(NB):
                    maxima(px, n, b)
                for b in range(NB):
                    normalise(px, n, b)
                for b in range(NB):
                    dve.wait_ge(px["biased"][b], n + 1)
                    add_rows(px["o_full"], px["added"], lambda k: xc[:, b, 2 * k:2 * k + 2, :], n, b, 0)
                    dve.wait_ge(px["added"][b], (n + 1) * 2)
                    norm_rows(px, xc[:, b], n, b)
                for b in range(NB):
                    dve.wait_ge(p4["b2_added"][b], c + 1)
                    add_rows(p4["y_full"], p4["y_ready"], lambda k: xc[:, b, 2 * k:2 * k + 2, :], c, b, 2)

        @block.scalar
        def _(act):
            def turned_rows(full, done, n, b, k0, ada):
                for d in range(DB):
                    act.wait_ge(full[b], n * DB + d + 1)
                    if ada is None:
                        nc.scalar.activation(xT[:, b, d, :], bank(b, k0 + d), ACT.Copy).then_inc(done[b], 1)
                    else:
                        nc.scalar.activation(xT[:, b, d, :], bank(b, k0 + d), ACT.Identity,
                                             scale=ada_a[:, ada, d, b:b + 1],
                                             bias=ada_b[:, ada, d, b:b + 1]).then_inc(done[b], 1)

            def queries(ph, c, b, name):
                for d in range(DB):
                    act.wait_ge(ph["q_full"][b], c * DB + d + 1)
                    nc.scalar.activation(qT[:, b, d, :], bank(b, 2 + d), ACT.Identity,
                                         bias=vec[:, VCOL[name] + d:VCOL[name] + d + 1]).then_inc(ph["q_ready"][b], 1)

            def exponentials(ph, c, b):
                act.wait_ge(ph["maxT_full"][b], c + 1)
                nc.scalar.activation(maxT[:, b, :], bank(b, 2)[0:PARTS * PR, 0:CH // 2].bitcast(BF16),
                                     ACT.Copy).then_inc(ph["maxT_ready"][b], 1)
                act.wait_ge(ph["pv_full"][1 - b], (c + b) * DB)
                for p in range(NP):
                    act.wait_ge(ph["st_full"][b], c * NP + p + 1)
                    nc.scalar.activation(probs[:, p, :], bank(b, p % 2), ACT.Exp,
                                         scale=SCALE).then_inc(ph["exp_done"][b], 1)

            act.wait_ge(vec_full, 1)
            nc.scalar.activation(vec[:], ps[:, 0, 0:NVEC], ACT.Copy).then_inc(vec_ready, 1)
            act.wait_ge(vec_ready, 1)
            nc.scalar.activation(silu[:, 0], vec[:, 0:4], ACT.Exp, scale=-1.0).then_inc(silu_exp, 1)

            act.wait_ge(ada_ready, 1)
            act.wait_ge(ctx_ready, 2)
            with act.Fori(0, NC) as c:
                for b in range(NB):
                    turned_rows(px["xT_full"], px["xT_ready"], c, b, 0, ADA_Q)
                for b in range(NB):
                    queries(px, c, b, "L0_xcond_bq")
                for b in range(NB):
                    exponentials(px, c, b)

            for b in range(NB):
                act.wait_ge(px["pv_full"][b], NC * DB)
                act.wait_ge(px["o_full"][b], NC * 2)
            with act.Fori(0, NC) as c:
                for b in range(NB):
                    turned_rows(p2["xT_full"], p2["xT_ready"], c, b, 0, ADA_1)
                for k, name in enumerate(("L1_xcond_sa_qb", "L1_xcond_sa_kb")):
                    for b in range(NB):
                        act.wait_ge(p2["parts_ready"][b], c * 4)
                        act.wait_ge(p2["parts_out"][b], c * 16 * PARTS * 4)
                        for d in range(DB):
                            u = k * DB + d
                            src = bank(b, 2 - 2 * k + d)
                            bias = vec[:, VCOL[name] + d:VCOL[name] + d + 1]
                            act.wait_ge(p2["qk_full"][b], c * 4 + u + 1)
                            nc.scalar.activation(q_full[:, b, u, :], src, ACT.Identity, bias=bias)
                            nc.scalar.activation(parts[:, b * 4 + u, 0, :], src, ACT.Identity,
                                                 bias=bias).then_inc(p2["qk_taken"][b], 1)

            for b in range(NB):
                act.wait_ge(p2["parts_ready"][b], 4 * NC)

            def group_exponentials(g, b):
                half = g * NB + b
                for s in range(STEPS):
                    act.wait_ge(sa_pv_done, half * STEPS + max(s - 1, 0))
                    for j in range(HG):
                        u = s * HG + j
                        act.wait_ge(sa_st_full, half * STEPS * HG + u + 1)
                        nc.scalar.activation(probs[:, (s % 2) * HG + j, :], ps[:, u % 3, :], ACT.Exp,
                                             scale=SCALE).then_inc(sa_exp_done, 1)
                    if s == TB:
                        act.wait_ge(sa_pv_done, half * STEPS + TB)
                        act.wait_ge(sums_out[0], half * 16)
                        nc.scalar.activation(sums[:, 0], ps[:, 3, :], ACT.Copy).then_inc(sums_taken[0], 1)

            with act.Fori(0, NG - 1) as g:
                for b in range(NB):
                    group_exponentials(g, b)
            for b in range(NB):
                group_exponentials(NG - 1, b)

            act.wait_ge(sa_pv_done, HALVES * STEPS)
            with act.Fori(0, NC) as c:
                n = c + NC
                for b in range(NB):
                    turned_rows(px["xT_full"], px["xT_ready"], n, b, 0, None)
                for b in range(NB):
                    queries(px, n, b, "L1_xcond_ca_qb")
                for b in range(NB):
                    exponentials(px, n, b)
                for b in range(NB):
                    turned_rows(p4["hT_full"], p4["hT_ready"], c, b, 2, ADA_2)
                for b in range(NB):
                    act.wait_ge(p4["y_full"][b], c * 2)
                    for f in range(FB):
                        act.wait_ge(p4["hid_full"][b], c * FB + f + 1)
                        at = VCOL["L1_xcond_ffn_b1"] + f
                        nc.scalar.activation(hidT[:, b, f, :], bank(b, f % 2), ACT.Gelu,
                                             bias=vec[:, at:at + 1]).then_inc(p4["hid_ready"][b], 1)


def dma_runs(terms):
    return 1 + sum(b != a + 1 for a, b in zip(terms, terms[1:]))


LOADS = dma_runs(Q_TERMS) + dma_runs(K_TERMS)

_INS = ["x", "ctx_1024", "cond_1024"] + ["L0_xcond_" + n for n in (
    "Wq", "bq", "Wkv", "bkv", "Wp", "bp", "Wss_q", "bss_q", "Wss_kv", "bss_kv")] + ["L1_xcond_" + n for n in (
        "ln1_g", "ln1_b", "aff1_w", "aff1_b", "ln2_g", "ln2_b", "aff2_w", "aff2_b", "sa_qw", "sa_qb", "sa_kw",
        "sa_kb", "sa_vw", "sa_vb", "sa_ow", "sa_ob", "ca_qw", "ca_qb", "ca_kw", "ca_kb", "ca_vw", "ca_vb",
        "ca_ow", "ca_ob", "ffn_w1", "ffn_b1", "ffn_w2", "ffn_b2")]


def kernel(**inputs):
    import numpy as _np
    import concourse.bacc as _bacc
    from concourse import mybir as _mybir
    from concourse.bass_utils import run_bass_kernel_spmd as _run

    nc = _bacc.Bacc("TRN2", target_bir_lowering=False, num_devices=1)
    arrays, tensors = {}, {}
    for name in _INS:
        a = _np.ascontiguousarray(inputs[name])
        arrays[f"in_{name}_dram"] = a
        tensors[name] = nc.dram_tensor(f"in_{name}_dram", a.shape, _mybir.dt.from_np(a.dtype),
                                       kind="ExternalInput").ap()
    out = nc.dram_tensor("out_0_dram", (NB, L, D), _mybir.dt.from_np(_np.dtype("float32")), kind="ExternalOutput").ap()
    build(nc, tensors, out)
    r = _run(nc, [arrays], core_ids=[0])
    return r.results[0]["out_0_dram"]
```

```python
from contextlib import ExitStack

import concourse.bass as bass
from concourse import mybir

ALU = mybir.AluOpType
ACT = mybir.ActivationFunctionType
AX = mybir.AxisListType
F32 = mybir.dt.float32
BF16 = mybir.dt.bfloat16
F32R = mybir.dt.float32r
I32 = mybir.dt.int32
ds = bass.ds

P = 128
NB = 2
L = 1024
D = 256
H = 16
DH = D // H
LK = 64
FF = 1024
EPS = 1e-5
NEWTON = 3
NORM_STEPS = 7 + 3 * NEWTON
SCALE = 1.0 / DH ** 0.5

DB = D // P
CH = 512
NC = L // CH
QB = CH // P
TB = L // P
HB = H // DB
NP = H // 2
PB = NP // DB
FB = FF // P

HG = 4
NG = H // HG
QT = HG * TB
STEPS = NC * TB
A_STEPS = STEPS - 2
PARTS = 3
PR = 32
Q_RUNS = ((0, 0, 0), (1, 1), (2,))
K_RUNS = ((0, 1, 2), (0, 1), (0,))
LOADS = len(Q_RUNS) + len(K_RUNS)
ROWS = sum(len(r) for r in Q_RUNS) * DH
ROWS_M = ROWS + PARTS

VECS = (("cond_1024", 4), ("L0_xcond_bq", 2), ("L0_xcond_bkv", 4), ("L0_xcond_bss_q", 4), ("L0_xcond_bss_kv", 4),
        ("L1_xcond_aff1_b", 4), ("L1_xcond_aff2_b", 4), ("L1_xcond_ln1_g", 2), ("L1_xcond_ln1_b", 2),
        ("L1_xcond_ln2_g", 2), ("L1_xcond_ln2_b", 2), ("L1_xcond_sa_qb", 2), ("L1_xcond_sa_kb", 2),
        ("L1_xcond_ca_qb", 2), ("L1_xcond_ca_kb", 2), ("L1_xcond_ffn_b1", 8))
VCOL = {}
for _name, _rows in VECS:
    VCOL[_name] = sum(r for n, r in VECS[:len(VCOL)])
NVEC = sum(r for _, r in VECS)
N_VECS0 = 5
NVEC0 = sum(r for _, r in VECS[:N_VECS0])
BROAD = ("L0_xcond_bv", "L0_xcond_bp", "L1_xcond_sa_vb", "L1_xcond_sa_ob", "L1_xcond_ca_vb", "L1_xcond_ca_ob",
         "L1_xcond_ffn_b2")
ADA = (("L0_xcond_Wss_q", "L0_xcond_bss_q"), ("L0_xcond_Wss_kv", "L0_xcond_bss_kv"),
       ("L1_xcond_aff1_w", "L1_xcond_aff1_b"), ("L1_xcond_aff2_w", "L1_xcond_aff2_b"))
ADA_Q, ADA_KV, ADA_1, ADA_2 = range(4)


def build(nc, t, out):
    with ExitStack() as ctx:
        def sb(name, shape, dt=F32):
            return ctx.enter_context(nc.sbuf_tensor(name, shape, dt))

        def sem(name):
            return ctx.enter_context(nc.semaphore(name))

        def sems(name, n=NB):
            return [sem(f"{name}_{k}") for k in range(n)]

        q_parts = nc.dram_tensor("q_parts", [H, DH, PARTS, NB * L], BF16, kind="Internal").ap()
        k_parts = nc.dram_tensor("k_parts", [H, DH, PARTS, NB * L], BF16, kind="Internal").ap()
        att_sums = nc.dram_tensor("att_sums", [H, 2, DH, NB * L], F32, kind="Internal").ap()

        region_words = 30720
        region_at = -(-nc.sbuf_base // 32) * 32
        sb("region", [P, region_words + 8])

        def at(name, word, shape, dt=F32):
            return nc.alloc_sbuf_tensor_at(name, [P] + list(shape), dt, offset=region_at + 4 * word)

        xT = at("xT", 0, [2, NB, DB, CH], F32R)
        qT = at("qT", 4096, [2, NB, DB, CH], F32R)
        outT = at("outT", 8192, [2, NB, DB, CH], F32R)
        hidT = at("hidT", 4096, [FB, 2, CH], F32R)
        parts = at("parts", 4096, [NB * 4, PARTS, CH], BF16)
        w_kv0 = at("w_kv0", 4096, [DB, 2 * D])
        w_raw = at("w_raw", 8192, [8, DB, D])
        qa = at("qa", 0, [HG, L], BF16)
        ka = at("ka", 2048, [HG, L], BF16)
        qs = [at(f"qs{b}", 4096 + 2048 * b, [HG, L], BF16) for b in range(NB)]
        ks = [at(f"ks{b}", 8192 + 2048 * b, [HG, L], BF16) for b in range(NB)]
        kbd = at("kbd", 12288, [2, NB, DB, HB * LK], F32R)
        v_all = at("v_all", 12288, [NB * TB, H, DH])
        w_q0 = at("w_q0", 16384, [2, DB, D], F32R)
        w_p0 = at("w_p0", 17408, [2, DB, D], F32R)
        v_grp = at("v_grp", 16384, [NB, TB, HG, 2 * DH])
        xc = at("xc", 16384, [NB, QB, D])
        attT = at("attT", 18432, [NB, DB, CH])
        denT = at("denT", 20480, [NB, DB, CH])
        w_sa = at("w_sa", 22528, [3, 2, DB, D], F32R)
        w_ada = at("w_ada", 25600, [4, DB, 2 * D])
        w_kv1 = at("w_kv1", 29696, [2, DB, D])
        w_1 = at("w_1", 22528, [2, DB, FF], F32R)
        w_2 = at("w_2", 26624, [2, FB, D], F32R)

        x_tok = sb("x_tok", [P, NB * TB, D])
        xh = sb("xh", [P, NB, QB, D])
        probs = sb("probs", [P, 2 * HG, CH])
        vbd = sb("vbd", [P, 2, NB, NP, 2 * DH])
        w_out = sb("w_out", [P, 3, 2, DB, D], F32R)
        tmp = sb("tmp", [P, 4, CH])
        bc = sb("bc", [P, len(BROAD), D])
        vrow = sb("vrow", [NVEC0, P])
        vrow1 = sb("vrow1", [NVEC - NVEC0, P])
        vec = sb("vec", [P, NVEC])
        silu = sb("silu", [P, 3, 4])
        ss = sb("ss", [P, 4, 4, NB])
        ada_a = sb("ada_a", [P, 4, DB, NB])
        ada_b = sb("ada_b", [P, 4, DB, NB])
        ident = sb("ident", [P, P])
        ident_h = sb("ident_h", [P, P], BF16)
        head_mask = sb("head_mask", [P, HB])
        half_mask = sb("half_mask", [P, 2])
        ones_bd = sb("ones_bd", [P, 2, DH])
        pick = sb("pick", [PARTS * PR, NP, 2, LK], BF16)
        ktx = sb("ktx", [P, 2, DB, NB, LK])
        stats = sb("stats", [P, NB, QB, 6])
        mean = sb("mean", [P, NB, QB])
        rstd = sb("rstd", [P, NB, QB])
        newton = sb("newton", [P, 4, QB])
        negmax = sb("negmax", [P, NB, QB, H])
        max_rest = sb("max_rest", [P, NB, QB, H])
        max_parts = sb("max_parts", [P, NB, QB, PARTS * PR], BF16)
        maxT = sb("maxT", [PARTS * PR, NB, CH], BF16)
        negmax_g = sb("negmax_g", [P, QT])
        max_rest_g = sb("max_rest_g", [P, QT])
        max_parts_g = sb("max_parts_g", [P, PARTS, QT], BF16)
        maxT_g = sb("maxT_g", [PARTS * QT, P], BF16)
        sums = sb("sums", [P, NC, CH])

        def view(area, at, *shape):
            n = 1
            for k in shape:
                n *= k
            names = "abcde"[:len(shape)]
            sizes = dict(zip(names, shape))
            return area[:, at:at + n].rearrange(f"p ({' '.join(names)}) -> p {' '.join(names)}", **sizes)

        xf = view(xh[:].rearrange("p b i n -> p (b i n)"), 0, NB, DB, CH)
        xh_words = xh[:].rearrange("p b i n -> p (b i n)")
        w_1raw = view(xh_words, 0, DB, FF)
        w_2raw = view(xh_words, 0, FB, D)
        p_area = probs[:].rearrange("p a n -> p (a n)")
        ctx_tok = view(p_area, 0, D)
        ctx_hat = view(p_area, D, D)
        vtx = view(p_area, 8 * D, 2, NB, D)
        q_full = view(p_area, 0, NB, 4, CH)
        ctxT = view(sums[:].rearrange("p a n -> p (a n)"), 0, 2, DB, NB, 2, LK)

        ps = ctx.enter_context(nc.psum_tensor("ps", [P, 8, CH], F32))

        def bank(b, k):
            return ps[:, 4 * b + k, :]

        vec_in, x_in = sems("vec_in", 2), sem("x_in")
        ctx_in, bc_in = sem("ctx_in"), sem("bc_in")
        w_ada_in, w_kv_in = sems("w_ada_in", 2), sems("w_kv_in", 2)
        w_0_in, w_sa_in, w_mlp_in = sem("w_0_in"), sem("w_sa_in"), sem("w_mlp_in")
        w_0_split, w_split = sem("w_0_split"), sem("w_split")
        consts_made, mask_step = sem("consts_made"), sem("mask_step")
        vec_full, vec_ready, silu_step, silu_exp, silu_ready = (
            sem("vec_full"), sem("vec_ready"), sem("silu_step"), sem("silu_exp"), sem("silu_ready"))
        ss_full, ss_step, ada_ready = sem("ss_full"), sem("ss_step"), sem("ada_ready")
        ctx_step, ctx_hat_ready, ctxT_full, ctxT_ready = (
            sem("ctx_step"), sem("ctx_hat_ready"), sem("ctxT_full"), sem("ctxT_ready"))
        ctx_k_full, ctx_v_full, ktx_ready, ktx_step, vtx_ready, vbd_ready, kbd_ready = (
            sem("ctx_k_full"), sem("ctx_v_full"), sem("ktx_ready"), sem("ktx_step"), sem("vtx_ready"),
            sem("vbd_ready"), sem("kbd_ready"))

        def phase(name, per_batch, common=()):
            return {w: sems(f"{name}_{w}") for w in per_batch} | {w: sem(f"{name}_{w}") for w in common}

        px = phase("x", ("xT_full", "xT_high", "xT_low", "q_full", "q_high", "q_low", "s_full", "max_done",
                         "maxT_full", "maxT_ready", "st_full", "exp_done", "pv_full", "recip_done", "outT_ready",
                         "o_full", "biased", "added", "normed"),
                   ("norm_step", "split_step", "log_done", "out_step"))
        p2 = phase("qkv", ("normed", "xT_full", "xT_high", "xT_low", "qk_full", "qk_taken", "mid_ready",
                           "parts_ready", "parts_out", "v_full", "v_ready"), ("norm_step", "split_step"))
        p4 = phase("l1", ("att_in", "recip_done", "outT_ready", "so_full", "x1_in", "x2_ready", "hT_full",
                          "hT_high", "hT_low", "hid_full", "hid_high", "hid_low", "y_full", "b2_added", "y_ready",
                          "y_out"), ("log_done", "out_step"))

        stack_a = sems("stack_a", HG)
        stack_s, shift_in, v_grp_ready = sems("stack_s"), sems("shift_in"), sem("v_grp_ready")
        sa_s_full, sa_max_done, sa_split_step, sa_maxT_full, sa_maxT_ready = (
            sem("sa_s_full"), sem("sa_max_done"), sem("sa_split_step"), sem("sa_maxT_full"), sem("sa_maxT_ready"))
        sa_st_full, sa_exp_done, sa_pv_done = sem("sa_st_full"), sem("sa_exp_done"), sem("sa_pv_done")
        sums_taken, sums_out = sems("sums_taken", NC), sems("sums_out", NC)
        ones_rows = sem("ones_rows")

        HALVES = NG * NB
        PARTS_OUT = 16 * 4 * NC

        def tile_plan(s):
            upto = [min(QT, -(-QT * k // A_STEPS)) for k in (s, s + 1)]
            return list(range(*upto))

        block = ctx.enter_context(nc.Block())

        @block.sync
        def _(sp):
            def load_vectors(names, tile, first, done):
                for name, rows in names:
                    src = t[name]
                    src = (src.rearrange("b (k p) -> (b k) p", p=P) if name == "cond_1024"
                           else src.rearrange("(k p) -> k p", p=P))
                    r = VCOL[name] - first
                    sp.dma_start(tile[r:r + rows, :], src).then_inc(done, 16)

            def load_weight(dst, name, done):
                sp.dma_start(dst, t[name].rearrange("(k p) n -> p k n", p=P)).then_inc(done, 16)

            x_dram = t["x"].rearrange("b (n p) d -> p (b n) d", p=P)

            def load_x(c):
                for b in range(NB):
                    rows = slice(b * TB + c * QB, b * TB + (c + 1) * QB)
                    sp.dma_start(x_tok[:, rows], x_dram[:, rows]).then_inc(x_in, 16)

            sp.dma_start(ctx_tok, t["ctx_1024"].rearrange("b k d -> (b k) d")).then_inc(ctx_in, 16)
            load_vectors(VECS[:N_VECS0], vrow, 0, vec_in[0])
            for n in (ADA_Q, ADA_KV):
                load_weight(w_ada[:, n], ADA[n][0], w_ada_in[0])
            load_weight(w_kv0[:], "L0_xcond_Wkv", w_kv_in[0])
            load_x(0)
            load_weight(w_raw[:, 0], "L0_xcond_Wq", w_0_in)
            load_weight(w_raw[:, 1], "L0_xcond_Wp", w_0_in)
            for k, name in enumerate(("sa_qw", "sa_kw", "sa_vw", "sa_ow", "ca_qw", "ca_ow")):
                load_weight(w_raw[:, 2 + k], "L1_xcond_" + name, w_sa_in)
            load_x(1)
            load_vectors(VECS[N_VECS0:], vrow1, NVEC0, vec_in[1])
            for n in (ADA_1, ADA_2):
                load_weight(w_ada[:, n], ADA[n][0], w_ada_in[1])
            load_weight(w_kv1[:, 0], "L1_xcond_ca_kw", w_kv_in[1])
            load_weight(w_kv1[:, 1], "L1_xcond_ca_vw", w_kv_in[1])

            with sp.Fori(0, NC) as c:
                for k in range(2):
                    for b in range(NB):
                        for d in range(DB):
                            u = k * DB + d
                            sp.wait_ge(p2["parts_ready"][b], c * 4 + u + 1)
                            to = (q_parts, k_parts)[k][d * HB:(d + 1) * HB, :, :, ds(c * CH + b * L, CH)]
                            sp.dma_start(to.rearrange("h d t n -> (h d) t n"),
                                         parts[:, b * 4 + u]).then_inc(p2["parts_out"][b], 16)

            def load_rows(dst, src, head, runs, b, done):
                row = 0
                for run in runs:
                    n = len(run)
                    if n > 1 and run[0] == run[1]:
                        rows = src[ds(head, 1), :, run[0], b * L:(b + 1) * L].rearrange("o d n -> (o d) n")
                        rows = rows.unsqueeze(1).to_broadcast([DH, n, L])
                    else:
                        rows = src[ds(head, 1), :, run[0]:run[0] + n, b * L:(b + 1) * L].rearrange(
                            "o d t n -> (o d) t n")
                    sp.dma_start(dst[row:row + n * DH, :], rows).then_inc(done, 16)
                    row += n * DH

            def load_stack_a(g, b, j):
                load_rows(qa[:, j, :], q_parts, g * HG + j, Q_RUNS, b, stack_a[j])
                load_rows(ka[:, j, :], k_parts, g * HG + j, K_RUNS, b, stack_a[j])

            def copy_stack(n, b):
                for j in range(HG):
                    sp.wait_ge(stack_a[j], (n + 1) * 16 * LOADS)
                sp.dma_start(qs[b][0:ROWS], qa[0:ROWS]).then_inc(stack_s[b], 16)
                sp.dma_start(ks[b][0:ROWS], ka[0:ROWS]).then_inc(stack_s[b], 16)

            def load_shift(a, b):
                sp.wait_ge(sa_maxT_ready, a + 1)
                for part in range(PARTS):
                    row = qs[b][ROWS + part:ROWS + part + 1].rearrange("o j (q n) -> o (j q) n", n=P)
                    sp.dma_start(row, maxT_g[part * QT:(part + 1) * QT, :]).then_inc(shift_in[b], 16)

            for b in range(NB):
                sp.wait_ge(p2["parts_out"][b], PARTS_OUT)
                sp.wait_ge(p2["v_full"][b], 2 * NC)
            for j in range(HG):
                load_stack_a(0, 0, j)
            copy_stack(0, 0)
            sp.wait_ge(stack_s[0], 16 * 2)
            for j in range(HG):
                sp.wait_ge(sa_s_full, TB * (j + 1))
                load_stack_a(0, 1, j)
            load_shift(0, 0)
            copy_stack(1, 1)
            with sp.Fori(0, NG - 1) as g:
                for b in range(NB):
                    half = g * NB + b
                    sp.wait_ge(stack_s[1 - b], (g + 1 + b) * 16 * 2)
                    for j in range(HG):
                        sp.wait_ge(sa_s_full, (half + 1) * QT + TB * (j + 1))
                        load_stack_a(g + 1, b, j)
                    load_shift(half + 1, 1 - b)
                    sp.wait_ge(sa_st_full, (half + 1) * STEPS * HG)
                    copy_stack(half + 2, b)
            load_shift(HALVES - 1, NB - 1)

            for ch in range(NC):
                sp.wait_ge(sums_out[ch], 16 * HALVES)
            out_tok = out.rearrange("b (n p) d -> p (b n) d", p=P)
            with sp.Fori(0, NC) as c:
                for b in range(NB):
                    sp.wait_ge(p4["outT_ready"][b], c * DB)
                    for d in range(DB):
                        for k, dst in enumerate((attT, denT)):
                            rows = att_sums[d * HB:(d + 1) * HB, k, :, ds(c * CH + b * L, CH)]
                            sp.dma_start(dst[:, b, d, :], rows).then_inc(p4["att_in"][b], 16)
                for b in range(NB):
                    sp.wait_ge(p4["y_ready"][b], (c + 1) * 2)
                    sp.dma_start(out_tok[:, ds(c * QB + b * TB, QB), :], xc[:, b]).then_inc(p4["y_out"][b], 16)
            for b in range(NB):
                sp.wait_ge(p4["y_out"][b], 16 * NC)

        @block.gpsimd
        def _(pool):
            names = {"L0_xcond_bv": t["L0_xcond_bkv"][D:2 * D]}
            for k, name in enumerate(BROAD):
                src = names.get(name, None)
                src = t[name] if src is None else src
                pool.dma_start(bc[:, k], src.partition_broadcast(P)).then_inc(bc_in, 16)
            nc.gpsimd.memset(max_parts[:], 0.0)
            nc.gpsimd.memset(ident[:], 0.0)
            nc.gpsimd.memset(head_mask[:], 1.0)
            nc.gpsimd.memset(half_mask[:], 1.0)
            nc.gpsimd.memset(ones_bd[:], 1.0)
            nc.gpsimd.memset(pick[:], 0.0).then_inc(mask_step, 1)
            pool.wait_ge(mask_step, 1)
            nc.gpsimd.affine_select(out=ident[:], in_=ident[:], compare_op=ALU.not_equal, fill=1.0, base=0,
                                    pattern=[[-1, P]], channel_multiplier=1)
            for tile, pat, width in ((head_mask, [[-DH, HB]], DH), (half_mask, [[-LK, 2]], LK),
                                     (ones_bd, [[-LK, 2], [0, DH]], LK)):
                nc.gpsimd.affine_select(out=tile[:], in_=tile[:], compare_op=ALU.is_ge, fill=0.0, base=0,
                                        pattern=pat, channel_multiplier=1)
            for part in range(PARTS):
                last = nc.gpsimd.affine_select(out=pick[:], in_=pick[:], compare_op=ALU.not_equal, fill=1.0,
                                               base=-part * PR, pattern=[[-2, NP], [-1, 2], [0, LK]],
                                               channel_multiplier=1)
                if part < PARTS - 1:
                    last.then_inc(mask_step, 1)
                    pool.wait_ge(mask_step, part + 2)
            last.then_inc(mask_step, 1)
            pool.wait_ge(mask_step, PARTS + 1)
            for tile, pat, width in ((head_mask, [[DH, HB]], DH), (half_mask, [[LK, 2]], LK),
                                     (ones_bd, [[LK, 2], [0, DH]], LK)):
                nc.gpsimd.affine_select(out=tile[:], in_=tile[:], compare_op=ALU.is_ge, fill=0.0, base=width - 1,
                                        pattern=pat, channel_multiplier=-1)
            nc.gpsimd.tensor_copy(ident_h[:], ident[:]).then_inc(consts_made, 1)

            def split(high, low, full, n):
                nc.gpsimd.tensor_copy(high, full).then_inc(w_split, 1)
                pool.wait_ge(w_split, 2 * n + 1)
                nc.gpsimd.tensor_tensor(low, full, high.bitcast(F32), ALU.subtract).then_inc(w_split, 1)

            pool.wait_ge(w_sa_in, 16 * 6)
            for k in range(6):
                dst = w_sa[:, k] if k < 3 else w_out[:, k - 3]
                split(dst[:, 0], dst[:, 1], w_raw[:, 2 + k], k)

            def low_rows(ph, high, low, n, b):
                for d in range(DB):
                    pool.wait_ge(ph[high][b], (n + 1) * 2 * DB - DB + d + 1)
                    nc.gpsimd.tensor_tensor(xT[:, 1, b, d, :], xf[:, b, d, :], xT[:, 0, b, d, :].bitcast(F32),
                                            ALU.subtract).then_inc(ph[low][b], 1)

            pool.wait_ge(bc_in, 16 * len(BROAD))
            with pool.Fori(0, NC) as c:
                for b in range(NB):
                    low_rows(px, "xT_high", "xT_low", c, b)
                for b in range(NB):
                    pool.wait_ge(px["normed"][b], c + 1)
                    rows = x_tok[:, ds(c * QB + b * TB, QB), :]
                    bias = bc[:, BROAD.index("L0_xcond_bp")].unsqueeze(1).to_broadcast([P, QB, D])
                    nc.gpsimd.tensor_tensor(rows, rows, bias, ALU.add).then_inc(px["biased"][b], 1)

            with pool.Fori(0, NC) as c:
                for b in range(NB):
                    low_rows(p2, "xT_high", "xT_low", c, b)
                for k in range(2):
                    for b in range(NB):
                        for u in (2 * k, 2 * k + 1):
                            pool.wait_ge(p2["mid_ready"][b], c * 4 + u + 1)
                            nc.gpsimd.tensor_tensor(parts[:, b * 4 + u, 2, :], q_full[:, b, u, :],
                                                    parts[:, b * 4 + u, 1, :],
                                                    ALU.subtract).then_inc(p2["parts_ready"][b], 1)

            for b in range(NB):
                pool.wait_ge(p2["parts_ready"][b], 4 * NC)
            for b in range(NB):
                pool.wait_ge(p2["parts_out"][b], PARTS_OUT)
            for b in range(NB):
                nc.gpsimd.memset(ks[b][ROWS:ROWS_M], 1.0).then_inc(ones_rows, 1)
            pool.wait_ge(ones_rows, NB)
            nc.gpsimd.memset(v_grp[:, :, :, :, DH:2 * DH], 1.0).then_inc(ones_rows, 1)

            def take_values(g, b):
                src = v_all[:, b * TB:(b + 1) * TB, ds(g * HG, HG), :]
                nc.gpsimd.tensor_copy(v_grp[:, b, :, :, 0:DH], src).then_inc(v_grp_ready, 1)

            def store_sums(g, b, ch):
                pool.wait_ge(sums_taken[ch], g * NB + b + 1)
                dst = att_sums[ds(g * HG, HG), :, :, b * L + ch * CH:b * L + (ch + 1) * CH]
                pool.dma_start(dst.rearrange("h k d n -> (h k d) n"), sums[:, ch]).then_inc(sums_out[ch], 16)

            pool.wait_ge(ones_rows, NB + 1)
            for b in range(NB):
                pool.wait_ge(p2["v_ready"][b], 2 * NC)
                take_values(0, b)
            for b in range(NB):
                pool.wait_ge(p2["xT_low"][b], NC * DB)
                pool.wait_ge(p2["v_full"][b], NC * 2)
            for k, (raw, dst, name) in enumerate(((w_1raw, w_1, "ffn_w1"), (w_2raw, w_2, "ffn_w2"))):
                pool.dma_start(raw, t["L1_xcond_" + name].rearrange("(k p) n -> p k n", p=P)).then_inc(w_mlp_in, 16)
                pool.wait_ge(w_mlp_in, 16 * (k + 1))
                split(dst[:, 0], dst[:, 1], raw, 6 + k)
                pool.wait_ge(w_split, 2 * (6 + k + 1))
            with pool.Fori(0, NG - 1) as g:
                for b in range(NB):
                    for ch in range(NC):
                        store_sums(g, b, ch)
                    pool.wait_ge(sa_pv_done, (g * NB + b + 1) * STEPS)
                    take_values(g + 1, b)
            for b in range(NB):
                for ch in range(NC):
                    store_sums(NG - 1, b, ch)

            def add_bias(name, b, done):
                bias = bc[:, BROAD.index(name)].unsqueeze(1).to_broadcast([P, QB, D])
                nc.gpsimd.tensor_tensor(xc[:, b], xc[:, b], bias, ALU.add).then_inc(done[b], 1)

            with pool.Fori(0, NC) as c:
                n = c + NC
                for b in range(NB):
                    pool.wait_ge(p4["y_out"][b], c * 16)
                    bias = bc[:, BROAD.index("L1_xcond_sa_ob")].unsqueeze(1).to_broadcast([P, QB, D])
                    nc.gpsimd.tensor_tensor(xc[:, b], x_tok[:, ds(c * QB + b * TB, QB), :], bias,
                                            ALU.add).then_inc(p4["x1_in"][b], 1)
                for b in range(NB):
                    pool.wait_ge(px["xT_full"][b], (n + 1) * DB)
                    add_bias("L1_xcond_ca_ob", b, px["biased"])
                for b in range(NB):
                    low_rows(p4, "hT_high", "hT_low", c, b)
                for b in range(NB):
                    pool.wait_ge(px["normed"][b], n + 1)
                    add_bias("L1_xcond_ffn_b2", b, p4["b2_added"])

        @block.tensor
        def _(pe):
            def transpose_rows(src, b, k0, done):
                for d in range(DB):
                    for i in range(QB):
                        last = nc.tensor.transpose(bank(b, k0 + d)[:, i * P:(i + 1) * P],
                                                   src[:, b, i, d * P:(d + 1) * P], ident[:])
                    last.then_inc(done[b], 1)

            PRODUCTS = ((0, 0), (1, 0), (0, 1))

            def products(out, left, right, n, low=None):
                for k, (l, r) in enumerate(PRODUCTS):
                    if r == 1 and low is not None:
                        pe.wait_ge(*low)
                    for d in range(n):
                        last = nc.tensor.matmul(out, left(l, d), right(r, d), start=(k == 0 and d == 0),
                                                stop=(k == len(PRODUCTS) - 1 and d == n - 1))
                return last

            def project(w, b, k0, done, low):
                for o in range(DB):
                    products(bank(b, k0 + o), lambda l, d: w[:, l, d, o * P:(o + 1) * P],
                             lambda r, d: xT[:, r, b, d, :], DB, low if o == 0 else None).then_inc(done[b], 1)

            def project_rows(src, w, b, k0, done):
                for i in range(QB):
                    last = products(bank(b, k0 + i // 2)[:, (i % 2) * D:(i % 2 + 1) * D],
                                    lambda l, d: src[:, l, b, d, i * P:(i + 1) * P], lambda r, d: w[:, r, d, :], DB)
                    if i % 2:
                        last.then_inc(done[b], 1)

            def scores(ph, c, b):
                pe.wait_ge(ph["q_high"][b], (c + 1) * DB)
                pe.wait_ge(ph["q_low"][b], (c + 1) * DB)
                for i in range(QB):
                    for d in range(DB):
                        u = i * DB + d
                        if u >= 2:
                            pe.wait_ge(ph["max_done"][b], c * QB * DB + u - 1)
                        products(bank(b, u % 2), lambda l, _: qT[:, l, b, d, i * P:(i + 1) * P],
                                 lambda r, _: kbd[:, r, b, d, :], 1).then_inc(ph["s_full"][b], 1)

            def attend(ph, a, c, b):
                pe.wait_ge(ph["split_step"], (c * NB + b + 1) * 4)
                turned = bank(b, 2)[0:PARTS * PR, 0:CH // 2].bitcast(BF16)
                for i in range(QB):
                    last = nc.tensor.transpose(turned[:, i * P:(i + 1) * P], max_parts[:, b, i, :], ident_h[:])
                last.then_inc(ph["maxT_full"][b], 1)
                pe.wait_ge(ph["maxT_ready"][b], c + 1)
                for d in range(DB):
                    for k in range(PB):
                        p = d * PB + k
                        if p >= 2:
                            pe.wait_ge(ph["exp_done"][b], c * NP + p - 1)
                        for l, r in PRODUCTS:
                            nc.tensor.matmul(bank(b, p % 2), kbd[:, l, b, d, k * P:(k + 1) * P], qT[:, r, b, d, :],
                                             start=(l == 0 and r == 0), stop=False)
                        nc.tensor.matmul(bank(b, p % 2), pick[:, p].rearrange("r e k -> r (e k)"), maxT[:, b, :],
                                         start=False, stop=True).then_inc(ph["st_full"][b], 1)
                    pe.wait_ge(ph["exp_done"][b], c * NP + (d + 1) * PB)
                    pe.wait_ge(ph["outT_ready"][b], c * DB + d)
                    for k in range(PB):
                        nc.tensor.matmul(bank(b, 2)[32 * k:32 * k + 32, :], vbd[:, a, b, d * PB + k, :],
                                         probs[:, d * PB + k, :], start=True, stop=True)
                    for k in range(PB):
                        last = nc.tensor.matmul(bank(b, 3)[32 * k:32 * k + 32, :],
                                                ones_bd[:].rearrange("p e k -> p (e k)"),
                                                probs[:, d * PB + k, :], start=True, stop=True)
                    last.then_inc(ph["pv_full"][b], 1)

            def prepare(a):
                cond = vec[:, 0:4].rearrange("p (b k) -> p k b", b=NB)
                silu_c = silu[:, 2, :].rearrange("p (b k) -> p k b", b=NB)
                pe.wait_ge(w_ada_in[a], 16 * 2)
                for n in (ADA_Q, ADA_KV) if a == 0 else (ADA_1, ADA_2):
                    for o in range(4):
                        for d in range(DB):
                            last = nc.tensor.matmul(ps[:, 1, (n * 4 + o) * NB:(n * 4 + o + 1) * NB],
                                                    w_ada[:, n, d, o * P:(o + 1) * P],
                                                    (silu_c if a == 0 else cond)[:, d, :],
                                                    start=(d == 0), stop=(d == DB - 1))
                last.then_inc(ss_full, 1)
                key_w = w_kv0[:, :, 0:D] if a == 0 else w_kv1[:, 0]
                val_w = w_kv0[:, :, D:2 * D] if a == 0 else w_kv1[:, 1]
                pe.wait_ge(w_kv_in[a], 16 * (a + 1))
                pe.wait_ge(ctxT_ready, 1 + (a == 0))
                for o in range(DB):
                    for b in range(NB):
                        for d in range(DB):
                            last = nc.tensor.matmul(ps[:, 3, (o * NB + b) * LK:(o * NB + b + 1) * LK],
                                                    key_w[:, d, o * P:(o + 1) * P], ctxT[:, a, d, b, 0, :],
                                                    start=(d == 0), stop=(d == DB - 1))
                last.then_inc(ctx_k_full, 1)
                for b in range(NB):
                    for d in range(DB):
                        last = nc.tensor.matmul(ps[:, 4, b * D:(b + 1) * D],
                                                ctxT[:, a, d, b].rearrange("p e k -> p (e k)"), val_w[:, d, :],
                                                start=(d == 0), stop=(d == DB - 1))
                last.then_inc(ctx_v_full, 1)

            def turn_vectors(k, tile, first, n):
                pe.wait_ge(vec_in[k], 16 * (N_VECS0 if k == 0 else len(VECS) - N_VECS0))
                nc.tensor.transpose(ps[:, 0, first:first + n], tile[:], ident[0:n, 0:n]).then_inc(vec_full, 1)

            pe.wait_ge(consts_made, 1)
            turn_vectors(0, vrow, 0, NVEC0)
            pe.wait_ge(ctx_hat_ready, 1)
            for k, src in enumerate((ctx_hat, ctx_tok)):
                for d in range(DB):
                    last = nc.tensor.transpose(ps[:, 2, (k * DB + d) * P:(k * DB + d + 1) * P],
                                               src[:, d * P:(d + 1) * P], ident[:])
            last.then_inc(ctxT_full, 1)
            pe.wait_ge(silu_ready, 1)
            prepare(0)

            pe.wait_ge(vbd_ready, 1)
            pe.wait_ge(kbd_ready, 1)
            pe.wait_ge(w_0_split, 4)
            with pe.Fori(0, NC) as c:
                for b in range(NB):
                    pe.wait_ge(px["normed"][b], c + 1)
                    pe.wait_ge(px["added"][b], c * 2)
                    transpose_rows(xh, b, 0, px["xT_full"])
                for b in range(NB):
                    pe.wait_ge(px["xT_high"][b], c * 2 * DB + DB)
                    project(w_q0, b, 2, px["q_full"], (px["xT_low"][b], (c + 1) * DB))
                for b in range(NB):
                    scores(px, c, b)
                for b in range(NB):
                    attend(px, 0, c, b)
                for b in range(NB):
                    pe.wait_ge(px["outT_ready"][b], (c + 1) * DB)
                    project_rows(outT, w_p0, b, 0, px["o_full"])

            for b in range(NB):
                pe.wait_ge(px["added"][b], 2 * NC)
            turn_vectors(1, vrow1, NVEC0, NVEC - NVEC0)
            prepare(1)
            pe.wait_ge(vec_ready, 2)
            pe.wait_ge(ss_step, 3)
            pe.wait_ge(ktx_ready, 2)
            pe.wait_ge(vtx_ready, 2)

            pe.wait_ge(w_split, 2 * 3)
            with pe.Fori(0, NC) as c:
                for b in range(NB):
                    pe.wait_ge(p2["normed"][b], c + 1)
                    pe.wait_ge(p2["qk_taken"][b], c * 4)
                    transpose_rows(xh, b, 0, p2["xT_full"])
                for b in range(NB):
                    pe.wait_ge(p2["xT_high"][b], c * 2 * DB + DB)
                    pe.wait_ge(p2["v_ready"][b], c * 2)
                    project(w_sa[:, 0], b, 2, p2["qk_full"], (p2["xT_low"][b], (c + 1) * DB))
                for b in range(NB):
                    project(w_sa[:, 1], b, 0, p2["qk_full"], None)
                for b in range(NB):
                    pe.wait_ge(p2["qk_taken"][b], c * 4 + 2)
                    project_rows(xT, w_sa[:, 2], b, 2, p2["v_full"])

            for b in range(NB):
                pe.wait_ge(p2["qk_taken"][b], 4 * NC)
                pe.wait_ge(p2["v_ready"][b], 2 * NC)

            def score_tile(a, n):
                j, q = n // TB, n % TB
                if q == 0:
                    pe.wait_ge(stack_a[j], (a + 1) * 16 * LOADS)
                if n == 0:
                    pe.wait_ge(sa_max_done, a * QT)
                    pe.wait_ge(sa_maxT_ready, a)
                elif n >= 2:
                    pe.wait_ge(sa_max_done, a * QT + n - 1)
                for k in range(2):
                    last = nc.tensor.matmul(ps[:, 4 + 2 * (n % 2) + k, :], qa[0:ROWS, j, q * P:(q + 1) * P],
                                            ka[0:ROWS, j, k * CH:(k + 1) * CH], start=True, stop=True)
                last.then_inc(sa_s_full, 1)

            def turn_maxima(a):
                pe.wait_ge(sa_split_step, (a + 1) * 4)
                nc.tensor.transpose(ps[0:PARTS * QT, 4, 0:P // 2].bitcast(BF16),
                                    max_parts_g[:].rearrange("p a n -> p (a n)"), ident_h[:]).then_inc(sa_maxT_full, 1)

            def weigh(half, b, s):
                ch, kb = s // TB, s % TB
                pe.wait_ge(sa_exp_done, half * STEPS * HG + (s + 1) * HG)
                if s == 0:
                    pe.wait_ge(v_grp_ready, half + 1)
                    pe.wait_ge(sums_taken[1], half)
                elif kb == 0:
                    pe.wait_ge(sums_taken[0], half + 1)
                for j in range(HG):
                    last = nc.tensor.matmul(ps[32 * j:32 * j + 32, 3, :], v_grp[:, b, kb, j, :],
                                            probs[:, (s % 2) * HG + j, :], start=(kb == 0), stop=(kb == TB - 1))
                last.then_inc(sa_pv_done, 1)

            def attend_group(g, b, more):
                half = g * NB + b
                pe.wait_ge(stack_s[b], (g + 1) * 16 * 2)
                pe.wait_ge(shift_in[b], (g + 1) * 16 * PARTS)
                pe.wait_ge(sa_exp_done, half * STEPS * HG)
                for s in range(STEPS):
                    ch, kb = s // TB, s % TB
                    tiles = tile_plan(s) if more else []
                    for j in range(HG):
                        u = s * HG + j
                        if u >= 3:
                            pe.wait_ge(sa_exp_done, half * STEPS * HG + u - 2)
                        nc.tensor.matmul(ps[:, u % 3, :], ks[b][0:ROWS_M, j, kb * P:(kb + 1) * P],
                                         qs[b][0:ROWS_M, j, ch * CH:(ch + 1) * CH],
                                         start=True, stop=True).then_inc(sa_st_full, 1)
                        if j < len(tiles):
                            score_tile(half + 1, tiles[j])
                    if s == STEPS - 1 and more:
                        turn_maxima(half + 1)
                    if s > 0:
                        weigh(half, b, s - 1)
                weigh(half, b, STEPS - 1)

            pe.wait_ge(ones_rows, NB + 1)
            for n in range(QT):
                score_tile(0, n)
            turn_maxima(0)
            with pe.Fori(0, NG - 1) as g:
                for b in range(NB):
                    attend_group(g, b, True)
            for b in range(NB):
                attend_group(NG - 1, b, b < NB - 1)

            pe.wait_ge(sa_exp_done, HALVES * STEPS * HG)
            pe.wait_ge(sa_max_done, HALVES * QT)
            pe.wait_ge(sa_maxT_ready, HALVES)
            for ch in range(NC):
                pe.wait_ge(sums_taken[ch], HALVES)
            pe.wait_ge(kbd_ready, 2)
            pe.wait_ge(vbd_ready, 2)
            pe.wait_ge(w_split, 2 * 8)
            with pe.Fori(0, NC) as c:
                n = c + NC
                for b in range(NB):
                    pe.wait_ge(p4["outT_ready"][b], (c + 1) * DB)
                    pe.wait_ge(p4["y_ready"][b], c * 2)
                    project_rows(outT, w_out[:, 0], b, 2, p4["so_full"])
                for b in range(NB):
                    pe.wait_ge(p4["x2_ready"][b], (c + 1) * 2)
                    pe.wait_ge(p4["hid_high"][b], c * FB)
                    transpose_rows(xc, b, 0, px["xT_full"])
                for b in range(NB):
                    pe.wait_ge(px["xT_high"][b], (n + 1) * 2 * DB)
                    project(w_out[:, 1], b, 2, px["q_full"], (px["xT_low"][b], (n + 1) * DB))
                for b in range(NB):
                    scores(px, n, b)
                for b in range(NB):
                    attend(px, 1, n, b)
                for b in range(NB):
                    pe.wait_ge(px["outT_ready"][b], (n + 1) * DB)
                    project_rows(outT, w_out[:, 2], b, 0, px["o_full"])
                for b in range(NB):
                    pe.wait_ge(px["normed"][b], n + 1)
                    transpose_rows(xh, b, 2, p4["hT_full"])
                for b in range(NB):
                    pe.wait_ge(p4["hT_high"][b], c * 2 * DB + DB)
                    for f in range(FB):
                        if f >= 2:
                            pe.wait_ge(p4["hid_high"][b], c * FB + f - 1)
                        products(bank(b, f % 2), lambda l, d: w_1[:, l, d, f * P:(f + 1) * P],
                                 lambda r, d: xT[:, r, b, d, :], DB,
                                 (p4["hT_low"][b], (c + 1) * DB) if f == 0 else None).then_inc(p4["hid_full"][b], 1)
                    for i in range(QB):
                        for f in range(FB):
                            if i == 0:
                                pe.wait_ge(p4["hid_low"][b], c * FB + f + 1)
                            for k, (l, r) in enumerate(PRODUCTS):
                                last = nc.tensor.matmul(bank(b, 2 + i // 2)[:, (i % 2) * D:(i % 2 + 1) * D],
                                                        hidT[:, f, l, i * P:(i + 1) * P], w_2[:, r, f, :],
                                                        start=(f == 0 and k == 0),
                                                        stop=(f == FB - 1 and k == len(PRODUCTS) - 1))
                        if i % 2:
                            last.then_inc(p4["y_full"][b], 1)

        @block.vector
        def _(dve):
            def aggregate(st, m, y, step, at):
                n = y.shape[1]
                v, w, a, q = (newton[:, k, 0:n] for k in range(4))
                dve.wait_ge(step, at)
                nc.vector.tensor_tensor(w, st[:, :, 1], st[:, :, 4], ALU.add)
                nc.vector.tensor_tensor(a, st[:, :, 1], st[:, :, 4], ALU.subtract)
                nc.vector.tensor_tensor(v, st[:, :, 2], st[:, :, 5], ALU.add).then_inc(step, 1)
                dve.wait_ge(step, at + 1)
                nc.vector.tensor_scalar(m, w, 0.5, None, ALU.mult)
                nc.vector.tensor_tensor(q, a, a, ALU.mult).then_inc(step, 1)
                dve.wait_ge(step, at + 2)
                nc.vector.scalar_tensor_tensor(out=a, in0=q, scalar=D / 4, in1=v, op0=ALU.mult,
                                               op1=ALU.add).then_inc(step, 1)
                dve.wait_ge(step, at + 3)
                at = at + 3
                nc.vector.tensor_scalar(v, a, 1.0 / D, EPS, ALU.mult, ALU.add).then_inc(step, 1)
                dve.wait_ge(step, at + 1)
                nc.vector.tensor_scalar(a.bitcast(I32), v.bitcast(I32), 1, None,
                                        ALU.logical_shift_right).then_inc(step, 1)
                dve.wait_ge(step, at + 2)
                nc.vector.tensor_scalar(y.bitcast(I32), a.bitcast(I32), -1.0, float(0x5f3759df), ALU.mult, ALU.add)
                nc.vector.tensor_scalar(w, v, -0.5, None, ALU.mult).then_inc(step, 1)
                for k in range(NEWTON):
                    dve.wait_ge(step, at + 3 + 3 * k)
                    nc.vector.tensor_tensor(a, y, w, ALU.mult).then_inc(step, 1)
                    dve.wait_ge(step, at + 4 + 3 * k)
                    nc.vector.tensor_tensor(a, a, y, ALU.mult).then_inc(step, 1)
                    dve.wait_ge(step, at + 5 + 3 * k)
                    nc.vector.scalar_tensor_tensor(out=y, in0=a, scalar=1.5, in1=y, op0=ALU.add,
                                                   op1=ALU.mult).then_inc(step, 1)
                dve.wait_ge(step, at + 3 + 3 * NEWTON)

            def norm_rows(ph, src, n, b):
                for i in range(QB):
                    last = nc.vector.bn_stats(stats[:, b, i, :], src[:, i, :])
                last.then_inc(ph["norm_step"], 1)
                aggregate(stats[:, b], mean[:, b, :], rstd[:, b, :], ph["norm_step"],
                          (n * NB + b) * NORM_STEPS + 1)
                for i in range(QB):
                    last = nc.vector.tensor_scalar(xh[:, b, i, :], src[:, i, :], mean[:, b, i:i + 1],
                                                   rstd[:, b, i:i + 1], ALU.subtract, ALU.mult)
                last.then_inc(ph["normed"][b], 1)

            def maxima(ph, c, b):
                for i in range(QB):
                    for d in range(DB):
                        u = i * DB + d
                        dve.wait_ge(ph["s_full"][b], c * QB * DB + u + 1)
                        last = nc.vector.tensor_reduce(negmax[:, b, i, d * HB:(d + 1) * HB],
                                                       bank(b, u % 2).rearrange("p (h k) -> p h k", k=LK),
                                                       AX.X, ALU.max, negate=True)
                        last.then_inc(ph["max_done"][b], 1)
                dve.wait_ge(ph["max_done"][b], (c + 1) * QB * DB)
                high, mid, low = (max_parts[:, b, :, k * PR:k * PR + H] for k in range(PARTS))
                at = (c * NB + b) * 4
                nc.vector.tensor_copy(high, negmax[:, b]).then_inc(ph["split_step"], 1)
                dve.wait_ge(ph["split_step"], at + 1)
                nc.vector.tensor_tensor(max_rest[:, b], negmax[:, b], high, ALU.subtract).then_inc(ph["split_step"], 1)
                dve.wait_ge(ph["split_step"], at + 2)
                nc.vector.tensor_copy(mid, max_rest[:, b]).then_inc(ph["split_step"], 1)
                dve.wait_ge(ph["split_step"], at + 3)
                nc.vector.tensor_tensor(low, max_rest[:, b], mid, ALU.subtract).then_inc(ph["split_step"], 1)

            def normalise(ph, num, den, n, b):
                r, u = tmp[:, b, :], tmp[:, 2 + b, :]
                for d in range(DB):
                    step = ((n * NB + b) * DB + d) * 4
                    dve.wait_ge(ph["recip_done"][b], n * DB + d + 1)
                    nc.vector.tensor_tensor(u, den(d), r, ALU.mult).then_inc(ph["out_step"], 1)
                    dve.wait_ge(ph["out_step"], step + 1)
                    nc.vector.scalar_tensor_tensor(out=u, in0=u, scalar=-2.0, in1=r, op0=ALU.add,
                                                   op1=ALU.mult).then_inc(ph["out_step"], 1)
                    dve.wait_ge(ph["out_step"], step + 2)
                    nc.vector.scalar_tensor_tensor(out=u, in0=num(d), scalar=-1.0, in1=u, op0=ALU.mult,
                                                   op1=ALU.mult).then_inc(ph["out_step"], 1)
                    dve.wait_ge(ph["out_step"], step + 3)
                    nc.vector.tensor_copy(outT[:, 0, b, d, :], u).then_inc(ph["out_step"], 1)
                    dve.wait_ge(ph["out_step"], step + 4)
                    nc.vector.tensor_tensor(outT[:, 1, b, d, :], u, outT[:, 0, b, d, :].bitcast(F32),
                                            ALU.subtract).then_inc(ph["outT_ready"][b], 1)

            def low_queries(ph, n, b, name):
                for d in range(DB):
                    dve.wait_ge(ph["q_high"][b], n * DB + d + 1)
                    nc.vector.scalar_tensor_tensor(out=qT[:, 1, b, d, :], in0=bank(b, 2 + d),
                                                   scalar=vec[:, VCOL[name] + d:VCOL[name] + d + 1],
                                                   in1=qT[:, 0, b, d, :].bitcast(F32), op0=ALU.add,
                                                   op1=ALU.subtract).then_inc(ph["q_low"][b], 1)

            def add_rows(full, done, dst, n, b, k0):
                for k in range(2):
                    dve.wait_ge(full[b], n * 2 + k + 1)
                    nc.vector.tensor_tensor(dst(k), bank(b, k0 + k).rearrange("p (i n) -> p i n", i=2), dst(k),
                                            ALU.add).then_inc(done[b], 1)

            dve.wait_ge(ctx_in, 16)
            nc.vector.bn_stats(stats[:, 0, 0, :], ctx_tok).then_inc(ctx_step, 1)
            aggregate(stats[:, 0, 0:1], mean[:, 0, 0:1], rstd[:, 0, 0:1], ctx_step, 1)
            nc.vector.tensor_scalar(ctx_hat, ctx_tok, mean[:, 0, 0:1], rstd[:, 0, 0:1], ALU.subtract,
                                    ALU.mult).then_inc(ctx_hat_ready, 1)
            dve.wait_ge(silu_exp, 1)
            nc.vector.tensor_scalar(silu[:, 1], silu[:, 0], 1.0, None, ALU.add).then_inc(silu_step, 1)
            dve.wait_ge(silu_step, 1)
            nc.vector.reciprocal(silu[:, 0], silu[:, 1]).then_inc(silu_step, 1)
            dve.wait_ge(silu_step, 2)
            nc.vector.tensor_tensor(silu[:, 2], vec[:, 0:4], silu[:, 0], ALU.mult).then_inc(silu_ready, 1)
            def prepare(a):
                sets = (ADA_Q, ADA_KV) if a == 0 else (ADA_1, ADA_2)
                dve.wait_ge(ss_full, a + 1)
                if a == 1:
                    dve.wait_ge(vec_ready, 2)
                for n in sets:
                    bias = ADA[n][1]
                    cols = vec[:, VCOL[bias]:VCOL[bias] + 4].unsqueeze(2).to_broadcast([P, 4, NB])
                    last = nc.vector.tensor_tensor(ss[:, n], ps[:, 1, n * 4 * NB:(n + 1) * 4 * NB].rearrange(
                        "p (o b) -> p o b", b=NB), cols, ALU.add)
                last.then_inc(ss_step, 1)
                dve.wait_ge(ss_step, 2 * a + 1)
                if a == 0:
                    for n in sets:
                        nc.vector.tensor_scalar(ada_a[:, n], ss[:, n, 0:DB, :], 1.0, None, ALU.add)
                        last = nc.vector.tensor_copy(ada_b[:, n], ss[:, n, DB:2 * DB, :])
                    last.then_inc(ss_step, 1)
                    dve.wait_ge(ss_step, 2)
                else:
                    for n, g, beta in ((ADA_1, "L1_xcond_ln1_g", "L1_xcond_ln1_b"),
                                       (ADA_2, "L1_xcond_ln2_g", "L1_xcond_ln2_b")):
                        gain = vec[:, VCOL[g]:VCOL[g] + DB].unsqueeze(2).to_broadcast([P, DB, NB])
                        shift = vec[:, VCOL[beta]:VCOL[beta] + DB].unsqueeze(2).to_broadcast([P, DB, NB])
                        nc.vector.tensor_tensor(ada_a[:, n], ss[:, n, 0:DB, :], gain, ALU.mult)
                        last = nc.vector.tensor_tensor(ada_b[:, n], ss[:, n, 0:DB, :], shift, ALU.mult)
                    last.then_inc(ss_step, 1)
                    dve.wait_ge(ss_step, 4)
                    for n in sets:
                        last = nc.vector.tensor_tensor(ada_b[:, n], ada_b[:, n], ss[:, n, DB:2 * DB, :], ALU.add)
                    last.then_inc(ada_ready, 1)
                    dve.wait_ge(ada_ready, 1)
                if a == 0:
                    dve.wait_ge(ctxT_full, 1)
                    for d in range(DB):
                        for b in range(NB):
                            src = ps[:, 2, d * P + b * LK:d * P + (b + 1) * LK].unsqueeze(1).to_broadcast([P, 2, LK])
                            last = nc.vector.tensor_scalar(ctxT[:, 0, d, b], src, ada_a[:, ADA_KV, d, b:b + 1],
                                                           ada_b[:, ADA_KV, d, b:b + 1], ALU.mult, ALU.add)
                    last.then_inc(ctxT_ready, 1)
                    for d in range(DB):
                        src = ps[:, 2, (DB + d) * P:(DB + d + 1) * P].rearrange("p (b k) -> p b k", b=NB)
                        last = nc.vector.tensor_copy(ctxT[:, 1, d], src.unsqueeze(2).to_broadcast([P, NB, 2, LK]))
                    last.then_inc(ctxT_ready, 1)
                dve.wait_ge(ctx_k_full, a + 1)
                bias = ("L0_xcond_bkv", "L1_xcond_ca_kb")[a]
                for o in range(DB):
                    last = nc.vector.tensor_scalar(ktx[:, a, o].rearrange("p b k -> p (b k)"),
                                                   ps[:, 3, o * NB * LK:(o + 1) * NB * LK],
                                                   vec[:, VCOL[bias] + o:VCOL[bias] + o + 1], None, ALU.add)
                last.then_inc(ktx_ready, 1)
                dve.wait_ge(bc_in, 16 * len(BROAD))
                dve.wait_ge(consts_made, 1)
                dve.wait_ge(ctx_v_full, a + 1)
                name = ("L0_xcond_bv", "L1_xcond_ca_vb")[a]
                nc.vector.tensor_tensor(vtx[:, a], ps[:, 4, :].rearrange("p (b n) -> p b n", b=NB),
                                        bc[:, BROAD.index(name)].unsqueeze(1).to_broadcast([P, NB, D]),
                                        ALU.add).then_inc(vtx_ready, 1)
                dve.wait_ge(vtx_ready, a + 1)
                for b in range(NB):
                    for e in range(2):
                        last = nc.vector.tensor_scalar(
                            vbd[:, a, b].rearrange("p n (e k) -> p n e k", e=2)[:, :, e, :],
                            vtx[:, a, b].rearrange("p (n e k) -> p n e k", e=2, k=DH)[:, :, e, :],
                            half_mask[:, e:e + 1], None, ALU.mult)
                last.then_inc(vbd_ready, 1)

            def spread_keys(a):
                words = DB * NB * LK
                full = ktx[:, a].rearrange("p o b k -> p (o b k)")
                high, low = tmp[:, 0, 0:words], tmp[:, 1, 0:words]
                dve.wait_ge(ktx_ready, a + 1)
                nc.vector.tensor_copy(high.bitcast(F32R), full).then_inc(ktx_step, 1)
                dve.wait_ge(ktx_step, 2 * a + 1)
                nc.vector.tensor_tensor(low, full, high, ALU.subtract).then_inc(ktx_step, 1)
                dve.wait_ge(ktx_step, 2 * a + 2)
                for part, src in enumerate((high, low)):
                    src = src.rearrange("p (o b k) -> p o b k", o=DB, b=NB)
                    for b in range(NB):
                        for o in range(DB):
                            last = nc.vector.tensor_tensor(
                                kbd[:, part, b, o, :].rearrange("p (h k) -> p h k", k=LK),
                                src[:, o, b, :].unsqueeze(1).to_broadcast([P, HB, LK]),
                                head_mask[:].unsqueeze(2).to_broadcast([P, HB, LK]), ALU.mult)
                last.then_inc(kbd_ready, 1)

            prepare(0)
            spread_keys(0)
            dve.wait_ge(w_0_in, 16 * 2)
            for k, dst in enumerate((w_q0, w_p0)):
                nc.vector.tensor_copy(dst[:, 0], w_raw[:, k]).then_inc(w_0_split, 1)
                dve.wait_ge(w_0_split, 2 * k + 1)
                nc.vector.tensor_tensor(dst[:, 1], w_raw[:, k], dst[:, 0].bitcast(F32),
                                        ALU.subtract).then_inc(w_0_split, 1)

            dve.wait_ge(x_in, 16 * NB * NC)
            dve.wait_ge(w_split, 2 * 6)
            with dve.Fori(0, NC) as c:
                for b in range(NB):
                    dve.wait_ge(px["xT_low"][b], c * DB)
                    norm_rows(px, x_tok[:, ds(c * QB + b * TB, QB), :], c, b)
                for b in range(NB):
                    low_queries(px, c, b, "L0_xcond_bq")
                for b in range(NB):
                    maxima(px, c, b)
                for b in range(NB):
                    normalise(px, lambda d: bank(b, 2), lambda d: bank(b, 3), c, b)
                for b in range(NB):
                    dve.wait_ge(px["biased"][b], c + 1)
                    add_rows(px["o_full"], px["added"],
                             lambda k: x_tok[:, ds(c * QB + b * TB + 2 * k, 2), :], c, b, 0)
            for b in range(NB):
                dve.wait_ge(px["added"][b], 2 * NC)
            prepare(1)

            for b in range(NB):
                dve.wait_ge(px["xT_low"][b], NC * DB)
            with dve.Fori(0, NC) as c:
                for b in range(NB):
                    dve.wait_ge(p2["xT_low"][b], c * DB)
                    norm_rows(p2, x_tok[:, ds(c * QB + b * TB, QB), :], c, b)
                for k in range(2):
                    for b in range(NB):
                        dve.wait_ge(p2["parts_out"][b], c * 16 * 4)
                        for u in (2 * k, 2 * k + 1):
                            full = q_full[:, b, u, :]
                            high, mid = parts[:, b * 4 + u, 0, :], parts[:, b * 4 + u, 1, :]
                            dve.wait_ge(p2["qk_taken"][b], c * 4 + u + 1)
                            nc.vector.tensor_tensor(full, full, high, ALU.subtract).then_inc(p2["split_step"], 1)
                            dve.wait_ge(p2["split_step"], c * NB * 4 + k * NB * 2 + b * 2 + u % 2 + 1)
                            nc.vector.tensor_copy(mid, full).then_inc(p2["mid_ready"][b], 1)
                for b in range(NB):
                    for k in range(2):
                        dve.wait_ge(p2["v_full"][b], c * 2 + k + 1)
                        bias = bc[:, BROAD.index("L1_xcond_sa_vb")].rearrange("p (h n) -> p h n", n=DH)
                        for i in range(2):
                            last = nc.vector.tensor_tensor(
                                v_all[:, ds(c * QB + b * TB + 2 * k + i, 1), :, :].rearrange("p o h n -> p (o h) n"),
                                bank(b, 2 + k)[:, i * D:(i + 1) * D].rearrange("p (h n) -> p h n", n=DH),
                                bias, ALU.add)
                        last.then_inc(p2["v_ready"][b], 1)

            def group_maxima(a):
                for n in range(QT):
                    dve.wait_ge(sa_s_full, a * QT + n + 1)
                    at = 4 + 2 * (n % 2)
                    nc.vector.tensor_reduce(negmax_g[:, n:n + 1], ps[:, at:at + 2, :].rearrange("p a n -> p (a n)"),
                                            AX.X, ALU.max, negate=True).then_inc(sa_max_done, 1)
                dve.wait_ge(sa_max_done, (a + 1) * QT)
                high, mid, low = (max_parts_g[:, k, :] for k in range(PARTS))
                nc.vector.tensor_copy(high, negmax_g[:]).then_inc(sa_split_step, 1)
                dve.wait_ge(sa_split_step, a * 4 + 1)
                nc.vector.tensor_tensor(max_rest_g[:], negmax_g[:], high, ALU.subtract).then_inc(sa_split_step, 1)
                dve.wait_ge(sa_split_step, a * 4 + 2)
                nc.vector.tensor_copy(mid, max_rest_g[:]).then_inc(sa_split_step, 1)
                dve.wait_ge(sa_split_step, a * 4 + 3)
                nc.vector.tensor_tensor(low, max_rest_g[:], mid, ALU.subtract).then_inc(sa_split_step, 1)
                dve.wait_ge(sa_maxT_full, a + 1)
                for b in range(NB):
                    dve.wait_ge(shift_in[b], shifts_before(a, b))
                nc.vector.tensor_copy(maxT_g[:], ps[0:PARTS * QT, 4, 0:P // 2].bitcast(BF16)).then_inc(sa_maxT_ready, 1)

            at_half = {}

            def shifts_before(a, b):
                g, nb = at_half["g"], at_half["b"]
                return (g + (1 if b < nb else 0)) * 16 * PARTS

            def take_sums_last(g, b):
                half = g * NB + b
                dve.wait_ge(sa_pv_done, (half + 1) * STEPS)
                dve.wait_ge(sums_out[1], half * 16)
                nc.vector.tensor_copy(sums[:, 1], ps[:, 3, :]).then_inc(sums_taken[1], 1)

            at_half.update(g=0, b=0)
            group_maxima(0)
            with dve.Fori(0, NG - 1) as g:
                for b in range(NB):
                    at_half.update(g=(g if b == 0 else g + 1), b=1 - b)
                    group_maxima(g * NB + b + 1)
                    take_sums_last(g, b)
            at_half.update(g=NG - 1, b=1)
            group_maxima(HALVES - 1)
            take_sums_last(NG - 1, 0)
            dve.wait_ge(v_grp_ready, HALVES)
            spread_keys(1)
            take_sums_last(NG - 1, 1)

            def add_last(c, b):
                dve.wait_ge(p4["b2_added"][b], c + 1)
                add_rows(p4["y_full"], p4["y_ready"], lambda k: xc[:, b, 2 * k:2 * k + 2, :], c, b, 2)

            dve.wait_ge(w_split, 2 * 8)
            with dve.Fori(0, NC) as c:
                n = c + NC
                dve.wait_ge(p4["y_full"][1], c * 2)
                for b in range(NB):
                    dve.wait_ge(p4["att_in"][b], (c + 1) * 16 * 2 * DB)
                    normalise(p4, lambda d: attT[:, b, d, :], lambda d: denT[:, b, d, :], c, b)
                for b in range(NB):
                    dve.wait_ge(p4["x1_in"][b], c + 1)
                    add_rows(p4["so_full"], p4["x2_ready"], lambda k: xc[:, b, 2 * k:2 * k + 2, :], c, b, 2)
                for b in range(NB):
                    for d in range(DB):
                        dve.wait_ge(px["xT_high"][b], (n * DB + d + 1) * 2)
                        nc.vector.tensor_tensor(xT[:, 1, b, d, :], bank(b, d), xT[:, 0, b, d, :].bitcast(F32),
                                                ALU.subtract).then_inc(px["xT_low"][b], 1)
                for b in range(NB):
                    low_queries(px, n, b, "L1_xcond_ca_qb")
                for b in range(NB):
                    maxima(px, n, b)
                for b in range(NB):
                    normalise(px, lambda d: bank(b, 2), lambda d: bank(b, 3), n, b)
                for b in range(NB):
                    dve.wait_ge(px["biased"][b], n + 1)
                    add_rows(px["o_full"], px["added"], lambda k: xc[:, b, 2 * k:2 * k + 2, :], n, b, 0)
                    dve.wait_ge(px["added"][b], (n + 1) * 2)
                    dve.wait_ge(p4["hT_low"][b], c * DB)
                    norm_rows(px, xc[:, b], n, b)
                for b in range(NB):
                    for f in range(FB):
                        dve.wait_ge(p4["hid_high"][b], c * FB + f + 1)
                        nc.vector.tensor_tensor(hidT[:, f, 1, :], tmp[:, f % 4, :], hidT[:, f, 0, :].bitcast(F32),
                                                ALU.subtract).then_inc(p4["hid_low"][b], 1)
                    if b > 0:
                        add_last(c, b - 1)
                add_last(c, NB - 1)

        @block.scalar
        def _(act):
            def turned_rows(full, high, n, b, k0, ada):
                for d in range(DB):
                    act.wait_ge(full[b], n * DB + d + 1)
                    if ada is None:
                        nc.scalar.activation(xT[:, 0, b, d, :], bank(b, k0 + d), ACT.Copy).then_inc(high[b], 2)
                    else:
                        nc.scalar.activation(xT[:, 0, b, d, :], bank(b, k0 + d), ACT.Identity,
                                             scale=ada_a[:, ada, d, b:b + 1],
                                             bias=ada_b[:, ada, d, b:b + 1]).then_inc(high[b], 1)
                for d in range(DB if ada is not None else 0):
                    nc.scalar.activation(xf[:, b, d, :], bank(b, k0 + d), ACT.Identity,
                                         scale=ada_a[:, ada, d, b:b + 1],
                                         bias=ada_b[:, ada, d, b:b + 1]).then_inc(high[b], 1)

            def queries(ph, c, b, name):
                for d in range(DB):
                    act.wait_ge(ph["q_full"][b], c * DB + d + 1)
                    nc.scalar.activation(qT[:, 0, b, d, :], bank(b, 2 + d), ACT.Identity,
                                         bias=vec[:, VCOL[name] + d:VCOL[name] + d + 1]).then_inc(ph["q_high"][b], 1)

            def reciprocals(ph, den, n, b):
                for d in range(DB):
                    if den is None:
                        act.wait_ge(ph["pv_full"][b], n * DB + d + 1)
                    act.wait_ge(ph["outT_ready"][b], n * DB + d)
                    src = bank(b, 3) if den is None else den[:, b, d, :]
                    nc.scalar.activation(tmp[:, b, :], src, ACT.Ln).then_inc(ph["log_done"], 1)
                    act.wait_ge(ph["log_done"], (n * NB + b) * DB + d + 1)
                    nc.scalar.activation(tmp[:, b, :], tmp[:, b, :], ACT.Exp,
                                         scale=-1.0).then_inc(ph["recip_done"][b], 1)

            def exponentials(ph, c, b):
                act.wait_ge(ph["maxT_full"][b], c + 1)
                nc.scalar.activation(maxT[:, b, :], bank(b, 2)[0:PARTS * PR, 0:CH // 2].bitcast(BF16),
                                     ACT.Copy).then_inc(ph["maxT_ready"][b], 1)
                act.wait_ge(ph["pv_full"][1 - b], (c + b) * DB)
                for p in range(NP):
                    act.wait_ge(ph["st_full"][b], c * NP + p + 1)
                    nc.scalar.activation(probs[:, p, :], bank(b, p % 2), ACT.Exp,
                                         scale=SCALE).then_inc(ph["exp_done"][b], 1)
                reciprocals(ph, None, c, b)

            act.wait_ge(vec_full, 1)
            nc.scalar.activation(vec[:, 0:NVEC0], ps[:, 0, 0:NVEC0], ACT.Copy).then_inc(vec_ready, 1)
            act.wait_ge(vec_ready, 1)
            nc.scalar.activation(silu[:, 0], vec[:, 0:4], ACT.Exp, scale=-1.0).then_inc(silu_exp, 1)

            act.wait_ge(vbd_ready, 1)
            act.wait_ge(kbd_ready, 1)
            with act.Fori(0, NC) as c:
                for b in range(NB):
                    turned_rows(px["xT_full"], px["xT_high"], c, b, 0, ADA_Q)
                for b in range(NB):
                    queries(px, c, b, "L0_xcond_bq")
                for b in range(NB):
                    exponentials(px, c, b)

            act.wait_ge(vec_full, 2)
            nc.scalar.activation(vec[:, NVEC0:NVEC], ps[:, 0, NVEC0:NVEC], ACT.Copy).then_inc(vec_ready, 1)
            act.wait_ge(vbd_ready, 2)
            with act.Fori(0, NC) as c:
                for b in range(NB):
                    turned_rows(p2["xT_full"], p2["xT_high"], c, b, 0, ADA_1)
                for k, name in enumerate(("L1_xcond_sa_qb", "L1_xcond_sa_kb")):
                    for b in range(NB):
                        act.wait_ge(p2["parts_ready"][b], c * 4)
                        act.wait_ge(p2["parts_out"][b], c * 16 * 4)
                        for d in range(DB):
                            u = k * DB + d
                            src = bank(b, 2 - 2 * k + d)
                            bias = vec[:, VCOL[name] + d:VCOL[name] + d + 1]
                            act.wait_ge(p2["qk_full"][b], c * 4 + u + 1)
                            nc.scalar.activation(q_full[:, b, u, :], src, ACT.Identity, bias=bias)
                            nc.scalar.activation(parts[:, b * 4 + u, 0, :], src, ACT.Identity,
                                                 bias=bias).then_inc(p2["qk_taken"][b], 1)

            for b in range(NB):
                act.wait_ge(p2["parts_ready"][b], 4 * NC)

            def group_exponentials(g, b):
                half = g * NB + b
                for s in range(STEPS):
                    act.wait_ge(sa_pv_done, half * STEPS + max(s - 1, 0))
                    for j in range(HG):
                        u = s * HG + j
                        act.wait_ge(sa_st_full, half * STEPS * HG + u + 1)
                        nc.scalar.activation(probs[:, (s % 2) * HG + j, :], ps[:, u % 3, :], ACT.Exp,
                                             scale=SCALE).then_inc(sa_exp_done, 1)
                    if s == TB:
                        act.wait_ge(sa_pv_done, half * STEPS + TB)
                        act.wait_ge(sums_out[0], half * 16)
                        nc.scalar.activation(sums[:, 0], ps[:, 3, :], ACT.Copy).then_inc(sums_taken[0], 1)

            with act.Fori(0, NG - 1) as g:
                for b in range(NB):
                    group_exponentials(g, b)
            for b in range(NB):
                group_exponentials(NG - 1, b)

            act.wait_ge(sa_pv_done, HALVES * STEPS)
            with act.Fori(0, NC) as c:
                n = c + NC
                for b in range(NB):
                    act.wait_ge(p4["att_in"][b], (c + 1) * 16 * 2 * DB)
                    reciprocals(p4, denT, c, b)
                for b in range(NB):
                    turned_rows(px["xT_full"], px["xT_high"], n, b, 0, None)
                for b in range(NB):
                    queries(px, n, b, "L1_xcond_ca_qb")
                for b in range(NB):
                    exponentials(px, n, b)
                for b in range(NB):
                    turned_rows(p4["hT_full"], p4["hT_high"], c, b, 2, ADA_2)
                for b in range(NB):
                    act.wait_ge(p4["y_full"][1 - b], (c + b) * 2)
                    for f in range(FB):
                        if f >= 4:
                            act.wait_ge(p4["hid_low"][b], c * FB + f - 3)
                        act.wait_ge(p4["hid_full"][b], c * FB + f + 1)
                        bias = vec[:, VCOL["L1_xcond_ffn_b1"] + f:VCOL["L1_xcond_ffn_b1"] + f + 1]
                        nc.scalar.activation(hidT[:, f, 0, :], bank(b, f % 2), ACT.Gelu, bias=bias)
                        nc.scalar.activation(tmp[:, f % 4, :], bank(b, f % 2), ACT.Gelu,
                                             bias=bias).then_inc(p4["hid_high"][b], 1)


_INS = ["x", "ctx_1024", "cond_1024"] + ["L0_xcond_" + n for n in (
    "Wq", "bq", "Wkv", "bkv", "Wp", "bp", "Wss_q", "bss_q", "Wss_kv", "bss_kv")] + ["L1_xcond_" + n for n in (
        "ln1_g", "ln1_b", "aff1_w", "aff1_b", "ln2_g", "ln2_b", "aff2_w", "aff2_b", "sa_qw", "sa_qb", "sa_kw",
        "sa_kb", "sa_vw", "sa_vb", "sa_ow", "sa_ob", "ca_qw", "ca_qb", "ca_kw", "ca_kb", "ca_vw", "ca_vb",
        "ca_ow", "ca_ob", "ffn_w1", "ffn_b1", "ffn_w2", "ffn_b2")]


def kernel(**inputs):
    import numpy as _np
    import concourse.bacc as _bacc
    from concourse import mybir as _mybir
    from concourse.bass_utils import run_bass_kernel_spmd as _run

    nc = _bacc.Bacc("TRN2", target_bir_lowering=False, num_devices=1)
    arrays, tensors = {}, {}
    for name in _INS:
        a = _np.ascontiguousarray(inputs[name])
        arrays[f"in_{name}_dram"] = a
        tensors[name] = nc.dram_tensor(f"in_{name}_dram", a.shape, _mybir.dt.from_np(a.dtype),
                                       kind="ExternalInput").ap()
    out = nc.dram_tensor("out_0_dram", (NB, L, D), _mybir.dt.from_np(_np.dtype("float32")), kind="ExternalOutput").ap()
    build(nc, tensors, out)
    r = _run(nc, [arrays], core_ids=[0])
    return r.results[0]["out_0_dram"]
```

```python
from contextlib import ExitStack

import concourse.bass as bass
from concourse import mybir

ALU = mybir.AluOpType
ACT = mybir.ActivationFunctionType
AX = mybir.AxisListType
F32 = mybir.dt.float32
BF16 = mybir.dt.bfloat16
F32R = mybir.dt.float32r
I32 = mybir.dt.int32
ds = bass.ds

P = 128
NB = 2
L = 1024
D = 256
H = 16
DH = D // H
LK = 64
FF = 1024
EPS = 1e-5
NEWTON = 3
NORM_STEPS = 6 + 3 * NEWTON
SCALE = 1.0 / DH ** 0.5

DB = D // P
CH = 512
NC = L // CH
QB = CH // P
TB = L // P
HB = H // DB
NP = H // 2
PB = NP // DB
FB = FF // P
HF = FB // 2
UNITS = [(c, b) for c in range(NC) for b in range(NB)]

HG = 4
NG = H // HG
QT = HG * TB
SEG = H * CH // P
STEPS = NC * TB
A_STEPS = STEPS - 2
PARTS = 3
PR = 32
Q_RUNS = ((0, 0, 0), (1, 1), (2,))
K_RUNS = ((0, 1, 2), (0, 1), (0,))
LOADS = len(Q_RUNS) + len(K_RUNS)
ROWS = sum(len(r) for r in Q_RUNS) * DH
ROWS_M = ROWS + PARTS

VECS = (("cond_1024", 4), ("L0_xcond_bq", 2), ("L0_xcond_bkv", 4), ("L0_xcond_bss_q", 4), ("L0_xcond_bss_kv", 4),
        ("L1_xcond_aff1_b", 4), ("L1_xcond_aff2_b", 4), ("L1_xcond_ln1_g", 2), ("L1_xcond_ln1_b", 2),
        ("L1_xcond_ln2_g", 2), ("L1_xcond_ln2_b", 2), ("L1_xcond_sa_qb", 2), ("L1_xcond_sa_kb", 2),
        ("L1_xcond_ca_qb", 2), ("L1_xcond_ca_kb", 2), ("L1_xcond_ffn_b1", 8))
VCOL = {}
for _name, _rows in VECS:
    VCOL[_name] = sum(r for n, r in VECS[:len(VCOL)])
NVEC = sum(r for _, r in VECS)
N_VECS0 = 5
NVEC0 = sum(r for _, r in VECS[:N_VECS0])
BROAD = ("L0_xcond_bv", "L0_xcond_bp", "L1_xcond_sa_vb", "L1_xcond_sa_ob", "L1_xcond_ca_vb", "L1_xcond_ca_ob",
         "L1_xcond_ffn_b2")
ADA = (("L0_xcond_Wss_q", "L0_xcond_bss_q"), ("L0_xcond_Wss_kv", "L0_xcond_bss_kv"),
       ("L1_xcond_aff1_w", "L1_xcond_aff1_b"), ("L1_xcond_aff2_w", "L1_xcond_aff2_b"))
ADA_Q, ADA_KV, ADA_1, ADA_2 = range(4)
SS_BANK, KEY_BANK, VALUE_BANK, CTX_BANK = (4, 1), (6, 3), (7, 2), 5


def build(nc, t, out):
    with ExitStack() as ctx:
        def sb(name, shape, dt=F32):
            return ctx.enter_context(nc.sbuf_tensor(name, shape, dt))

        def sem(name):
            return ctx.enter_context(nc.semaphore(name))

        def sems(name, n=NB):
            return [sem(f"{name}_{k}") for k in range(n)]

        q_parts = nc.dram_tensor("q_parts", [H, DH, PARTS, NB * L], BF16, kind="Internal").ap()
        k_parts = nc.dram_tensor("k_parts", [H, DH, PARTS, NB * L], BF16, kind="Internal").ap()
        att_sums = nc.dram_tensor("att_sums", [H, 2, DH, NB * L], F32, kind="Internal").ap()

        att_recip = nc.dram_tensor("att_recip", [H, NB * L], F32, kind="Internal").ap()

        region_words = 30720
        region_at = -(-nc.sbuf_base // 32) * 32
        sb("region", [P, region_words + 8])

        def at(name, word, shape, dt=F32):
            return nc.alloc_sbuf_tensor_at(name, [P] + list(shape), dt, offset=region_at + 4 * word)

        def per_batch(name, word, shape, dt=F32):
            return [at(f"{name}{b}", word + 4096 * b, shape, dt) for b in range(NB)]

        xT = at("xT", 0, [2, NB, DB, CH], F32R)
        qT = per_batch("qT", 4096, [2, DB, CH], F32R)
        outT = per_batch("outT", 6144, [2, DB, CH], F32R)
        hidT = per_batch("hidT", 4096, [HF, 2, CH], F32R)
        parts = per_batch("parts", 4096, [4, PARTS, CH], BF16)
        w_kv0 = at("w_kv0", 4096, [DB, 2 * D])
        w_raw = at("w_raw", 8192, [8, DB, D])
        qa = at("qa", 0, [HG, L], BF16)
        ka = at("ka", 2048, [HG, L], BF16)
        qs = per_batch("qs", 4096, [HG, L], BF16)
        ks = per_batch("ks", 6144, [HG, L], BF16)
        kbd = at("kbd", 12288, [2, NB, DB, HB * LK], F32R)
        v_all = at("v_all", 12288, [NB * TB, H, DH])
        w_q0 = at("w_q0", 16384, [2, DB, D], F32R)
        w_p0 = at("w_p0", 17408, [2, DB, D], F32R)
        v_grp = at("v_grp", 16384, [NB, TB, HG, 2 * DH])
        attT = at("attT", 18432, [NB, DB, CH])
        vtx = at("vtx", 18432, [2, NB, D])
        stats_x = at("stats_x", 19456, [NB * TB, 6])
        recT = at("recT", 20480, [NB, DB, CH])
        q_full = at("q_full", 18432, [NB, 4, CH])
        w_sa = at("w_sa", 22528, [3, 2, DB, D], F32R)
        w_ada = at("w_ada", 25600, [4, DB, 2 * D])
        w_kv1 = at("w_kv1", 29696, [2, DB, D])
        w_1 = at("w_1", 22528, [2, DB, FF], F32R)
        w_2 = at("w_2", 26624, [2, FB, D], F32R)

        x_tok = sb("x_tok", [P, NB * TB, D])
        xh = sb("xh", [P, NB, QB, D])
        probs = sb("probs", [P, 2 * HG, CH])
        vbd = sb("vbd", [P, 2, NB, NP, 2 * DH])
        w_out = sb("w_out", [P, 3, 2, DB, D], F32R)
        tmp = sb("tmp", [P, 4, CH])
        bc = sb("bc", [P, len(BROAD), D])
        vec = sb("vec", [P, NVEC])
        silu = sb("silu", [P, 3, 4])
        ss = sb("ss", [P, 4, 4, NB])
        ada_a = sb("ada_a", [P, 4, DB, NB])
        ada_b = sb("ada_b", [P, 4, DB, NB])
        ident = sb("ident", [P, P])
        ident_h = sb("ident_h", [P, P], BF16)
        head_mask = sb("head_mask", [P, HB])
        half_mask = sb("half_mask", [P, 2])
        ones_bd = sb("ones_bd", [P, 2, DH])
        pick = sb("pick", [PARTS * PR, NP, 2, LK], BF16)
        ktx = sb("ktx", [P, 2, DB, NB, LK])
        stats = sb("stats", [P, NB, QB, 6])
        mean = sb("mean", [P, NB, QB])
        rstd = sb("rstd", [P, NB, QB])
        mean_x = sb("mean_x", [P, NB * TB])
        rstd_x = sb("rstd_x", [P, NB * TB])
        newton = sb("newton", [P, 4, NB * TB])
        negmax = sb("negmax", [P, NB, QB, H])
        max_rest = sb("max_rest", [P, NB, QB, H])
        max_parts = sb("max_parts", [P, NB, QB, PARTS * PR], BF16)
        maxT = sb("maxT", [PARTS * PR, NB, CH], BF16)
        negmax_g = sb("negmax_g", [P, QT])
        den_seg = sb("den_seg", [P, SEG])
        rec_seg = sb("rec_seg", [P, SEG])
        max_rest_g = sb("max_rest_g", [P, QT])
        max_parts_g = sb("max_parts_g", [P, PARTS, QT], BF16)
        maxT_g = sb("maxT_g", [PARTS * QT, P], BF16)
        sums = sb("sums", [P, NC, CH])

        def view(area, at, *shape):
            n = 1
            for k in shape:
                n *= k
            names = "abcde"[:len(shape)]
            sizes = dict(zip(names, shape))
            return area[:, at:at + n].rearrange(f"p ({' '.join(names)}) -> p {' '.join(names)}", **sizes)

        xf = view(xh[:].rearrange("p b i n -> p (b i n)"), 0, NB, DB, CH)
        xh_words = xh[:].rearrange("p b i n -> p (b i n)")
        w_1raw = view(xh_words, 0, DB, FF)
        w_2raw = view(xh_words, 0, FB, D)
        p_area = probs[:].rearrange("p a n -> p (a n)")
        ctx_tok = view(p_area, 0, D)
        ctx_hat = view(p_area, D, D)
        p_bf16 = p_area.bitcast(BF16)
        qa_first = view(p_bf16, 0, HG, L)
        ka_first = view(p_bf16, HG * L, HG, L)
        vrow = p_area[0:NVEC0, 2 * D:2 * D + P]
        vrow1 = p_area[0:NVEC - NVEC0, 3 * D:3 * D + P]
        ctxT = view(sums[:].rearrange("p a n -> p (a n)"), 0, 2, DB, NB, 2, LK)

        def token_rows(c, b, first=0, n=QB):
            at = c * QB + b * TB + first
            return x_tok[:, at:at + n, :]

        ps = ctx.enter_context(nc.psum_tensor("ps", [P, 8, CH], F32))

        def bank(b, k):
            return ps[:, 4 * (NB - 1 - b) + k, :]

        vec_in, x_in = sems("vec_in", 2), sem("x_in")
        ctx_in, bc_in = sem("ctx_in"), sem("bc_in")
        w_ada_in, w_kv_in = sems("w_ada_in", 2), sems("w_kv_in", 2)
        w_0_in, w_sa_in, w_mlp_in = sem("w_0_in"), sem("w_sa_in"), sem("w_mlp_in")
        w_0_split, w_split = sem("w_0_split"), sem("w_split")
        x_step = sem("x_step")
        consts_made, mask_step = sem("consts_made"), sem("mask_step")
        vec_full, vec_ready, silu_step, silu_exp, silu_ready = (
            sem("vec_full"), sem("vec_ready"), sem("silu_step"), sem("silu_exp"), sem("silu_ready"))
        ss_full, ss_step, ada_ready = sem("ss_full"), sem("ss_step"), sem("ada_ready")
        ctx_step, ctx_hat_ready, ctxT_full, ctxT_ready = (
            sem("ctx_step"), sem("ctx_hat_ready"), sem("ctxT_full"), sem("ctxT_ready"))
        ctx_k_full, ctx_v_full, ktx_ready, ktx_step, vtx_ready, vbd_ready, kbd_ready = (
            sem("ctx_k_full"), sem("ctx_v_full"), sem("ktx_ready"), sem("ktx_step"), sem("vtx_ready"),
            sem("vbd_ready"), sem("kbd_ready"))

        def phase(name, per_batch, common=()):
            return {w: sems(f"{name}_{w}") for w in per_batch} | {w: sem(f"{name}_{w}") for w in common}

        px = phase("x", ("xT_full", "xT_high", "xT_low", "q_full", "q_high", "q_low", "s_full", "max_done",
                         "maxT_full", "maxT_ready", "st_full", "exp_done", "pv_full", "outT_ready",
                         "o_full", "biased", "added", "normed"),
                   ("norm_step", "split_step", "out_step"))
        p2 = phase("qkv", ("normed", "xT_full", "xT_high", "xT_low", "qk_full", "qk_taken", "mid_ready",
                           "parts_ready", "parts_out", "v_full", "v_ready"), ("norm_step", "split_step"))
        p4 = phase("l1", ("att_in", "outT_ready", "so_full", "x1_in", "x2_ready", "hT_full",
                          "hT_high", "hT_low", "hid_full", "hid_taken", "hid_low", "y_full", "b2_added", "y_ready",
                          "y_out"), ("out_step", "hid_step", "hid_used"))

        stack_a = sems("stack_a", HG)
        stack_s, shift_in, v_grp_ready = sems("stack_s"), sems("shift_in"), sem("v_grp_ready")
        sa_s_full, sa_max_done, sa_split_step, sa_maxT_full, sa_maxT_ready = (
            sem("sa_s_full"), sem("sa_max_done"), sem("sa_split_step"), sem("sa_maxT_full"), sem("sa_maxT_ready"))
        sa_st_full, sa_exp_done, sa_pv_done = sem("sa_st_full"), sem("sa_exp_done"), sem("sa_pv_done")
        sums_taken, sums_out = sems("sums_taken", NC), sems("sums_out", NC)
        ones_rows = sem("ones_rows")
        den_in, rec_done, rec_out = sem("den_in"), sem("rec_done"), sem("rec_out")

        HALVES = NG * NB
        PARTS_OUT = 16 * 4 * NC

        def tile_plan(s):
            upto = [min(QT, (QT * k + A_STEPS // 2) // A_STEPS) if k else 0 for k in (s, s + 1)]
            return list(range(*upto))

        def score_bank(u):
            return 1 if u == STEPS * HG - 1 else u % 3

        block = ctx.enter_context(nc.Block())

        @block.sync
        def _(sp):
            def load_vectors(names, tile, first, done):
                for name, rows in names:
                    src = t[name]
                    src = (src.rearrange("b (k p) -> (b k) p", p=P) if name == "cond_1024"
                           else src.rearrange("(k p) -> k p", p=P))
                    r = VCOL[name] - first
                    sp.dma_start(tile[r:r + rows, :], src).then_inc(done, 16)

            def load_weight(dst, name, done):
                sp.dma_start(dst, t[name].rearrange("(k p) n -> p k n", p=P)).then_inc(done, 16)

            x_dram = t["x"].rearrange("b (n p) d -> p (b n) d", p=P)

            def load_x(c):
                for b in range(NB):
                    rows = slice(b * TB + c * QB, b * TB + (c + 1) * QB)
                    sp.dma_start(x_tok[:, rows], x_dram[:, rows]).then_inc(x_in, 16)

            sp.dma_start(ctx_tok, t["ctx_1024"].rearrange("b k d -> (b k) d")).then_inc(ctx_in, 16)
            load_vectors(VECS[:N_VECS0], vrow, 0, vec_in[0])
            for n in (ADA_Q, ADA_KV):
                load_weight(w_ada[:, n], ADA[n][0], w_ada_in[0])
            load_x(0)
            load_x(1)
            load_weight(w_kv0[:], "L0_xcond_Wkv", w_kv_in[0])
            load_weight(w_raw[:, 0], "L0_xcond_Wq", w_0_in)
            load_weight(w_raw[:, 1], "L0_xcond_Wp", w_0_in)
            for k, name in enumerate(("sa_qw", "sa_kw", "sa_vw", "sa_ow", "ca_qw", "ca_ow")):
                load_weight(w_raw[:, 2 + k], "L1_xcond_" + name, w_sa_in)
            load_vectors(VECS[N_VECS0:], vrow1, NVEC0, vec_in[1])
            for n in (ADA_1, ADA_2):
                load_weight(w_ada[:, n], ADA[n][0], w_ada_in[1])
            load_weight(w_kv1[:, 0], "L1_xcond_ca_kw", w_kv_in[1])
            load_weight(w_kv1[:, 1], "L1_xcond_ca_vw", w_kv_in[1])

            def store_parts(c, b):
                for u in range(4):
                    k, d = u // DB, u % DB
                    sp.wait_ge(p2["parts_ready"][b], c * 4 + u + 1)
                    to = (q_parts, k_parts)[k][d * HB:(d + 1) * HB, :, :, c * CH + b * L:(c + 1) * CH + b * L]
                    sp.dma_start(to.rearrange("h d t n -> (h d) t n"),
                                 parts[b][:, u]).then_inc(p2["parts_out"][b], 16)

            def load_rows(dst, src, head, runs, b, done):
                row = 0
                for run in runs:
                    n = len(run)
                    if n > 1 and run[0] == run[1]:
                        rows = src[ds(head, 1), :, run[0], b * L:(b + 1) * L].rearrange("o d n -> (o d) n")
                        rows = rows.unsqueeze(1).to_broadcast([DH, n, L])
                    else:
                        rows = src[ds(head, 1), :, run[0]:run[0] + n, b * L:(b + 1) * L].rearrange(
                            "o d t n -> (o d) t n")
                    sp.dma_start(dst[row:row + n * DH, :], rows).then_inc(done, 16)
                    row += n * DH

            def load_stack_a(g, b, j, q_to=qa, k_to=ka):
                load_rows(q_to[:, j, :], q_parts, g * HG + j, Q_RUNS, b, stack_a[j])
                load_rows(k_to[:, j, :], k_parts, g * HG + j, K_RUNS, b, stack_a[j])

            def copy_stack(n, b, q_from=qa, k_from=ka):
                for j in range(HG):
                    sp.wait_ge(stack_a[j], (n + 1) * 16 * LOADS)
                sp.dma_start(qs[b][0:ROWS], q_from[0:ROWS]).then_inc(stack_s[b], 16)
                sp.dma_start(ks[b][0:ROWS], k_from[0:ROWS]).then_inc(stack_s[b], 16)

            def load_shift(a, b):
                sp.wait_ge(sa_maxT_ready, a + 1)
                rows = qs[b][ROWS:ROWS_M].rearrange("r j (q n) -> r (j q) n", n=P)
                sp.dma_start(rows, maxT_g[:]).then_inc(shift_in[b], 16)

            for c, b in UNITS[:-1]:
                store_parts(c, b)
            sp.wait_ge(p2["parts_out"][0], PARTS_OUT)
            sp.wait_ge(px["pv_full"][NB - 1], NC * DB)
            for j in range(HG):
                load_stack_a(0, 0, j, qa_first, ka_first)
            store_parts(*UNITS[-1])
            copy_stack(0, 0, qa_first, ka_first)
            sp.wait_ge(p2["parts_out"][NB - 1], PARTS_OUT)
            for b in range(NB):
                sp.wait_ge(p2["v_full"][b], 2 * NC)
            for j in range(HG):
                load_stack_a(0, 1, j)
            load_shift(0, 0)
            copy_stack(1, 1)
            with sp.Fori(0, NG - 1) as g:
                for b in range(NB):
                    half = g * NB + b
                    sp.wait_ge(stack_s[1 - b], (g + 1 + b) * 16 * 2)
                    for j in range(HG):
                        if j < HG - 1:
                            sp.wait_ge(sa_s_full, (half + 1) * QT + TB * (j + 1))
                        else:
                            load_shift(half + 1, 1 - b)
                        load_stack_a(g + 1, b, j)
                    sp.wait_ge(sa_st_full, (half + 1) * STEPS * HG)
                    copy_stack(half + 2, b)
            load_shift(HALVES - 1, NB - 1)

            def load_sums(c, b):
                sp.wait_ge(p4["outT_ready"][b], c * DB)
                for d in range(DB):
                    tok = slice(c * CH + b * L, (c + 1) * CH + b * L)
                    sp.dma_start(attT[:, b, d, :],
                                 att_sums[d * HB:(d + 1) * HB, 0, :, tok]).then_inc(p4["att_in"][b], 16)
                    rec = att_recip[d * HB:(d + 1) * HB, tok].unsqueeze(1).to_broadcast([HB, DH, CH])
                    sp.dma_start(recT[:, b, d, :], rec).then_inc(p4["att_in"][b], 16)

            for c, b in UNITS:
                sp.wait_ge(rec_out, 16 * (b * NC + c + 1))
                load_sums(c, b)
            out_tok = out.rearrange("b (n p) d -> p (b n) d", p=P)
            for c, b in UNITS:
                sp.wait_ge(p4["y_ready"][b], (c + 1) * 2)
                at_row = c * QB + b * TB
                sp.dma_start(out_tok[:, at_row:at_row + QB, :], token_rows(c, b)).then_inc(p4["y_out"][b], 16)
            for b in range(NB):
                sp.wait_ge(p4["y_out"][b], 16 * NC)

        @block.gpsimd
        def _(pool):
            nc.gpsimd.memset(ident[:], 0.0).then_inc(mask_step, 1)
            pool.wait_ge(mask_step, 1)
            nc.gpsimd.affine_select(out=ident[:], in_=ident[:], compare_op=ALU.not_equal, fill=1.0, base=0,
                                    pattern=[[-1, P]], channel_multiplier=1).then_inc(consts_made, 1)
            nc.gpsimd.memset(max_parts[:], 0.0)
            nc.gpsimd.memset(head_mask[:], 1.0)
            nc.gpsimd.memset(half_mask[:], 1.0)
            nc.gpsimd.memset(ones_bd[:], 1.0)
            nc.gpsimd.memset(pick[:], 0.0).then_inc(mask_step, 1)
            pool.wait_ge(mask_step, 2)
            for tile, pat, width in ((head_mask, [[-DH, HB]], DH), (half_mask, [[-LK, 2]], LK),
                                     (ones_bd, [[-LK, 2], [0, DH]], LK)):
                nc.gpsimd.affine_select(out=tile[:], in_=tile[:], compare_op=ALU.is_ge, fill=0.0, base=0,
                                        pattern=pat, channel_multiplier=1)
            for part in range(PARTS):
                last = nc.gpsimd.affine_select(out=pick[:], in_=pick[:], compare_op=ALU.not_equal, fill=1.0,
                                               base=-part * PR, pattern=[[-2, NP], [-1, 2], [0, LK]],
                                               channel_multiplier=1)
                if part < PARTS - 1:
                    last.then_inc(mask_step, 1)
                    pool.wait_ge(mask_step, part + 3)
            last.then_inc(mask_step, 1)
            pool.wait_ge(mask_step, PARTS + 2)
            for tile, pat, width in ((head_mask, [[DH, HB]], DH), (half_mask, [[LK, 2]], LK),
                                     (ones_bd, [[LK, 2], [0, DH]], LK)):
                nc.gpsimd.affine_select(out=tile[:], in_=tile[:], compare_op=ALU.is_ge, fill=0.0, base=width - 1,
                                        pattern=pat, channel_multiplier=-1)
            nc.gpsimd.tensor_copy(ident_h[:], ident[:]).then_inc(consts_made, 1)
            names = {"L0_xcond_bv": t["L0_xcond_bkv"][D:2 * D]}
            for k, name in enumerate(BROAD):
                src = names.get(name, None)
                src = t[name] if src is None else src
                pool.dma_start(bc[:, k], src.partition_broadcast(P)).then_inc(bc_in, 16)

            def split(high, low, full, n):
                nc.gpsimd.tensor_copy(high, full).then_inc(w_split, 1)
                pool.wait_ge(w_split, 2 * n + 1)
                nc.gpsimd.tensor_tensor(low, full, high.bitcast(F32), ALU.subtract).then_inc(w_split, 1)

            pool.wait_ge(w_sa_in, 16 * 6)
            for k in range(6):
                dst = w_sa[:, k] if k < 3 else w_out[:, k - 3]
                split(dst[:, 0], dst[:, 1], w_raw[:, 2 + k], k)

            def low_rows(ph, high, low, n, b):
                for d in range(DB):
                    pool.wait_ge(ph[high][b], (n + 1) * 2 * DB - DB + d + 1)
                    nc.gpsimd.tensor_tensor(xT[:, 1, b, d, :], xf[:, b, d, :], xT[:, 0, b, d, :].bitcast(F32),
                                            ALU.subtract).then_inc(ph[low][b], 1)

            pool.wait_ge(bc_in, 16 * len(BROAD))
            with pool.Fori(0, NC) as c:
                for b in range(NB):
                    low_rows(px, "xT_high", "xT_low", c, b)
                    pool.wait_ge(px["normed"][b], c + 1)
                    rows = x_tok[:, ds(c * QB + b * TB, QB), :]
                    bias = bc[:, BROAD.index("L0_xcond_bp")].unsqueeze(1).to_broadcast([P, QB, D])
                    nc.gpsimd.tensor_tensor(rows, rows, bias, ALU.add).then_inc(px["biased"][b], 1)

            low_rows(p2, "xT_high", "xT_low", *UNITS[0])
            for i, (c, b) in enumerate(UNITS):
                for u in range(4):
                    if u == 3 and i + 1 < len(UNITS):
                        low_rows(p2, "xT_high", "xT_low", *UNITS[i + 1])
                    pool.wait_ge(p2["mid_ready"][b], c * 4 + u + 1)
                    nc.gpsimd.tensor_tensor(parts[b][:, u, 2, :], q_full[:, b, u, :], parts[b][:, u, 1, :],
                                            ALU.subtract).then_inc(p2["parts_ready"][b], 1)

            for b in range(NB):
                pool.wait_ge(p2["parts_ready"][b], 4 * NC)
            for b in range(NB):
                pool.wait_ge(p2["parts_out"][b], PARTS_OUT)
            for b in range(NB):
                nc.gpsimd.memset(ks[b][ROWS:ROWS_M], 1.0).then_inc(ones_rows, 1)
            pool.wait_ge(ones_rows, NB)
            nc.gpsimd.memset(v_grp[:, :, :, :, DH:2 * DH], 1.0).then_inc(ones_rows, 1)

            def take_values(g, b):
                src = v_all[:, b * TB:(b + 1) * TB, ds(g * HG, HG), :]
                nc.gpsimd.tensor_copy(v_grp[:, b, :, :, 0:DH], src).then_inc(v_grp_ready, 1)

            def store_sums(g, b, ch):
                pool.wait_ge(sums_taken[ch], g * NB + b + 1)
                dst = att_sums[ds(g * HG, HG), :, :, b * L + ch * CH:b * L + (ch + 1) * CH]
                pool.dma_start(dst.rearrange("h k d n -> (h k d) n"), sums[:, ch]).then_inc(sums_out[ch], 16)

            def invert_sums(c, b):
                at = b * NC + c
                pool.wait_ge(sums_out[c], (HALVES - NB + b + 1) * 16)
                pool.wait_ge(rec_out, at * 16)
                tok = slice(b * L + c * CH, b * L + (c + 1) * CH)
                pool.dma_start(den_seg[:], att_sums[:, 1, 0, tok].rearrange("h (s n) -> h s n", n=SEG)).then_inc(
                    den_in, 16)
                pool.wait_ge(rec_done, at + 1)
                pool.dma_start(att_recip[:, tok].rearrange("h (s n) -> h s n", n=SEG), rec_seg[:]).then_inc(
                    rec_out, 16)

            pool.wait_ge(ones_rows, NB + 1)
            for b in range(NB):
                pool.wait_ge(p2["v_ready"][b], 2 * NC)
                take_values(0, b)
            for b in range(NB):
                pool.wait_ge(p2["xT_low"][b], NC * DB)
                pool.wait_ge(p2["v_full"][b], NC * 2)
            for k, (raw, dst, name) in enumerate(((w_1raw, w_1, "ffn_w1"), (w_2raw, w_2, "ffn_w2"))):
                pool.dma_start(raw, t["L1_xcond_" + name].rearrange("(k p) n -> p k n", p=P)).then_inc(w_mlp_in, 16)
                pool.wait_ge(w_mlp_in, 16 * (k + 1))
                split(dst[:, 0], dst[:, 1], raw, 6 + k)
                pool.wait_ge(w_split, 2 * (6 + k + 1))
            with pool.Fori(0, NG - 1) as g:
                for b in range(NB):
                    for ch in range(NC):
                        store_sums(g, b, ch)
                    pool.wait_ge(sa_pv_done, (g * NB + b + 1) * STEPS)
                    take_values(g + 1, b)
            def add_bias(name, c, b, done):
                bias = bc[:, BROAD.index(name)].unsqueeze(1).to_broadcast([P, QB, D])
                nc.gpsimd.tensor_tensor(token_rows(c, b), token_rows(c, b), bias, ALU.add).then_inc(done[b], 1)

            def bias_cross(c, b):
                pool.wait_ge(px["xT_full"][b], (c + NC + 1) * DB)
                add_bias("L1_xcond_ca_ob", c, b, px["biased"])

            def low_cross(c, b):
                low_rows(px, "xT_high", "xT_low", c + NC, b)

            for c, b in UNITS:
                add_bias("L1_xcond_sa_ob", c, b, p4["x1_in"])
            for b in range(NB):
                for c in range(NC):
                    store_sums(NG - 1, b, c)
                    invert_sums(c, b)
                    if (c, b) == (1, 0):
                        low_cross(0, 0)
                    elif (c, b) == (0, 1):
                        bias_cross(0, 0)
            for i, (c, b) in enumerate(UNITS):
                if i + 1 < len(UNITS):
                    low_cross(*UNITS[i + 1])
                    bias_cross(*UNITS[i + 1])
                low_rows(p4, "hT_high", "hT_low", c, b)
                pool.wait_ge(px["normed"][b], c + NC + 1)
                add_bias("L1_xcond_ffn_b2", c, b, p4["b2_added"])

        @block.tensor
        def _(pe):
            def transpose_rows(rows, b, k0, done):
                for d in range(DB):
                    for i in range(QB):
                        last = nc.tensor.transpose(bank(b, k0 + d)[:, i * P:(i + 1) * P],
                                                   rows[:, i, d * P:(d + 1) * P], ident[:])
                    last.then_inc(done[b], 1)

            PRODUCTS = ((0, 0), (1, 0), (0, 1))

            def products(out, left, right, n, low=None):
                for k, (l, r) in enumerate(PRODUCTS):
                    if r == 1 and low is not None:
                        pe.wait_ge(*low)
                    for d in range(n):
                        last = nc.tensor.matmul(out, left(l, d), right(r, d), start=(k == 0 and d == 0),
                                                stop=(k == len(PRODUCTS) - 1 and d == n - 1))
                return last

            def project(w, b, k0, done, low):
                for o in range(DB):
                    products(bank(b, k0 + o), lambda l, d: w[:, l, d, o * P:(o + 1) * P],
                             lambda r, d: xT[:, r, b, d, :], DB, low if o == 0 else None).then_inc(done[b], 1)

            def project_rows(src, w, b, k0, done):
                for i in range(QB):
                    last = products(bank(b, k0 + i // 2)[:, (i % 2) * D:(i % 2 + 1) * D],
                                    lambda l, d: src[:, l, d, i * P:(i + 1) * P], lambda r, d: w[:, r, d, :], DB)
                    if i % 2:
                        last.then_inc(done[b], 1)

            def scores(ph, c, b, blocks=range(QB)):
                pe.wait_ge(ph["q_high"][b], (c + 1) * DB)
                pe.wait_ge(ph["q_low"][b], (c + 1) * DB)
                for i in blocks:
                    for d in range(DB):
                        u = i * DB + d
                        if u >= 2:
                            pe.wait_ge(ph["max_done"][b], c * QB * DB + u - 1)
                        products(bank(b, u % 2), lambda l, _: qT[b][:, l, d, i * P:(i + 1) * P],
                                 lambda r, _: kbd[:, r, b, d, :], 1).then_inc(ph["s_full"][b], 1)

            def shift(ph, n, b):
                pe.wait_ge(ph["split_step"], (n * NB + b + 1) * 4)
                turned = bank(b, 2)[0:PARTS * PR, 0:CH // 2].bitcast(BF16)
                for i in range(QB):
                    last = nc.tensor.transpose(turned[:, i * P:(i + 1) * P], max_parts[:, b, i, :], ident_h[:])
                last.then_inc(ph["maxT_full"][b], 1)

            def attend(ph, a, c, b, d):
                pe.wait_ge(ph["maxT_ready"][b], c + 1)
                for k in range(PB):
                    p = d * PB + k
                    if p >= 2:
                        pe.wait_ge(ph["exp_done"][b], c * NP + p - 1)
                    for l, r in PRODUCTS:
                        nc.tensor.matmul(bank(b, p % 2), kbd[:, l, b, d, k * P:(k + 1) * P], qT[b][:, r, d, :],
                                         start=(l == 0 and r == 0), stop=False)
                    nc.tensor.matmul(bank(b, p % 2), pick[:, p].rearrange("r e k -> r (e k)"), maxT[:, b, :],
                                     start=False, stop=True).then_inc(ph["st_full"][b], 1)
                pe.wait_ge(ph["exp_done"][b], c * NP + (d + 1) * PB)
                if d > 0:
                    pe.wait_ge(ph["out_step"], ((c * NB + b) * DB + d) * 3 - 1)
                for k in range(PB):
                    nc.tensor.matmul(bank(b, 2)[32 * k:32 * k + 32, :], vbd[:, a, b, d * PB + k, :],
                                     probs[:, d * PB + k, :], start=True, stop=True)
                for k in range(PB):
                    last = nc.tensor.matmul(bank(b, 3)[32 * k:32 * k + 32, :],
                                            ones_bd[:].rearrange("p e k -> p (e k)"),
                                            probs[:, d * PB + k, :], start=True, stop=True)
                last.then_inc(ph["pv_full"][b], 1)

            def prepare_norms(a):
                cond = vec[:, 0:4].rearrange("p (b k) -> p k b", b=NB)
                silu_c = silu[:, 2, :].rearrange("p (b k) -> p k b", b=NB)
                pe.wait_ge(w_ada_in[a], 16 * 2)
                for n in (ADA_Q, ADA_KV) if a == 0 else (ADA_1, ADA_2):
                    for o in range(4):
                        for d in range(DB):
                            last = nc.tensor.matmul(ps[:, SS_BANK[a], (n * 4 + o) * NB:(n * 4 + o + 1) * NB],
                                                    w_ada[:, n, d, o * P:(o + 1) * P],
                                                    (silu_c if a == 0 else cond)[:, d, :],
                                                    start=(d == 0), stop=(d == DB - 1))
                last.then_inc(ss_full, 1)

            def prepare_context(a):
                key_w = w_kv0[:, :, 0:D] if a == 0 else w_kv1[:, 0]
                val_w = w_kv0[:, :, D:2 * D] if a == 0 else w_kv1[:, 1]
                pe.wait_ge(w_kv_in[a], 16 * (a + 1))
                pe.wait_ge(ctxT_ready, 1 + (a == 0))
                for o in range(DB):
                    for b in range(NB):
                        for d in range(DB):
                            last = nc.tensor.matmul(ps[:, KEY_BANK[a], (o * NB + b) * LK:(o * NB + b + 1) * LK],
                                                    key_w[:, d, o * P:(o + 1) * P], ctxT[:, a, d, b, 0, :],
                                                    start=(d == 0), stop=(d == DB - 1))
                last.then_inc(ctx_k_full, 1)
                for b in range(NB):
                    for d in range(DB):
                        last = nc.tensor.matmul(ps[:, VALUE_BANK[a], b * D:(b + 1) * D],
                                                ctxT[:, a, d, b].rearrange("p e k -> p (e k)"), val_w[:, d, :],
                                                start=(d == 0), stop=(d == DB - 1))
                last.then_inc(ctx_v_full, 1)

            def turn_vectors(k, tile, first, n):
                pe.wait_ge(vec_in[k], 16 * (N_VECS0 if k == 0 else len(VECS) - N_VECS0))
                nc.tensor.transpose(ps[:, 0, first:first + n], tile, ident[0:n, 0:n]).then_inc(vec_full, 1)

            pe.wait_ge(consts_made, 1)
            turn_vectors(0, vrow, 0, NVEC0)
            pe.wait_ge(ctx_hat_ready, 1)
            for k, src in enumerate((ctx_hat, ctx_tok)):
                for d in range(DB):
                    last = nc.tensor.transpose(ps[:, CTX_BANK, (k * DB + d) * P:(k * DB + d + 1) * P],
                                               src[:, d * P:(d + 1) * P], ident[:])
            last.then_inc(ctxT_full, 1)
            pe.wait_ge(silu_ready, 1)
            prepare_norms(0)
            prepare_context(0)

            def turn_first(c, b):
                pe.wait_ge(px["normed"][b], c + 1)
                transpose_rows(xh[:, b], b, 0, px["xT_full"])

            def query_first(c, b):
                pe.wait_ge(px["xT_high"][b], c * 2 * DB + DB)
                pe.wait_ge(px["added"][b], c * 2)
                project(w_q0, b, 2, px["q_full"], (px["xT_low"][b], (c + 1) * DB))

            def out_first(c, b):
                pe.wait_ge(px["outT_ready"][b], (c + 1) * DB)
                project_rows(outT[b], w_p0, b, 2, px["o_full"])

            def turn_second(c, b):
                pe.wait_ge(p2["normed"][b], c + 1)
                pe.wait_ge(p2["qk_taken"][b], c * 4)
                transpose_rows(xh[:, b], b, 0, p2["xT_full"])

            def qk_second(c, b):
                pe.wait_ge(px["added"][b], 2 * NC)
                pe.wait_ge(p2["xT_high"][b], c * 2 * DB + DB)
                pe.wait_ge(p2["v_ready"][b], c * 2)
                project(w_sa[:, 0], b, 2, p2["qk_full"], (p2["xT_low"][b], (c + 1) * DB))
                project(w_sa[:, 1], b, 0, p2["qk_full"], None)

            def values_second(c, b):
                pe.wait_ge(p2["qk_taken"][b], c * 4 + 2)
                project_rows(xT[:, :, b], w_sa[:, 2], b, 2, p2["v_full"])

            pe.wait_ge(ss_step, 2)
            pe.wait_ge(ctxT_ready, 2)
            turn_first(0, 0)
            pe.wait_ge(vec_ready, 1)
            turn_vectors(1, vrow1, NVEC0, NVEC - NVEC0)
            prepare_norms(1)
            pe.wait_ge(vtx_ready, 1)
            pe.wait_ge(w_0_split, 4)
            query_first(0, 0)
            pe.wait_ge(kbd_ready, 1)
            scores(px, 0, 0)
            prepare_context(1)
            pe.wait_ge(consts_made, 2)
            pe.wait_ge(vec_ready, 2)
            pe.wait_ge(ss_step, 3)
            for i, (c, b) in enumerate(UNITS):
                final = i + 1 == len(UNITS)
                if final:
                    pe.wait_ge(w_split, 2 * 3)
                    turn_second(*UNITS[0])
                else:
                    turn_first(*UNITS[i + 1])
                shift(px, c, b)
                if i == 0:
                    pe.wait_ge(vbd_ready, 1)
                attend(px, 0, c, b, 0)
                if i > 0:
                    out_first(*UNITS[i - 1])
                if i == 0:
                    pe.wait_ge(ktx_ready, 2)
                    pe.wait_ge(vtx_ready, 2)
                if final:
                    qk_second(*UNITS[0])
                else:
                    query_first(*UNITS[i + 1])
                attend(px, 0, c, b, 1)
                if not final:
                    scores(px, *UNITS[i + 1])
            turn_second(*UNITS[1])
            values_second(*UNITS[0])
            out_first(*UNITS[-1])

            for i, (c, b) in enumerate(UNITS[1:]):
                qk_second(c, b)
                if i + 2 < len(UNITS):
                    turn_second(*UNITS[i + 2])
                values_second(c, b)

            pe.wait_ge(p2["qk_taken"][0], 4 * NC)
            pe.wait_ge(p2["v_ready"][0], 2 * NC)

            def score_tile(a, n, q_at=qa, k_at=ka):
                j, q = n // TB, n % TB
                if q == 0:
                    pe.wait_ge(stack_a[j], (a + 1) * 16 * LOADS)
                if n == 0:
                    pe.wait_ge(sa_max_done, a * QT)
                    pe.wait_ge(sa_maxT_ready, a)
                elif n >= 2:
                    pe.wait_ge(sa_max_done, a * QT + n - 1)
                for k in range(2):
                    last = nc.tensor.matmul(ps[:, 4 + 2 * (n % 2) + k, :], q_at[0:ROWS, j, q * P:(q + 1) * P],
                                            k_at[0:ROWS, j, k * CH:(k + 1) * CH], start=True, stop=True)
                last.then_inc(sa_s_full, 1)

            def turn_maxima(a):
                pe.wait_ge(sa_split_step, (a + 1) * 4)
                nc.tensor.transpose(ps[0:PARTS * QT, 4, 0:P // 2].bitcast(BF16),
                                    max_parts_g[:].rearrange("p a n -> p (a n)"), ident_h[:]).then_inc(sa_maxT_full, 1)

            def weigh(half, b, s):
                ch, kb = s // TB, s % TB
                pe.wait_ge(sa_exp_done, half * STEPS * HG + (s + 1) * HG)
                if s == 0:
                    pe.wait_ge(v_grp_ready, half + 1)
                    pe.wait_ge(sums_taken[1], half)
                elif kb == 0:
                    pe.wait_ge(sums_taken[0], half + 1)
                for j in range(HG):
                    last = nc.tensor.matmul(ps[32 * j:32 * j + 32, 3, :], v_grp[:, b, kb, j, :],
                                            probs[:, (s % 2) * HG + j, :], start=(kb == 0), stop=(kb == TB - 1))
                last.then_inc(sa_pv_done, 1)

            def scores_step(g, b, s, more):
                half = g * NB + b
                ch, kb = s // TB, s % TB
                tiles = tile_plan(s) if more else []
                for j in range(HG):
                    u = s * HG + j
                    if u >= 3:
                        before = 2 if u == STEPS * HG - 1 else 3
                        pe.wait_ge(sa_exp_done, half * STEPS * HG + u - before + 1)
                    nc.tensor.matmul(ps[:, score_bank(u), :], ks[b][0:ROWS_M, j, kb * P:(kb + 1) * P],
                                     qs[b][0:ROWS_M, j, ch * CH:(ch + 1) * CH],
                                     start=True, stop=True).then_inc(sa_st_full, 1)
                    if j == 0 and s == 0:
                        pe.wait_ge(sa_exp_done, half * STEPS * HG)
                    if j == 0 and len(tiles) > 0:
                        score_tile(half + 1, tiles[0])
                    elif j == HG - 1 and len(tiles) > 1:
                        score_tile(half + 1, tiles[1])

            def begin_group(g, b, more, first=False):
                half = g * NB + b
                pe.wait_ge(stack_s[b], (g + 1) * 16 * 2)
                pe.wait_ge(shift_in[b], (g + 1) * 16)
                if not first:
                    pe.wait_ge(sa_exp_done, half * STEPS * HG - 3)
                scores_step(g, b, 0, more)

            def attend_group(g, b, more, following, beside=None):
                half = g * NB + b
                for s in range(1, STEPS):
                    scores_step(g, b, s, more)
                    if s == A_STEPS and more:
                        turn_maxima(half + 1)
                    weigh(half, b, s - 1)
                    if more:
                        for n in tile_plan(s)[2:]:
                            score_tile(half + 1, n)
                    if beside is not None:
                        beside(s)
                if following is not None:
                    begin_group(*following)
                weigh(half, b, STEPS - 1)

            for n in range(QT):
                score_tile(0, n, qa_first, ka_first)
            turn_maxima(0)
            pe.wait_ge(ones_rows, NB + 1)
            pe.wait_ge(p2["qk_taken"][NB - 1], 4 * NC)
            pe.wait_ge(p2["v_ready"][NB - 1], 2 * NC)
            begin_group(0, 0, True, True)
            with pe.Fori(0, NG - 1) as g:
                attend_group(g, 0, True, (g, 1, True))
                attend_group(g, 1, True, (g + 1, 0, True))

            def out_self(c, b):
                pe.wait_ge(p4["outT_ready"][b], (c + 1) * DB)
                pe.wait_ge(p4["y_ready"][b], c * 2)
                project_rows(outT[b], w_out[:, 0], b, 2, p4["so_full"])

            def turn_cross(c, b):
                pe.wait_ge(p4["x2_ready"][b], (c + 1) * 2)
                pe.wait_ge(p4["hid_taken"][b], c * FB)
                transpose_rows(token_rows(c, b), b, 0, px["xT_full"])

            def query_cross(c, b):
                n = c + NC
                pe.wait_ge(px["xT_high"][b], n * 2 * DB + DB)
                project(w_out[:, 1], b, 2, px["q_full"], (px["xT_low"][b], (n + 1) * DB))

            def out_cross(c, b):
                pe.wait_ge(px["outT_ready"][b], (c + NC + 1) * DB)
                project_rows(outT[b], w_out[:, 2], b, 2, px["o_full"])

            def hidden(c, b, part):
                for f in range(part * HF, (part + 1) * HF):
                    if f >= 2:
                        pe.wait_ge(p4["hid_taken"][b], c * FB + f - 1)
                    products(bank(b, f % 2), lambda l, d: w_1[:, l, d, f * P:(f + 1) * P],
                             lambda r, d: xT[:, r, b, d, :], DB,
                             (p4["hT_low"][b], (c + 1) * DB) if f == 0 else None).then_inc(p4["hid_full"][b], 1)

            def mlp_out(c, b, part):
                for i in range(QB):
                    for f in range(part * HF, (part + 1) * HF):
                        if i == 0:
                            pe.wait_ge(p4["hid_low"][b], c * FB + f + 1)
                        for k, (l, r) in enumerate(PRODUCTS):
                            last = nc.tensor.matmul(bank(b, 2 + i // 2)[:, (i % 2) * D:(i % 2 + 1) * D],
                                                    hidT[b][:, f % HF, l, i * P:(i + 1) * P], w_2[:, r, f, :],
                                                    start=(f == 0 and k == 0 and i % 2 == 0),
                                                    stop=(f == FB - 1 and k == len(PRODUCTS) - 1 and i % 2 == 1))
                    if part == 0:
                        if i == QB - 1:
                            last.then_inc(p4["hid_used"], 1)
                    elif i % 2:
                        last.then_inc(p4["y_full"][b], 1)

            def start_last(s):
                if s == 3:
                    pe.wait_ge(sa_max_done, HALVES * QT)
                    pe.wait_ge(sa_maxT_ready, HALVES)
                    out_self(0, 0)
                elif s == 5:
                    turn_cross(0, 0)
                elif s == 8:
                    query_cross(0, 0)
                elif s >= STEPS - QB:
                    pe.wait_ge(kbd_ready, 2)
                    scores(px, NC, 0, (s - (STEPS - QB),))

            attend_group(NG - 1, 0, True, (NG - 1, 1, False))
            attend_group(NG - 1, 1, False, None, start_last)
            pe.wait_ge(vbd_ready, 2)
            for i, (c, b) in enumerate(UNITS):
                after = UNITS[i + 1] if i + 1 < len(UNITS) else None
                shift(px, c + NC, b)
                for d in range(DB):
                    attend(px, 1, c + NC, b, d)
                if i > 0:
                    mlp_out(*UNITS[i - 1], 1)
                else:
                    pe.wait_ge(sa_exp_done, HALVES * STEPS * HG)
                    for ch in range(NC):
                        pe.wait_ge(sums_taken[ch], HALVES)
                out_cross(c, b)
                if after:
                    out_self(*after)
                    turn_cross(*after)
                    query_cross(*after)
                pe.wait_ge(px["normed"][b], c + NC + 1)
                transpose_rows(xh[:, b], b, 2, p4["hT_full"])
                if after:
                    scores(px, after[0] + NC, after[1])
                pe.wait_ge(w_split, 2 * 8)
                pe.wait_ge(p4["hT_high"][b], c * 2 * DB + DB)
                hidden(c, b, 0)
                mlp_out(c, b, 0)
                hidden(c, b, 1)
            mlp_out(*UNITS[-1], 1)

        @block.vector
        def _(dve):
            def aggregate(st, m, y, step, at):
                n = y.shape[1]
                v, w, a, q = (newton[:, k, 0:n] for k in range(4))
                dve.wait_ge(step, at)
                nc.vector.tensor_tensor(w, st[:, :, 1], st[:, :, 4], ALU.add)
                nc.vector.tensor_tensor(a, st[:, :, 1], st[:, :, 4], ALU.subtract)
                nc.vector.tensor_tensor(v, st[:, :, 2], st[:, :, 5], ALU.add).then_inc(step, 1)
                dve.wait_ge(step, at + 1)
                nc.vector.tensor_scalar(m, w, 0.5, None, ALU.mult)
                nc.vector.tensor_tensor(q, a, a, ALU.mult).then_inc(step, 1)
                dve.wait_ge(step, at + 2)
                nc.vector.scalar_tensor_tensor(out=a, in0=q, scalar=D / 4, in1=v, op0=ALU.mult,
                                               op1=ALU.add).then_inc(step, 1)
                dve.wait_ge(step, at + 3)
                nc.vector.tensor_scalar(v, a, 1.0 / D, EPS, ALU.mult, ALU.add)
                nc.vector.tensor_scalar(w, a, -0.5 / D, -0.5 * EPS, ALU.mult, ALU.add).then_inc(step, 1)
                dve.wait_ge(step, at + 4)
                nc.vector.tensor_scalar(y.bitcast(I32), v.bitcast(I32), -0.5, float(0x5f3759df), ALU.mult,
                                        ALU.add).then_inc(step, 1)
                for k in range(NEWTON):
                    dve.wait_ge(step, at + 5 + 3 * k)
                    nc.vector.tensor_tensor(a, y, w, ALU.mult).then_inc(step, 1)
                    dve.wait_ge(step, at + 6 + 3 * k)
                    nc.vector.tensor_tensor(a, a, y, ALU.mult).then_inc(step, 1)
                    dve.wait_ge(step, at + 7 + 3 * k)
                    nc.vector.scalar_tensor_tensor(out=y, in0=a, scalar=1.5, in1=y, op0=ALU.add,
                                                   op1=ALU.mult).then_inc(step, 1)
                dve.wait_ge(step, at + 5 + 3 * NEWTON)

            def norm_rows(ph, src, n, b):
                for i in range(QB):
                    last = nc.vector.bn_stats(stats[:, b, i, :], src[:, i, :])
                last.then_inc(ph["norm_step"], 1)
                steps = (n % NC * NB + b) * NORM_STEPS
                aggregate(stats[:, b], mean[:, b, :], rstd[:, b, :], ph["norm_step"], steps + 1)
                for i in range(QB):
                    last = nc.vector.tensor_scalar(xh[:, b, i, :], src[:, i, :], mean[:, b, i:i + 1],
                                                   rstd[:, b, i:i + 1], ALU.subtract, ALU.mult)
                last.then_inc(ph["normed"][b], 1)

            def maxima(ph, c, b):
                for i in range(QB):
                    for d in range(DB):
                        u = i * DB + d
                        dve.wait_ge(ph["s_full"][b], c * QB * DB + u + 1)
                        last = nc.vector.tensor_reduce(negmax[:, b, i, d * HB:(d + 1) * HB],
                                                       bank(b, u % 2).rearrange("p (h k) -> p h k", k=LK),
                                                       AX.X, ALU.max, negate=True)
                        last.then_inc(ph["max_done"][b], 1)
                dve.wait_ge(ph["max_done"][b], (c + 1) * QB * DB)
                high, mid, low = (max_parts[:, b, :, k * PR:k * PR + H] for k in range(PARTS))
                at = (c * NB + b) * 4
                nc.vector.tensor_copy(high, negmax[:, b]).then_inc(ph["split_step"], 1)
                dve.wait_ge(ph["split_step"], at + 1)
                nc.vector.tensor_tensor(max_rest[:, b], negmax[:, b], high, ALU.subtract).then_inc(ph["split_step"], 1)
                dve.wait_ge(ph["split_step"], at + 2)
                nc.vector.tensor_copy(mid, max_rest[:, b]).then_inc(ph["split_step"], 1)
                dve.wait_ge(ph["split_step"], at + 3)
                nc.vector.tensor_tensor(low, max_rest[:, b], mid, ALU.subtract).then_inc(ph["split_step"], 1)

            def split_out(ph, u, b, d, at):
                dve.wait_ge(ph["out_step"], at)
                nc.vector.tensor_copy(outT[b][:, 0, d, :], u).then_inc(ph["out_step"], 1)
                dve.wait_ge(ph["out_step"], at + 1)
                nc.vector.tensor_tensor(outT[b][:, 1, d, :], u, outT[b][:, 0, d, :].bitcast(F32),
                                        ALU.subtract).then_inc(ph["outT_ready"][b], 1)

            def normalise(n, b, d):
                r, u = tmp[:, b, :], tmp[:, 2 + b, :]
                step = ((n * NB + b) * DB + d) * 3
                dve.wait_ge(px["pv_full"][b], n * DB + d + 1)
                nc.vector.reciprocal(r, bank(b, 3)).then_inc(px["out_step"], 1)
                dve.wait_ge(px["out_step"], step + 1)
                nc.vector.tensor_tensor(u, bank(b, 2), r, ALU.mult).then_inc(px["out_step"], 1)
                split_out(px, u, b, d, step + 2)

            def low_queries(ph, n, b, name):
                for d in range(DB):
                    dve.wait_ge(ph["q_high"][b], n * DB + d + 1)
                    nc.vector.scalar_tensor_tensor(out=qT[b][:, 1, d, :], in0=bank(b, 2 + d),
                                                   scalar=vec[:, VCOL[name] + d:VCOL[name] + d + 1],
                                                   in1=qT[b][:, 0, d, :].bitcast(F32), op0=ALU.add,
                                                   op1=ALU.subtract).then_inc(ph["q_low"][b], 1)

            def add_rows(full, done, dst, n, b, k0):
                for k in range(2):
                    dve.wait_ge(full[b], n * 2 + k + 1)
                    nc.vector.tensor_tensor(dst(k), bank(b, k0 + k).rearrange("p (i n) -> p i n", i=2), dst(k),
                                            ALU.add).then_inc(done[b], 1)

            def scale_first(c, b):
                dve.wait_ge(px["xT_low"][b], c * DB)
                for i in range(QB):
                    n = b * TB + c * QB + i
                    last = nc.vector.tensor_scalar(xh[:, b, i, :], x_tok[:, n, :], mean_x[:, n:n + 1],
                                                   rstd_x[:, n:n + 1], ALU.subtract, ALU.mult)
                last.then_inc(px["normed"][b], 1)

            dve.wait_ge(ctx_in, 16)
            nc.vector.bn_stats(stats[:, 0, 0, :], ctx_tok).then_inc(ctx_step, 1)
            aggregate(stats[:, 0, 0:1], mean[:, 0, 0:1], rstd[:, 0, 0:1], ctx_step, 1)
            nc.vector.tensor_scalar(ctx_hat, ctx_tok, mean[:, 0, 0:1], rstd[:, 0, 0:1], ALU.subtract,
                                    ALU.mult).then_inc(ctx_hat_ready, 1)
            dve.wait_ge(silu_exp, 1)
            nc.vector.tensor_scalar(silu[:, 1], silu[:, 0], 1.0, None, ALU.add).then_inc(silu_step, 1)
            dve.wait_ge(silu_step, 1)
            nc.vector.reciprocal(silu[:, 0], silu[:, 1]).then_inc(silu_step, 1)
            dve.wait_ge(silu_step, 2)
            nc.vector.tensor_tensor(silu[:, 2], vec[:, 0:4], silu[:, 0], ALU.mult).then_inc(silu_ready, 1)
            def prepare(a):
                sets = (ADA_Q, ADA_KV) if a == 0 else (ADA_1, ADA_2)
                dve.wait_ge(ss_full, a + 1)
                if a == 1:
                    dve.wait_ge(vec_ready, 2)
                for n in sets:
                    bias = ADA[n][1]
                    cols = vec[:, VCOL[bias]:VCOL[bias] + 4].unsqueeze(2).to_broadcast([P, 4, NB])
                    last = nc.vector.tensor_tensor(ss[:, n], ps[:, SS_BANK[a], n * 4 * NB:(n + 1) * 4 * NB].rearrange(
                        "p (o b) -> p o b", b=NB), cols, ALU.add)
                last.then_inc(ss_step, 1)
                dve.wait_ge(ss_step, 2 * a + 1)
                if a == 0:
                    for n in sets:
                        nc.vector.tensor_scalar(ada_a[:, n], ss[:, n, 0:DB, :], 1.0, None, ALU.add)
                        last = nc.vector.tensor_copy(ada_b[:, n], ss[:, n, DB:2 * DB, :])
                    last.then_inc(ss_step, 1)
                    dve.wait_ge(ss_step, 2)
                else:
                    for n, g, beta in ((ADA_1, "L1_xcond_ln1_g", "L1_xcond_ln1_b"),
                                       (ADA_2, "L1_xcond_ln2_g", "L1_xcond_ln2_b")):
                        gain = vec[:, VCOL[g]:VCOL[g] + DB].unsqueeze(2).to_broadcast([P, DB, NB])
                        shift = vec[:, VCOL[beta]:VCOL[beta] + DB].unsqueeze(2).to_broadcast([P, DB, NB])
                        nc.vector.tensor_tensor(ada_a[:, n], ss[:, n, 0:DB, :], gain, ALU.mult)
                        last = nc.vector.tensor_tensor(ada_b[:, n], ss[:, n, 0:DB, :], shift, ALU.mult)
                    last.then_inc(ss_step, 1)
                    dve.wait_ge(ss_step, 4)
                    for n in sets:
                        last = nc.vector.tensor_tensor(ada_b[:, n], ada_b[:, n], ss[:, n, DB:2 * DB, :], ALU.add)
                    last.then_inc(ada_ready, 1)
                    dve.wait_ge(ada_ready, 1)
                if a == 0:
                    dve.wait_ge(ctxT_full, 1)
                    for d in range(DB):
                        for b in range(NB):
                            src = ps[:, CTX_BANK, d * P + b * LK:d * P + (b + 1) * LK]
                            src = src.unsqueeze(1).to_broadcast([P, 2, LK])
                            last = nc.vector.tensor_scalar(ctxT[:, 0, d, b], src, ada_a[:, ADA_KV, d, b:b + 1],
                                                           ada_b[:, ADA_KV, d, b:b + 1], ALU.mult, ALU.add)
                    last.then_inc(ctxT_ready, 1)
                    for d in range(DB):
                        src = ps[:, CTX_BANK, (DB + d) * P:(DB + d + 1) * P].rearrange("p (b k) -> p b k", b=NB)
                        last = nc.vector.tensor_copy(ctxT[:, 1, d], src.unsqueeze(2).to_broadcast([P, NB, 2, LK]))
                    last.then_inc(ctxT_ready, 1)

            def context(a):
                dve.wait_ge(ctx_k_full, a + 1)
                bias = ("L0_xcond_bkv", "L1_xcond_ca_kb")[a]
                for o in range(DB):
                    last = nc.vector.tensor_scalar(ktx[:, a, o].rearrange("p b k -> p (b k)"),
                                                   ps[:, KEY_BANK[a], o * NB * LK:(o + 1) * NB * LK],
                                                   vec[:, VCOL[bias] + o:VCOL[bias] + o + 1], None, ALU.add)
                last.then_inc(ktx_ready, 1)
                dve.wait_ge(bc_in, 16 * len(BROAD))
                dve.wait_ge(consts_made, 2)
                dve.wait_ge(ctx_v_full, a + 1)
                name = ("L0_xcond_bv", "L1_xcond_ca_vb")[a]
                nc.vector.tensor_tensor(vtx[:, a], ps[:, VALUE_BANK[a], :].rearrange("p (b n) -> p b n", b=NB),
                                        bc[:, BROAD.index(name)].unsqueeze(1).to_broadcast([P, NB, D]),
                                        ALU.add).then_inc(vtx_ready, 1)
                dve.wait_ge(vtx_ready, a + 1)
                for b in range(NB):
                    for e in range(2):
                        last = nc.vector.tensor_scalar(
                            vbd[:, a, b].rearrange("p n (e k) -> p n e k", e=2)[:, :, e, :],
                            vtx[:, a, b].rearrange("p (n e k) -> p n e k", e=2, k=DH)[:, :, e, :],
                            half_mask[:, e:e + 1], None, ALU.mult)
                last.then_inc(vbd_ready, 1)

            def spread_keys(a):
                words = DB * NB * LK
                full = ktx[:, a].rearrange("p o b k -> p (o b k)")
                high, low = tmp[:, 0, 0:words], tmp[:, 1, 0:words]
                dve.wait_ge(ktx_ready, a + 1)
                nc.vector.tensor_copy(high.bitcast(F32R), full).then_inc(ktx_step, 1)
                dve.wait_ge(ktx_step, 2 * a + 1)
                nc.vector.tensor_tensor(low, full, high, ALU.subtract).then_inc(ktx_step, 1)
                dve.wait_ge(ktx_step, 2 * a + 2)
                for part, src in enumerate((high, low)):
                    src = src.rearrange("p (o b k) -> p o b k", o=DB, b=NB)
                    for b in range(NB):
                        for o in range(DB):
                            last = nc.vector.tensor_tensor(
                                kbd[:, part, b, o, :].rearrange("p (h k) -> p h k", k=LK),
                                src[:, o, b, :].unsqueeze(1).to_broadcast([P, HB, LK]),
                                head_mask[:].unsqueeze(2).to_broadcast([P, HB, LK]), ALU.mult)
                last.then_inc(kbd_ready, 1)

            dve.wait_ge(x_in, 16 * NB * NC)
            for n in range(NB * TB):
                last = nc.vector.bn_stats(stats_x[:, n, :], x_tok[:, n, :])
            last.then_inc(x_step, 1)
            aggregate(stats_x, mean_x[:], rstd_x[:], x_step, 1)
            scale_first(*UNITS[0])
            prepare(0)
            context(0)
            spread_keys(0)
            dve.wait_ge(w_0_in, 16 * 2)
            for k, dst in enumerate((w_q0, w_p0)):
                nc.vector.tensor_copy(dst[:, 0], w_raw[:, k]).then_inc(w_0_split, 1)
                dve.wait_ge(w_0_split, 2 * k + 1)
                nc.vector.tensor_tensor(dst[:, 1], w_raw[:, k], dst[:, 0].bitcast(F32),
                                        ALU.subtract).then_inc(w_0_split, 1)

            scale_first(*UNITS[1])

            def norm_unit(k):
                if k < len(UNITS):
                    scale_first(*UNITS[k])
                elif k < 2 * len(UNITS):
                    c, b = UNITS[k - len(UNITS)]
                    if c == 0:
                        dve.wait_ge(px["xT_low"][b], NC * DB)
                    else:
                        dve.wait_ge(p2["xT_low"][b], c * DB)
                    norm_rows(p2, token_rows(c, b), c, b)

            def add_first(c, b):
                dve.wait_ge(px["biased"][b], c + 1)
                add_rows(px["o_full"], px["added"],
                         lambda k: token_rows(c, b, 2 * k, 2), c, b, 2)

            def split_qk(c, b):
                dve.wait_ge(p2["parts_out"][b], c * 16 * 4)
                for u in range(4):
                    full = q_full[:, b, u, :]
                    high, mid = parts[b][:, u, 0, :], parts[b][:, u, 1, :]
                    dve.wait_ge(p2["qk_taken"][b], c * 4 + u + 1)
                    nc.vector.tensor_tensor(full, full, high, ALU.subtract).then_inc(p2["split_step"], 1)
                    dve.wait_ge(p2["split_step"], (c * NB + b) * 4 + u + 1)
                    nc.vector.tensor_copy(mid, full).then_inc(p2["mid_ready"][b], 1)

            def add_values(c, b):
                for k in range(2):
                    dve.wait_ge(p2["v_full"][b], c * 2 + k + 1)
                    bias = bc[:, BROAD.index("L1_xcond_sa_vb")].unsqueeze(1).to_broadcast([P, 2, D])
                    at_block = c * QB + b * TB + 2 * k
                    nc.vector.tensor_tensor(
                        v_all[:, at_block:at_block + 2].rearrange("p o h n -> p o (h n)"),
                        bank(b, 2 + k).rearrange("p (o n) -> p o n", o=2), bias, ALU.add).then_inc(p2["v_ready"][b], 1)

            low_queries(px, 0, 0, "L0_xcond_bq")
            maxima(px, 0, 0)
            prepare(1)
            context(1)
            for i, (c, b) in enumerate(UNITS):
                final = i + 1 == len(UNITS)
                if i > 0:
                    add_first(*UNITS[i - 1])
                normalise(c, b, 0)
                if not final:
                    low_queries(px, *UNITS[i + 1], "L0_xcond_bq")
                norm_unit(i + 2)
                if not final:
                    maxima(px, *UNITS[i + 1])
                normalise(c, b, 1)
            split_qk(*UNITS[0])
            add_values(*UNITS[0])
            add_first(*UNITS[-1])

            for i, (c, b) in enumerate(UNITS[1:]):
                norm_unit(len(UNITS) + i + 2)
                split_qk(c, b)
                add_values(c, b)

            def group_maxima(g, b):
                a = g * NB + b
                for n in range(QT):
                    dve.wait_ge(sa_s_full, a * QT + n + 1)
                    at = 4 + 2 * (n % 2)
                    nc.vector.tensor_reduce(negmax_g[:, n:n + 1], ps[:, at:at + 2, :].rearrange("p a n -> p (a n)"),
                                            AX.X, ALU.max, negate=True).then_inc(sa_max_done, 1)
                dve.wait_ge(sa_max_done, (a + 1) * QT)
                high, mid, low = (max_parts_g[:, k, :] for k in range(PARTS))
                nc.vector.tensor_copy(high, negmax_g[:]).then_inc(sa_split_step, 1)
                dve.wait_ge(sa_split_step, a * 4 + 1)
                nc.vector.tensor_tensor(max_rest_g[:], negmax_g[:], high, ALU.subtract).then_inc(sa_split_step, 1)
                dve.wait_ge(sa_split_step, a * 4 + 2)
                nc.vector.tensor_copy(mid, max_rest_g[:]).then_inc(sa_split_step, 1)
                dve.wait_ge(sa_split_step, a * 4 + 3)
                nc.vector.tensor_tensor(low, max_rest_g[:], mid, ALU.subtract).then_inc(sa_split_step, 1)
                dve.wait_ge(sa_maxT_full, a + 1)
                for k in range(NB):
                    dve.wait_ge(shift_in[k], (g + (k < b)) * 16)
                nc.vector.tensor_copy(maxT_g[:], ps[0:PARTS * QT, 4, 0:P // 2].bitcast(BF16)).then_inc(sa_maxT_ready, 1)

            def invert_sums(n):
                dve.wait_ge(den_in, (n + 1) * 16)
                nc.vector.reciprocal(rec_seg[:], den_seg[:]).then_inc(rec_done, 1)

            group_maxima(0, 0)
            with dve.Fori(0, NG - 1) as g:
                group_maxima(g, 1)
                group_maxima(g + 1, 0)
            group_maxima(NG - 1, 1)
            invert_sums(0)
            dve.wait_ge(sa_pv_done, (HALVES - 1) * STEPS)

            def out_of_sums(c, b):
                dve.wait_ge(p4["att_in"][b], (c + 1) * 16 * 2 * DB)
                dve.wait_ge(p4["y_full"][b], c * 2)
                for d in range(DB):
                    u = tmp[:, b + 2 * d, :]
                    step = ((c * NB + b) * DB + d) * 2
                    nc.vector.tensor_tensor(u, attT[:, b, d, :], recT[:, b, d, :],
                                            ALU.mult).then_inc(p4["out_step"], 1)
                    split_out(p4, u, b, d, step + 1)

            def add_to(full, done, c, b):
                add_rows(full, done, lambda k: token_rows(c % NC, b, 2 * k, 2), c, b, 2)

            def add_last(c, b):
                dve.wait_ge(p4["b2_added"][b], c + 1)
                add_to(p4["y_full"], p4["y_ready"], c, b)

            def start_cross(c, b):
                dve.wait_ge(p4["x1_in"][b], c + 1)
                add_to(p4["so_full"], p4["x2_ready"], c, b)

            out_of_sums(0, 0)
            start_cross(0, 0)
            dve.wait_ge(v_grp_ready, HALVES)
            spread_keys(1)
            invert_sums(1)
            low_queries(px, NC, 0, "L1_xcond_ca_qb")
            invert_sums(2)
            maxima(px, NC, 0)
            for i, (c, b) in enumerate(UNITS):
                n = c + NC
                after = UNITS[i + 1] if i + 1 < len(UNITS) else None
                normalise(n, b, 0)
                if i == 0:
                    invert_sums(3)
                normalise(n, b, 1)
                if i > 0:
                    add_last(*UNITS[i - 1])
                if after:
                    out_of_sums(*after)
                dve.wait_ge(px["biased"][b], n + 1)
                add_to(px["o_full"], px["added"], n, b)
                if after:
                    start_cross(*after)
                dve.wait_ge(px["added"][b], (n + 1) * 2)
                dve.wait_ge(p4["hT_low"][b], c * DB)
                norm_rows(px, token_rows(c, b), n, b)
                if after:
                    low_queries(px, after[0] + NC, after[1], "L1_xcond_ca_qb")
                    maxima(px, after[0] + NC, after[1])
                for f in range(FB):
                    dve.wait_ge(p4["hid_taken"][b], c * FB + f + 1)
                    if f == HF:
                        dve.wait_ge(p4["hid_used"], c * NB + b + 1)
                    nc.vector.tensor_copy(hidT[b][:, f % HF, 0, :],
                                          tmp[:, b + 2 * (f % 2), :]).then_inc(p4["hid_step"], 1)
                    dve.wait_ge(p4["hid_step"], (c * NB + b) * FB + f + 1)
                    nc.vector.tensor_tensor(hidT[b][:, f % HF, 1, :], tmp[:, b + 2 * (f % 2), :],
                                            hidT[b][:, f % HF, 0, :].bitcast(F32),
                                            ALU.subtract).then_inc(p4["hid_low"][b], 1)
            add_last(*UNITS[-1])

        @block.scalar
        def _(act):
            def turned(to, b, d, k0, ada):
                if ada is None:
                    return nc.scalar.activation(to, bank(b, k0 + d), ACT.Copy)
                return nc.scalar.activation(to, bank(b, k0 + d), ACT.Identity, scale=ada_a[:, ada, d, b:b + 1],
                                            bias=ada_b[:, ada, d, b:b + 1])

            def turned_high(full, high, n, b, k0, ada):
                for d in range(DB):
                    act.wait_ge(full[b], n * DB + d + 1)
                    turned(xT[:, 0, b, d, :], b, d, k0, ada).then_inc(high[b], 1)

            def turned_full(high, b, k0, ada):
                for d in range(DB):
                    turned(xf[:, b, d, :], b, d, k0, ada).then_inc(high[b], 1)

            def queries(ph, c, b, name):
                for d in range(DB):
                    act.wait_ge(ph["q_full"][b], c * DB + d + 1)
                    nc.scalar.activation(qT[b][:, 0, d, :], bank(b, 2 + d), ACT.Identity,
                                         bias=vec[:, VCOL[name] + d:VCOL[name] + d + 1]).then_inc(ph["q_high"][b], 1)

            def take_maxima(n, b):
                act.wait_ge(px["maxT_full"][b], n + 1)
                nc.scalar.activation(maxT[:, b, :], bank(b, 2)[0:PARTS * PR, 0:CH // 2].bitcast(BF16),
                                     ACT.Copy).then_inc(px["maxT_ready"][b], 1)

            def exponentials(n, b, d):
                if b > 0:
                    act.wait_ge(px["pv_full"][b - 1], n * DB + d + 1)
                elif n > 0:
                    act.wait_ge(px["pv_full"][NB - 1], (n - 1) * DB + d + 1)
                for p in range(d * PB, (d + 1) * PB):
                    act.wait_ge(px["st_full"][b], n * NP + p + 1)
                    nc.scalar.activation(probs[:, p, :], bank(b, p % 2), ACT.Exp,
                                         scale=SCALE).then_inc(px["exp_done"][b], 1)

            act.wait_ge(vec_full, 1)
            nc.scalar.activation(vec[:, 0:NVEC0], ps[:, 0, 0:NVEC0], ACT.Copy).then_inc(vec_ready, 1)
            act.wait_ge(vec_ready, 1)
            nc.scalar.activation(silu[:, 0], vec[:, 0:4], ACT.Exp, scale=-1.0).then_inc(silu_exp, 1)


            def queries_first(c, b):
                queries(px, c, b, "L0_xcond_bq")

            def take_qk(c, b):
                act.wait_ge(p2["parts_ready"][b], c * 4)
                act.wait_ge(p2["parts_out"][b], c * 16 * 4)
                for u in range(4):
                    k, d = u // DB, u % DB
                    name = ("L1_xcond_sa_qb", "L1_xcond_sa_kb")[k]
                    src = bank(b, 2 - 2 * k + d)
                    bias = vec[:, VCOL[name] + d:VCOL[name] + d + 1]
                    act.wait_ge(p2["qk_full"][b], c * 4 + u + 1)
                    nc.scalar.activation(q_full[:, b, u, :], src, ACT.Identity, bias=bias)
                    nc.scalar.activation(parts[b][:, u, 0, :], src, ACT.Identity,
                                         bias=bias).then_inc(p2["qk_taken"][b], 1)

            def turned_second(c, b):
                turned_high(p2["xT_full"], p2["xT_high"], c, b, 0, ADA_1)
                turned_full(p2["xT_high"], b, 0, ADA_1)

            turned_high(px["xT_full"], px["xT_high"], 0, 0, 0, ADA_Q)
            turned_full(px["xT_high"], 0, 0, ADA_Q)
            act.wait_ge(vec_full, 2)
            nc.scalar.activation(vec[:, NVEC0:NVEC], ps[:, 0, NVEC0:NVEC], ACT.Copy).then_inc(vec_ready, 1)
            queries_first(0, 0)
            act.wait_ge(w_split, 2 * 6)
            for i, (c, b) in enumerate(UNITS):
                final = i + 1 == len(UNITS)
                nxt = UNITS[(i + 1) % len(UNITS)]
                ph, ada = (p2, ADA_1) if final else (px, ADA_Q)
                turned_high(ph["xT_full"], ph["xT_high"], *nxt, 0, ada)
                take_maxima(c, b)
                if i == 0:
                    act.wait_ge(vec_ready, 2)
                exponentials(c, b, 0)
                turned_full(ph["xT_high"], nxt[1], 0, ada)
                if final:
                    take_qk(*nxt)
                else:
                    queries_first(*nxt)
                exponentials(c, b, 1)

            for i, (c, b) in enumerate(UNITS[1:]):
                turned_second(c, b)
                take_qk(c, b)

            for b in range(NB):
                act.wait_ge(p2["parts_ready"][b], 4 * NC)

            def step_exponentials(g, b, s):
                half = g * NB + b
                for j in range(HG):
                    u = s * HG + j
                    act.wait_ge(sa_st_full, half * STEPS * HG + u + 1)
                    nc.scalar.activation(probs[:, (s % 2) * HG + j, :], ps[:, score_bank(u), :], ACT.Exp,
                                         scale=SCALE).then_inc(sa_exp_done, 1)

            def take_sums(g, b, ch):
                half = g * NB + b
                act.wait_ge(sa_pv_done, half * STEPS + (ch + 1) * TB)
                act.wait_ge(sums_out[ch], half * 16)
                nc.scalar.activation(sums[:, ch], ps[:, 3, :], ACT.Copy).then_inc(sums_taken[ch], 1)

            def group_exponentials(g, b, following, beside=None):
                half = g * NB + b
                for s in range(1, STEPS):
                    act.wait_ge(sa_pv_done, half * STEPS + s - 1)
                    step_exponentials(g, b, s)
                    if s == TB:
                        take_sums(g, b, 0)
                    if beside is not None:
                        beside(s)
                if following is not None:
                    act.wait_ge(sa_pv_done, (half + 1) * STEPS - 1)
                    step_exponentials(*following, 0)
                take_sums(g, b, 1)

            step_exponentials(0, 0, 0)
            with act.Fori(0, NG - 1) as g:
                group_exponentials(g, 0, (g, 1))
                group_exponentials(g, 1, (g + 1, 0))

            def take_turned(c, b):
                turned_high(px["xT_full"], px["xT_high"], c + NC, b, 0, None)
                turned_full(px["xT_high"], b, 0, None)

            def take_queries(c, b):
                queries(px, c + NC, b, "L1_xcond_ca_qb")

            def start_last(s):
                if s == 6:
                    act.wait_ge(w_split, 2 * 8)
                    take_turned(0, 0)
                elif s == 9:
                    take_queries(0, 0)

            group_exponentials(NG - 1, 0, (NG - 1, 1))
            group_exponentials(NG - 1, 1, None, start_last)
            act.wait_ge(sa_pv_done, HALVES * STEPS)
            for i, (c, b) in enumerate(UNITS):
                take_maxima(c + NC, b)
                for d in range(DB):
                    exponentials(c + NC, b, d)
                if i + 1 < len(UNITS):
                    take_turned(*UNITS[i + 1])
                    take_queries(*UNITS[i + 1])
                turned_high(p4["hT_full"], p4["hT_high"], c, b, 2, ADA_2)
                turned_full(p4["hT_high"], b, 2, ADA_2)
                for f in range(FB):
                    if f >= 2:
                        act.wait_ge(p4["hid_low"][b], c * FB + f - 1)
                    act.wait_ge(p4["hid_full"][b], c * FB + f + 1)
                    bias = vec[:, VCOL["L1_xcond_ffn_b1"] + f:VCOL["L1_xcond_ffn_b1"] + f + 1]
                    nc.scalar.activation(tmp[:, b + 2 * (f % 2), :], bank(b, f % 2), ACT.Gelu,
                                         bias=bias).then_inc(p4["hid_taken"][b], 1)


_INS = ["x", "ctx_1024", "cond_1024"] + ["L0_xcond_" + n for n in (
    "Wq", "bq", "Wkv", "bkv", "Wp", "bp", "Wss_q", "bss_q", "Wss_kv", "bss_kv")] + ["L1_xcond_" + n for n in (
        "ln1_g", "ln1_b", "aff1_w", "aff1_b", "ln2_g", "ln2_b", "aff2_w", "aff2_b", "sa_qw", "sa_qb", "sa_kw",
        "sa_kb", "sa_vw", "sa_vb", "sa_ow", "sa_ob", "ca_qw", "ca_qb", "ca_kw", "ca_kb", "ca_vw", "ca_vb",
        "ca_ow", "ca_ob", "ffn_w1", "ffn_b1", "ffn_w2", "ffn_b2")]


def kernel(**inputs):
    import numpy as _np
    import concourse.bacc as _bacc
    from concourse import mybir as _mybir
    from concourse.bass_utils import run_bass_kernel_spmd as _run

    nc = _bacc.Bacc("TRN2", target_bir_lowering=False, num_devices=1)
    arrays, tensors = {}, {}
    for name in _INS:
        a = _np.ascontiguousarray(inputs[name])
        arrays[f"in_{name}_dram"] = a
        tensors[name] = nc.dram_tensor(f"in_{name}_dram", a.shape, _mybir.dt.from_np(a.dtype),
                                       kind="ExternalInput").ap()
    out = nc.dram_tensor("out_0_dram", (NB, L, D), _mybir.dt.from_np(_np.dtype("float32")), kind="ExternalOutput").ap()
    build(nc, tensors, out)
    r = _run(nc, [arrays], core_ids=[0])
    return r.results[0]["out_0_dram"]
```
